# Optimizing a Trainium2 kernel written in Bass

```python
import numpy as np
import jax
import jax.numpy as jnp

def _softmax(x, axis=-1):
    return jax.nn.softmax(x, axis=axis)

def _gelu(x):
    return jax.nn.gelu(x, approximate=True)

def _silu(x):
    return jax.nn.silu(x)

def _sigmoid(x):
    return jax.nn.sigmoid(x)

def _layernorm(x, axis=-1, eps=1e-05):
    m = jnp.mean(x, axis=axis, keepdims=True)
    v = jnp.var(x, axis=axis, keepdims=True)
    return (x - m) / jnp.sqrt(v + eps)

def _scatter_add(tgt, idx, src, axis=0):
    return tgt.at[idx].add(src)

def _segment_sum(src, seg, n):
    return jax.ops.segment_sum(src, seg, n)
kernel_name = 'mk_decoder_preln_d2_seqx_r8_c795b5'

def setup_inputs(seed: int=0):
    np.random.seed(seed)
    _w = jnp.asarray

    def _rec_inputs():
        import jax
        import jax.numpy as jnp
        _rk = jax.random.key(seed)
        x = -0.0002928 + 1 * jax.random.normal(jax.random.fold_in(_rk, 1), (4, 256, 256), jnp.float32)
        _lenS = 256 - jax.random.randint(jax.random.fold_in(_rk, 7), (4,), 0, max(1, 256 // 4) + 1, jnp.int32)
        _lenS2 = 512 - jax.random.randint(jax.random.fold_in(_rk, 8), (4,), 0, max(1, 512 // 4) + 1, jnp.int32)
        _ctx_512P = jax.random.normal(jax.random.fold_in(_rk, 11), (4, 16, 64), jnp.float32)
        _ctx_512c = jax.random.dirichlet(jax.random.fold_in(_rk, 511), 0.3 * jnp.ones((16,), jnp.float32), (4, 512))
        _ctx_512t = jnp.einsum('bsk,bkd->bsd', _ctx_512c, _ctx_512P)
        _ctx_512t = _ctx_512t * jax.lax.rsqrt(jnp.mean(jnp.square(_ctx_512t)) + 1e-12) * 0.953939
        ctx_512 = 0.000227908 + 0.99994 * (_ctx_512t + 0.3 * jax.random.normal(jax.random.fold_in(_rk, 611), (4, 512, 64), jnp.float32))
        return (x, ctx_512)
    x, ctx_512 = _rec_inputs()

    def _L0_attn_setup():
        import jax, jax.numpy as jnp
        import numpy as np
        D_MODEL = 256
        NUM_HEADS = 16
        HEAD_DIM = D_MODEL // NUM_HEADS
        LAYER_IDX = 0
        NUM_LAYERS = 13
        REINIT_LAMBDA = 0.8

        def _heads(t, B, S):
            return t.reshape(B, S, NUM_HEADS, HEAD_DIM).transpose(0, 2, 1, 3)
        key = jax.random.key(seed)
        ks = jax.random.split(key, 8)
        B, S = (2, 256)
        x = jax.random.normal(ks[0], (B, S, D_MODEL), dtype=jnp.float32)
        init = 1.0 / np.sqrt(D_MODEL)

        def w(k):
            return jax.random.uniform(k, (D_MODEL, D_MODEL), dtype=jnp.float32, minval=-init, maxval=init)
        lam_init = REINIT_LAMBDA * ((LAYER_IDX + 1) / NUM_LAYERS)
        return {'x': x, 'q1_w': w(ks[1]), 'k1_w': w(ks[2]), 'q2_w': w(ks[3]), 'k2_w': w(ks[4]), 'v_w': w(ks[5]), 'o_w': w(ks[6]), 'lambda_param': jnp.full((NUM_HEADS,), lam_init, dtype=jnp.float32)}
    _L0_attn_all = _L0_attn_setup()
    _L0_attn_in = {k: v for k, v in _L0_attn_all.items() if k in ('q1_w', 'k1_w', 'q2_w', 'k2_w', 'v_w', 'o_w', 'lambda_param')}
    del _L0_attn_all

    def _L0_xattn_setup():
        import jax, jax.numpy as jnp
        import numpy as np
        B, S, L = (2, 128, 128)
        DIM_Q, H, K, D_C, D_CQ, R = (256, 16, 128, 64, 192, 64)

        def _rope_tables(seq_len, dim, dtype):
            inv_freq = 1.0 / 10000.0 ** (jnp.arange(0, dim, 2, dtype=dtype) / dim)
            t = jnp.arange(seq_len, dtype=dtype)
            freqs = t[:, None] * inv_freq[None, :]
            sin = jnp.repeat(jnp.sin(freqs), 2, axis=-1)
            cos = jnp.repeat(jnp.cos(freqs), 2, axis=-1)
            return (sin, cos)

        def _rotate_half(x):
            h = x.shape[-1] // 2
            return jnp.concatenate([-x[..., h:], x[..., :h]], axis=-1)
        key = jax.random.key(seed)
        ks = jax.random.split(key, 8)
        s_in = 1.0 / np.sqrt(DIM_Q)
        s_k = 1.0 / np.sqrt(K)
        s_cq = 1.0 / np.sqrt(D_CQ)
        s_c = 1.0 / np.sqrt(D_C)
        return {'hidden_q': jax.random.normal(ks[0], (B, S, DIM_Q), jnp.float32), 'kv_c': jax.random.normal(ks[1], (B, L, D_C), jnp.float32), 'Wq': jax.random.normal(ks[2], (H * K, DIM_Q), jnp.float32) * s_in, 'w_kc_q': jax.random.normal(ks[3], (H, K, D_CQ), jnp.float32) * s_k, 'w_kc_kv': jax.random.normal(ks[4], (H, K, D_C), jnp.float32) * s_k, 'W_qr': jax.random.normal(ks[5], (H, D_CQ, R), jnp.float32) * s_cq / np.sqrt(R), 'W_kr': jax.random.normal(ks[6], (H, D_C, R), jnp.float32) * s_c, 'Wo': jax.random.normal(ks[7], (DIM_Q, H * K), jnp.float32) * s_k}
    _L0_xattn_all = _L0_xattn_setup()
    _L0_xattn_in = {k: v for k, v in _L0_xattn_all.items() if k in ('Wq', 'w_kc_q', 'w_kc_kv', 'W_qr', 'W_kr', 'Wo')}
    del _L0_xattn_all

    def _L0_ffn_setup():
        import jax, jax.numpy as jnp
        import numpy as np
        B, S, H, I, E, F, K, R, TOPK = (1, 128, 256, 176, 64, 8, 8, 8, 6)
        ISH = 2 * I

        def _fused_linear(x, W, qa, qb, scale, w):
            out = x @ W.T
            a = jnp.einsum('th,krh->tkr', x, qa)
            b = jnp.einsum('tkr,khr->tkh', a, qb)
            mix = jnp.einsum('tkh,tk->th', b, w)
            return out + scale[None, :] * mix

        def _moe_forward(hidden_states, gate_weight, inv_mapping, mask_up_W, gate_W, gate_qa, gate_qb, gate_scale, up_W, up_qa, up_qb, up_scale, down_W, down_qa, down_qb, down_scale, sh_gate_W, sh_up_W, sh_down_W):
            b, s, h = hidden_states.shape
            x = hidden_states.reshape(-1, h)
            T = x.shape[0]
            scores = jax.nn.softmax(x @ gate_weight.T, axis=-1)
            topk_w, topk_idx = jax.lax.top_k(scores, TOPK)
            w_dense = jnp.zeros((T, E), x.dtype).at[jnp.arange(T)[:, None], topk_idx].add(topk_w)
            flat = w_dense[:, inv_mapping]
            scalar = flat.sum(-1)
            soft = jax.nn.softmax(jnp.where(flat == 0, -1000000000.0, flat), axis=-1)

            def expert(muW, gW, gqa, gqb, gs, uW, uqa, uqb, us, dW, dqa, dqb, ds, w):
                xe = x + w @ muW.T
                gate = jax.nn.silu(_fused_linear(xe, gW, gqa, gqb, gs, w))
                up = _fused_linear(xe, uW, uqa, uqb, us, w)
                return _fused_linear(gate * up, dW, dqa, dqb, ds, w)
            outs = jax.vmap(expert, in_axes=(0,) * 13 + (1,))(mask_up_W, gate_W, gate_qa, gate_qb, gate_scale, up_W, up_qa, up_qb, up_scale, down_W, down_qa, down_qb, down_scale, soft)
            y = jnp.einsum('fth,tf->th', outs, scalar).reshape(b, s, h)
            sh = jax.nn.silu(hidden_states @ sh_gate_W.T) * (hidden_states @ sh_up_W.T) @ sh_down_W.T
            return y + sh
        key = jax.random.key(seed)
        ks = jax.random.split(key, 20)
        g = lambda k, shape, s=0.02: jax.random.normal(k, shape, jnp.float32) * s
        return {'hidden_states': jax.random.normal(ks[0], (B, S, H), jnp.float32), 'gate_weight': g(ks[1], (E, H)), 'inv_mapping': jnp.arange(E, dtype=jnp.int32).reshape(F, K), 'mask_up_W': g(ks[2], (F, H, K)), 'gate_W': g(ks[3], (F, I, H)), 'gate_qa': g(ks[4], (F, K, R, H)), 'gate_qb': g(ks[5], (F, K, I, R)), 'gate_scale': jnp.full((F, I), 0.1, jnp.float32), 'up_W': g(ks[6], (F, I, H)), 'up_qa': g(ks[7], (F, K, R, H)), 'up_qb': g(ks[8], (F, K, I, R)), 'up_scale': jnp.full((F, I), 0.1, jnp.float32), 'down_W': g(ks[9], (F, H, I)), 'down_qa': g(ks[10], (F, K, R, I)), 'down_qb': g(ks[11], (F, K, H, R)), 'down_scale': jnp.full((F, H), 0.1, jnp.float32), 'sh_gate_W': g(ks[12], (ISH, H)), 'sh_up_W': g(ks[13], (ISH, H)), 'sh_down_W': g(ks[14], (H, ISH))}
    _L0_ffn_all = _L0_ffn_setup()
    _L0_ffn_in = {k: v for k, v in _L0_ffn_all.items() if k in ('gate_weight', 'inv_mapping', 'mask_up_W', 'gate_W', 'gate_qa', 'gate_qb', 'gate_scale', 'up_W', 'up_qa', 'up_qb', 'up_scale', 'down_W', 'down_qa', 'down_qb', 'down_scale', 'sh_gate_W', 'sh_up_W', 'sh_down_W')}
    del _L0_ffn_all

    def _L1_attn_setup():
        import jax, jax.numpy as jnp
        import numpy as np
        from jax import lax
        D_MODEL = 256
        D_INNER = 512
        D_CONV = 4
        B, T = (4, 256)

        def _rmsnorm(h):
            n = jnp.sqrt(jnp.sum(h * h, axis=-1, keepdims=True))
            return h / jnp.maximum(n, 1e-12) * h.shape[-1] ** 0.5

        def _mamba_fallback(h, W_in, conv_w, conv_b, W_out):
            xz = jnp.einsum('btd,ed->bte', h, W_in)
            xp, z = jnp.split(xz, 2, axis=-1)
            xc = lax.conv_general_dilated(xp.transpose(0, 2, 1), conv_w, window_strides=(1,), padding=[(D_CONV - 1, 0)], dimension_numbers=('NCH', 'OIH', 'NCH'), feature_group_count=D_INNER) + conv_b[None, :, None]
            xc = xc.transpose(0, 2, 1)
            y = jax.nn.silu(xc) * jax.nn.silu(z)
            return jnp.einsum('bte,de->btd', y, W_out)
        key = jax.random.key(seed)
        ks = jax.random.split(key, 7)
        std = 0.02
        return {'x': jax.random.normal(ks[0], (B, T, D_MODEL), jnp.float32), 'W_in': jax.random.normal(ks[1], (2 * D_INNER, D_MODEL), jnp.float32) * std, 'conv_w': jax.random.normal(ks[2], (D_INNER, 1, D_CONV), jnp.float32) * std, 'conv_b': jnp.zeros((D_INNER,), jnp.float32), 'W_out': jax.random.normal(ks[3], (D_MODEL, D_INNER), jnp.float32) * std, 'W_mlp1': jax.random.normal(ks[4], (4 * D_MODEL, D_MODEL), jnp.float32) * std, 'W_mlp2': jax.random.normal(ks[5], (D_MODEL, 4 * D_MODEL), jnp.float32) * std}
    _L1_attn_all = _L1_attn_setup()
    _L1_attn_in = {k: v for k, v in _L1_attn_all.items() if k in ('W_in', 'conv_w', 'conv_b', 'W_out', 'W_mlp1', 'W_mlp2')}
    del _L1_attn_all

    def _L1_xattn_setup():
        import jax, jax.numpy as jnp
        import numpy as np
        B, S, L = (2, 128, 128)
        DIM_Q, H, K, D_C, D_CQ, R = (256, 16, 128, 64, 192, 64)

        def _rope_tables(length, dim):
            inv = 1.0 / 10000.0 ** (jnp.arange(0, dim, 2, dtype=jnp.float32) / dim)
            f = jnp.arange(length, dtype=jnp.float32)[:, None] * inv[None, :]
            sin = jnp.repeat(jnp.sin(f), 2, axis=-1)
            cos = jnp.repeat(jnp.cos(f), 2, axis=-1)
            return (sin, cos)

        def _rotate_half(x):
            half = x.shape[-1] // 2
            return jnp.concatenate([-x[..., half:], x[..., :half]], axis=-1)

        def _apply_rope(x, sin, cos):
            return x * cos + _rotate_half(x) * sin
        key = jax.random.key(seed)
        ks = jax.random.split(key, 8)
        return {'hidden_q': jax.random.normal(ks[0], (B, S, DIM_Q), jnp.float32), 'kv_c': jax.random.normal(ks[1], (B, L, D_C), jnp.float32), 'Wq': jax.random.normal(ks[2], (H * K, DIM_Q), jnp.float32) / np.sqrt(DIM_Q).astype(np.float32), 'w_kc_q': jax.random.normal(ks[3], (H, K, D_CQ), jnp.float32) / np.sqrt(K).astype(np.float32), 'w_kc_kv': jax.random.normal(ks[4], (H, K, D_C), jnp.float32) / np.sqrt(K).astype(np.float32), 'W_qr': jax.random.normal(ks[5], (H, D_CQ, R), jnp.float32) / np.float32(np.sqrt(D_CQ) * np.sqrt(R)), 'W_kr': jax.random.normal(ks[6], (H, D_C, R), jnp.float32) / np.sqrt(D_C).astype(np.float32), 'Wo': jax.random.normal(ks[7], (DIM_Q, H * K), jnp.float32) / np.sqrt(H * K).astype(np.float32)}
    _L1_xattn_all = _L1_xattn_setup()
    _L1_xattn_in = {k: v for k, v in _L1_xattn_all.items() if k in ('Wq', 'w_kc_q', 'w_kc_kv', 'W_qr', 'W_kr', 'Wo')}
    del _L1_xattn_all

    def _L1_ffn_setup():
        import jax, jax.numpy as jnp
        import numpy as np
        FP8_MAX = 448.0
        GLOBAL_DIV = 448.0 * 6.0

        def _fp8(x):
            return x.astype(jnp.float8_e4m3fn).astype(jnp.float32)

        def _reorder_quantize_x(x, idx):
            scale = jnp.max(jnp.abs(x)) / GLOBAL_DIV
            xr = (x / scale)[:, idx]
            scale_x = jnp.max(jnp.abs(xr), axis=1, keepdims=True) / FP8_MAX
            qx = _fp8(xr / scale_x)
            return (qx, scale_x, scale)

        def _qlinear(qx, scale_x, scale, W, idx, out_idx=None):
            Wr = W[:, idx]
            w_scale = jnp.max(jnp.abs(Wr), axis=1, keepdims=True) / FP8_MAX
            qw = _fp8(Wr / w_scale)
            y = qx * scale_x @ (qw * w_scale).T * scale
            if out_idx is not None:
                y = y[:, out_idx]
            return y
        key = jax.random.key(seed)
        ks = jax.random.split(key, 6)
        B, S, H, I = (2, 128, 256, 704)
        return {'x': jax.random.normal(ks[0], (B, S, H), jnp.float32), 'w_gate': jax.random.normal(ks[1], (I, H), jnp.float32) * 0.02, 'w_up': jax.random.normal(ks[2], (I, H), jnp.float32) * 0.02, 'w_down': jax.random.normal(ks[3], (H, I), jnp.float32) * 0.02, 'up_reorder_index': jax.random.permutation(ks[4], jnp.arange(H, dtype=jnp.int64)), 'down_reorder_index': jax.random.permutation(ks[5], jnp.arange(I, dtype=jnp.int64))}
    _L1_ffn_all = _L1_ffn_setup()
    _L1_ffn_in = {k: v for k, v in _L1_ffn_all.items() if k in ('w_gate', 'w_up', 'w_down', 'up_reorder_index', 'down_reorder_index')}
    del _L1_ffn_all
    return {'x': x, 'ctx_512': ctx_512, 'L0_attn_q1_w': _L0_attn_in['q1_w'], 'L0_attn_k1_w': _L0_attn_in['k1_w'], 'L0_attn_q2_w': _L0_attn_in['q2_w'], 'L0_attn_k2_w': _L0_attn_in['k2_w'], 'L0_attn_v_w': _L0_attn_in['v_w'], 'L0_attn_o_w': _L0_attn_in['o_w'], 'L0_attn_lambda_param': _L0_attn_in['lambda_param'], 'L0_xattn_Wq': _L0_xattn_in['Wq'], 'L0_xattn_w_kc_q': _L0_xattn_in['w_kc_q'], 'L0_xattn_w_kc_kv': _L0_xattn_in['w_kc_kv'], 'L0_xattn_W_qr': _L0_xattn_in['W_qr'], 'L0_xattn_W_kr': _L0_xattn_in['W_kr'], 'L0_xattn_Wo': _L0_xattn_in['Wo'], 'L0_ffn_gate_weight': _L0_ffn_in['gate_weight'], 'L0_ffn_inv_mapping': _L0_ffn_in['inv_mapping'], 'L0_ffn_mask_up_W': _L0_ffn_in['mask_up_W'], 'L0_ffn_gate_W': _L0_ffn_in['gate_W'], 'L0_ffn_gate_qa': _L0_ffn_in['gate_qa'], 'L0_ffn_gate_qb': _L0_ffn_in['gate_qb'], 'L0_ffn_gate_scale': _L0_ffn_in['gate_scale'], 'L0_ffn_up_W': _L0_ffn_in['up_W'], 'L0_ffn_up_qa': _L0_ffn_in['up_qa'], 'L0_ffn_up_qb': _L0_ffn_in['up_qb'], 'L0_ffn_up_scale': _L0_ffn_in['up_scale'], 'L0_ffn_down_W': _L0_ffn_in['down_W'], 'L0_ffn_down_qa': _L0_ffn_in['down_qa'], 'L0_ffn_down_qb': _L0_ffn_in['down_qb'], 'L0_ffn_down_scale': _L0_ffn_in['down_scale'], 'L0_ffn_sh_gate_W': _L0_ffn_in['sh_gate_W'], 'L0_ffn_sh_up_W': _L0_ffn_in['sh_up_W'], 'L0_ffn_sh_down_W': _L0_ffn_in['sh_down_W'], 'L1_attn_W_in': _L1_attn_in['W_in'], 'L1_attn_conv_w': _L1_attn_in['conv_w'], 'L1_attn_conv_b': _L1_attn_in['conv_b'], 'L1_attn_W_out': _L1_attn_in['W_out'], 'L1_attn_W_mlp1': _L1_attn_in['W_mlp1'], 'L1_attn_W_mlp2': _L1_attn_in['W_mlp2'], 'L1_xattn_Wq': _L1_xattn_in['Wq'], 'L1_xattn_w_kc_q': _L1_xattn_in['w_kc_q'], 'L1_xattn_w_kc_kv': _L1_xattn_in['w_kc_kv'], 'L1_xattn_W_qr': _L1_xattn_in['W_qr'], 'L1_xattn_W_kr': _L1_xattn_in['W_kr'], 'L1_xattn_Wo': _L1_xattn_in['Wo'], 'L1_ffn_w_gate': _L1_ffn_in['w_gate'], 'L1_ffn_w_up': _L1_ffn_in['w_up'], 'L1_ffn_w_down': _L1_ffn_in['w_down'], 'L1_ffn_up_reorder_index': _L1_ffn_in['up_reorder_index'], 'L1_ffn_down_reorder_index': _L1_ffn_in['down_reorder_index']}

def reference(x, ctx_512, L0_attn_q1_w, L0_attn_k1_w, L0_attn_q2_w, L0_attn_k2_w, L0_attn_v_w, L0_attn_o_w, L0_attn_lambda_param, L0_xattn_Wq, L0_xattn_w_kc_q, L0_xattn_w_kc_kv, L0_xattn_W_qr, L0_xattn_W_kr, L0_xattn_Wo, L0_ffn_gate_weight, L0_ffn_inv_mapping, L0_ffn_mask_up_W, L0_ffn_gate_W, L0_ffn_gate_qa, L0_ffn_gate_qb, L0_ffn_gate_scale, L0_ffn_up_W, L0_ffn_up_qa, L0_ffn_up_qb, L0_ffn_up_scale, L0_ffn_down_W, L0_ffn_down_qa, L0_ffn_down_qb, L0_ffn_down_scale, L0_ffn_sh_gate_W, L0_ffn_sh_up_W, L0_ffn_sh_down_W, L1_attn_W_in, L1_attn_conv_w, L1_attn_conv_b, L1_attn_W_out, L1_attn_W_mlp1, L1_attn_W_mlp2, L1_xattn_Wq, L1_xattn_w_kc_q, L1_xattn_w_kc_kv, L1_xattn_W_qr, L1_xattn_W_kr, L1_xattn_Wo, L1_ffn_w_gate, L1_ffn_w_up, L1_ffn_w_down, L1_ffn_up_reorder_index, L1_ffn_down_reorder_index):
    import jax
    import jax.numpy as jnp

    def _L0_attn_ref(x, q1_w, k1_w, q2_w, k2_w, v_w, o_w, lambda_param):
        import jax, jax.numpy as jnp
        import numpy as np
        D_MODEL = 256
        NUM_HEADS = 16
        HEAD_DIM = D_MODEL // NUM_HEADS
        LAYER_IDX = 0
        NUM_LAYERS = 13
        REINIT_LAMBDA = 0.8

        def _heads(t, B, S):
            return t.reshape(B, S, NUM_HEADS, HEAD_DIM).transpose(0, 2, 1, 3)
        B, S, _ = x.shape
        q1 = _heads(x @ q1_w.T, B, S)
        k1 = _heads(x @ k1_w.T, B, S)
        q2 = _heads(x @ q2_w.T, B, S)
        k2 = _heads(x @ k2_w.T, B, S)
        v = _heads(x @ v_w.T, B, S)
        scale = jnp.sqrt(jnp.float32(HEAD_DIM))
        attn1 = jax.nn.softmax(jnp.einsum('bhqd,bhkd->bhqk', q1, k1) / scale, axis=-1)
        attn2 = jax.nn.softmax(jnp.einsum('bhqd,bhkd->bhqk', q2, k2) / scale, axis=-1)
        lam = lambda_param.reshape(1, NUM_HEADS, 1, 1)
        out = jnp.einsum('bhqk,bhkd->bhqd', attn1 - lam * attn2, v)
        out = out.transpose(0, 2, 1, 3).reshape(B, S, D_MODEL)
        return out @ o_w.T

    def _L0_xattn_ref(hidden_q, kv_c, Wq, w_kc_q, w_kc_kv, W_qr, W_kr, Wo):
        import jax, jax.numpy as jnp
        import numpy as np
        B, S, L = (2, 128, 128)
        DIM_Q, H, K, D_C, D_CQ, R = (256, 16, 128, 64, 192, 64)

        def _rope_tables(seq_len, dim, dtype):
            inv_freq = 1.0 / 10000.0 ** (jnp.arange(0, dim, 2, dtype=dtype) / dim)
            t = jnp.arange(seq_len, dtype=dtype)
            freqs = t[:, None] * inv_freq[None, :]
            sin = jnp.repeat(jnp.sin(freqs), 2, axis=-1)
            cos = jnp.repeat(jnp.cos(freqs), 2, axis=-1)
            return (sin, cos)

        def _rotate_half(x):
            h = x.shape[-1] // 2
            return jnp.concatenate([-x[..., h:], x[..., :h]], axis=-1)
        b, s, _ = hidden_q.shape
        l = kv_c.shape[1]
        q_hk = (hidden_q @ Wq.T).reshape(b, s, H, K)
        q_big = jnp.einsum('bshk,hkq->bshq', q_hk, w_kc_q)
        sin, cos = _rope_tables(l, D_C, kv_c.dtype)
        kv_rope = kv_c * cos[None] + _rotate_half(kv_c) * sin[None]
        q_r = jnp.einsum('bshq,hqr->bhsr', q_big, W_qr)
        k_r = jnp.einsum('bld,hdr->bhlr', kv_rope, W_kr)
        scores = jnp.einsum('bhsr,bhlr->bhsl', q_r, k_r)
        attn = jax.nn.softmax(scores, axis=-1)
        ctx_c = jnp.einsum('bhsl,bld->bhsd', attn, kv_rope)
        ctx_lat = jnp.einsum('bhsd,hkd->bshk', ctx_c, w_kc_kv)
        out = ctx_lat.reshape(b, s, H * K) @ Wo.T
        return out

    def _L0_ffn_ref(hidden_states, gate_weight, inv_mapping, mask_up_W, gate_W, gate_qa, gate_qb, gate_scale, up_W, up_qa, up_qb, up_scale, down_W, down_qa, down_qb, down_scale, sh_gate_W, sh_up_W, sh_down_W):
        import jax, jax.numpy as jnp
        import numpy as np
        B, S, H, I, E, F, K, R, TOPK = (1, 128, 256, 176, 64, 8, 8, 8, 6)
        ISH = 2 * I

        def _fused_linear(x, W, qa, qb, scale, w):
            out = x @ W.T
            a = jnp.einsum('th,krh->tkr', x, qa)
            b = jnp.einsum('tkr,khr->tkh', a, qb)
            mix = jnp.einsum('tkh,tk->th', b, w)
            return out + scale[None, :] * mix

        def _moe_forward(hidden_states, gate_weight, inv_mapping, mask_up_W, gate_W, gate_qa, gate_qb, gate_scale, up_W, up_qa, up_qb, up_scale, down_W, down_qa, down_qb, down_scale, sh_gate_W, sh_up_W, sh_down_W):
            b, s, h = hidden_states.shape
            x = hidden_states.reshape(-1, h)
            T = x.shape[0]
            scores = jax.nn.softmax(x @ gate_weight.T, axis=-1)
            topk_w, topk_idx = jax.lax.top_k(scores, TOPK)
            w_dense = jnp.zeros((T, E), x.dtype).at[jnp.arange(T)[:, None], topk_idx].add(topk_w)
            flat = w_dense[:, inv_mapping]
            scalar = flat.sum(-1)
            soft = jax.nn.softmax(jnp.where(flat == 0, -1000000000.0, flat), axis=-1)

            def expert(muW, gW, gqa, gqb, gs, uW, uqa, uqb, us, dW, dqa, dqb, ds, w):
                xe = x + w @ muW.T
                gate = jax.nn.silu(_fused_linear(xe, gW, gqa, gqb, gs, w))
                up = _fused_linear(xe, uW, uqa, uqb, us, w)
                return _fused_linear(gate * up, dW, dqa, dqb, ds, w)
            outs = jax.vmap(expert, in_axes=(0,) * 13 + (1,))(mask_up_W, gate_W, gate_qa, gate_qb, gate_scale, up_W, up_qa, up_qb, up_scale, down_W, down_qa, down_qb, down_scale, soft)
            y = jnp.einsum('fth,tf->th', outs, scalar).reshape(b, s, h)
            sh = jax.nn.silu(hidden_states @ sh_gate_W.T) * (hidden_states @ sh_up_W.T) @ sh_down_W.T
            return y + sh
        return _moe_forward(hidden_states, gate_weight, inv_mapping, mask_up_W, gate_W, gate_qa, gate_qb, gate_scale, up_W, up_qa, up_qb, up_scale, down_W, down_qa, down_qb, down_scale, sh_gate_W, sh_up_W, sh_down_W)

    def _L1_attn_ref(x, W_in, conv_w, conv_b, W_out, W_mlp1, W_mlp2):
        import jax, jax.numpy as jnp
        import numpy as np
        from jax import lax
        D_MODEL = 256
        D_INNER = 512
        D_CONV = 4
        B, T = (4, 256)

        def _rmsnorm(h):
            n = jnp.sqrt(jnp.sum(h * h, axis=-1, keepdims=True))
            return h / jnp.maximum(n, 1e-12) * h.shape[-1] ** 0.5

        def _mamba_fallback(h, W_in, conv_w, conv_b, W_out):
            xz = jnp.einsum('btd,ed->bte', h, W_in)
            xp, z = jnp.split(xz, 2, axis=-1)
            xc = lax.conv_general_dilated(xp.transpose(0, 2, 1), conv_w, window_strides=(1,), padding=[(D_CONV - 1, 0)], dimension_numbers=('NCH', 'OIH', 'NCH'), feature_group_count=D_INNER) + conv_b[None, :, None]
            xc = xc.transpose(0, 2, 1)
            y = jax.nn.silu(xc) * jax.nn.silu(z)
            return jnp.einsum('bte,de->btd', y, W_out)
        h = _rmsnorm(x)
        x = x + _mamba_fallback(h, W_in, conv_w, conv_b, W_out)
        h = _rmsnorm(x)
        m = jnp.einsum('bte,de->btd', jax.nn.relu(jnp.einsum('btd,ed->bte', h, W_mlp1)), W_mlp2)
        return x + m

    def _L1_xattn_ref(hidden_q, kv_c, Wq, w_kc_q, w_kc_kv, W_qr, W_kr, Wo):
        import jax, jax.numpy as jnp
        import numpy as np
        B, S, L = (2, 128, 128)
        DIM_Q, H, K, D_C, D_CQ, R = (256, 16, 128, 64, 192, 64)

        def _rope_tables(length, dim):
            inv = 1.0 / 10000.0 ** (jnp.arange(0, dim, 2, dtype=jnp.float32) / dim)
            f = jnp.arange(length, dtype=jnp.float32)[:, None] * inv[None, :]
            sin = jnp.repeat(jnp.sin(f), 2, axis=-1)
            cos = jnp.repeat(jnp.cos(f), 2, axis=-1)
            return (sin, cos)

        def _rotate_half(x):
            half = x.shape[-1] // 2
            return jnp.concatenate([-x[..., half:], x[..., :half]], axis=-1)

        def _apply_rope(x, sin, cos):
            return x * cos + _rotate_half(x) * sin
        Bv, Sv, _ = hidden_q.shape
        _, Lv, _ = kv_c.shape
        q_hk = (hidden_q @ Wq.T).reshape(Bv, Sv, H, K)
        q_big = jnp.einsum('bshk,hkq->bshq', q_hk, w_kc_q)
        sin_q, cos_q = _rope_tables(Sv, D_CQ)
        q_big = _apply_rope(q_big, sin_q[None, :, None, :], cos_q[None, :, None, :])
        sin_k, cos_k = _rope_tables(Lv, D_C)
        kv_r = _apply_rope(kv_c, sin_k[None], cos_k[None])
        q_r = jnp.einsum('bshq,hqr->bhsr', q_big, W_qr)
        k_r = jnp.einsum('bld,hdr->bhlr', kv_r, W_kr)
        scores = jnp.einsum('bhsr,bhlr->bhsl', q_r, k_r)
        attn = jax.nn.softmax(scores, axis=-1)
        ctx_c = jnp.einsum('bhsl,bld->bhsd', attn, kv_r)
        ctx_lat = jnp.einsum('bhsd,hkd->bhsk', ctx_c, w_kc_kv)
        ctx = ctx_lat.transpose(0, 2, 1, 3).reshape(Bv, Sv, H * K)
        return ctx @ Wo.T

    def _L1_ffn_ref(x, w_gate, w_up, w_down, up_reorder_index, down_reorder_index):
        import jax, jax.numpy as jnp
        import numpy as np
        FP8_MAX = 448.0
        GLOBAL_DIV = 448.0 * 6.0

        def _fp8(x):
            return x.astype(jnp.float8_e4m3fn).astype(jnp.float32)

        def _reorder_quantize_x(x, idx):
            scale = jnp.max(jnp.abs(x)) / GLOBAL_DIV
            xr = (x / scale)[:, idx]
            scale_x = jnp.max(jnp.abs(xr), axis=1, keepdims=True) / FP8_MAX
            qx = _fp8(xr / scale_x)
            return (qx, scale_x, scale)

        def _qlinear(qx, scale_x, scale, W, idx, out_idx=None):
            Wr = W[:, idx]
            w_scale = jnp.max(jnp.abs(Wr), axis=1, keepdims=True) / FP8_MAX
            qw = _fp8(Wr / w_scale)
            y = qx * scale_x @ (qw * w_scale).T * scale
            if out_idx is not None:
                y = y[:, out_idx]
            return y
        B, S, H = x.shape
        xf = x.reshape(B * S, H)
        qx, sx, sc = _reorder_quantize_x(xf, up_reorder_index)
        g = _qlinear(qx, sx, sc, w_gate, up_reorder_index, out_idx=down_reorder_index)
        u = _qlinear(qx, sx, sc, w_up, up_reorder_index, out_idx=down_reorder_index)
        t = jax.nn.silu(g) * u
        qt, st, sct = _reorder_quantize_x(t, down_reorder_index)
        y = _qlinear(qt, st, sct, w_down, down_reorder_index)
        return y.reshape(B, S, H)
    x = x + _L0_attn_ref(_layernorm(x, axis=-1), L0_attn_q1_w, L0_attn_k1_w, L0_attn_q2_w, L0_attn_k2_w, L0_attn_v_w, L0_attn_o_w, L0_attn_lambda_param)
    x = x + _L0_xattn_ref(_layernorm(x, axis=-1), ctx_512, L0_xattn_Wq, L0_xattn_w_kc_q, L0_xattn_w_kc_kv, L0_xattn_W_qr, L0_xattn_W_kr, L0_xattn_Wo)
    x = x + _L0_ffn_ref(_layernorm(x, axis=-1), L0_ffn_gate_weight, L0_ffn_inv_mapping, L0_ffn_mask_up_W, L0_ffn_gate_W, L0_ffn_gate_qa, L0_ffn_gate_qb, L0_ffn_gate_scale, L0_ffn_up_W, L0_ffn_up_qa, L0_ffn_up_qb, L0_ffn_up_scale, L0_ffn_down_W, L0_ffn_down_qa, L0_ffn_down_qb, L0_ffn_down_scale, L0_ffn_sh_gate_W, L0_ffn_sh_up_W, L0_ffn_sh_down_W)
    x = x + _L1_attn_ref(_layernorm(x, axis=-1), L1_attn_W_in, L1_attn_conv_w, L1_attn_conv_b, L1_attn_W_out, L1_attn_W_mlp1, L1_attn_W_mlp2)
    x = x + _L1_xattn_ref(_layernorm(x, axis=-1), ctx_512, L1_xattn_Wq, L1_xattn_w_kc_q, L1_xattn_w_kc_kv, L1_xattn_W_qr, L1_xattn_W_kr, L1_xattn_Wo)
    x = x + _L1_ffn_ref(_layernorm(x, axis=-1), L1_ffn_w_gate, L1_ffn_w_up, L1_ffn_w_down, L1_ffn_up_reorder_index, L1_ffn_down_reorder_index)
    return x

_drawn_inputs = setup_inputs


def setup_inputs(seed=0):
    import zlib

    import numpy as np

    out = dict(_drawn_inputs(seed))
    spreads = {'L0_attn_lambda_param': (0.0615384615957737, 0.6),
     'L0_ffn_gate_scale': (0.10000000149011612, 0.6),
     'L0_ffn_up_scale': (0.10000000149011612, 0.6),
     'L0_ffn_down_scale': (0.10000000149011612, 0.6),
     'L1_attn_conv_b': (0.0, 0.8)}
    factors = {'L0_attn_q1_w': 7.171,
     'L0_attn_k1_w': 6.715,
     'L0_attn_q2_w': 8.0,
     'L0_attn_k2_w': 8.0,
     'L0_attn_v_w': 3.497,
     'L0_attn_o_w': 3.497,
     'L0_ffn_gate_weight': 8.0,
     'L0_ffn_mask_up_W': 8.0,
     'L0_ffn_gate_W': 8.0,
     'L0_ffn_gate_qa': 8.0,
     'L0_ffn_gate_qb': 8.0,
     'L0_ffn_up_W': 8.0,
     'L0_ffn_up_qa': 8.0,
     'L0_ffn_up_qb': 8.0,
     'L0_ffn_down_W': 8.0,
     'L0_ffn_down_qa': 8.0,
     'L0_ffn_down_qb': 8.0,
     'L0_ffn_sh_gate_W': 4.427,
     'L0_ffn_sh_up_W': 4.428,
     'L0_ffn_sh_down_W': 4.369,
     'L1_attn_W_in': 8.0,
     'L1_attn_conv_w': 8.0,
     'L1_attn_W_out': 8.0,
     'L1_ffn_w_gate': 4.959,
     'L1_ffn_w_up': 4.569,
     'L1_ffn_w_down': 4.559,
     'L1_attn_W_mlp1': 2.872,
     'L1_xattn_Wq': 2.894,
     'L1_xattn_w_kc_q': 2.904,
     'L1_xattn_W_qr': 2.902,
     'L1_xattn_W_kr': 2.877}
    for name, (base, spread) in spreads.items():
        noise = np.random.default_rng([zlib.crc32(name.encode()), seed]).standard_normal(out[name].shape)
        drawn = base * np.exp(spread * noise) if base else spread * noise
        out[name] = jnp.asarray(drawn.astype(out[name].dtype))
    for name, factor in factors.items():
        out[name] = (out[name] * factor).astype(out[name].dtype)
    return out
```

```python
from contextlib import ExitStack

import concourse.bass as bass
from concourse import mybir

LAST_STAGE = 6

P = 128
NB, S, D = 4, 256, 256
T = NB * S
TB = S // P
NT = T // P
KD = D // P
H = 16
HD = D // H
LC = 512
LT = LC // P
DC, DCQ, R, KH = 64, 192, 64, 128
QH = DCQ // 2
EPS = 1e-5
DI, TAPS, MLP = 512, 4, 1024
XPAD = S + TAPS - 1
FI = 704
FC = (FI + P - 1) // P
FH = FI // 2
FP8_MAX = 448.0
FP8_NORMAL = 2.0 ** -6
FP8_ROUND = 1.5 * 2.0 ** 20
EXPONENT = 0x7F800000
TINY = 1e-30
NX, NE, MK, MR, MI, TOPK = 64, 8, 8, 8, 176, 6
ML = MI - P
MS = 352
ABSENT = -7.0
EGU, EQB, EGS, EQA, EDA, EDW, EDS, EXPERT = 0, 768, 1152, 1536, 1792, 1920, 2432, 2688
CQR, CKR, CKC, CWQ, CKV, CWO, CHUNK = 0, 768, 1024, 2048, 3072, 3328, 4352
SLOTS = 4

F32 = mybir.dt.float32
BF16 = mybir.dt.bfloat16
I32 = mybir.dt.int32
ALU = mybir.AluOpType
ACT = mybir.ActivationFunctionType
AX = mybir.AxisListType
RMAX = bass.bass_isa.ReduceOp.max


def carve(region, start, *dims, rows=P, base=0):
    n = 1
    for d in dims:
        n *= d
    ap = region[base:base + rows, start:start + n]
    names = ["a", "b", "c", "d"][:len(dims)]
    if len(dims) > 1:
        ap = ap.rearrange(f"p ({' '.join(names)}) -> p {' '.join(names)}",
                          **dict(zip(names[1:], dims[1:])))
    return ap


def carve_as(region, start, dt, *dims, rows=P, base=0):
    n = 1
    for d in dims:
        n *= d
    ap = region[base:base + rows, start:start + n // 2].bitcast(dt)
    names = ["a", "b", "c", "d"][:len(dims)]
    if len(dims) > 1:
        ap = ap.rearrange(f"p ({' '.join(names)}) -> p {' '.join(names)}",
                          **dict(zip(names[1:], dims[1:])))
    return ap


def schedule():
    ev = []
    add = lambda *e: ev.append(e)
    n = NB * H

    def folds(layer, c, part):
        if part == 0:
            add("fold_n", layer, c)
        elif part == 1 and layer == 0:
            add("fold_l", c)
        elif part == 2 and layer == 0:
            add("fold_z", c)
        elif part in (1, 2):
            add("fold_y", c, part - 1)
        elif part == 3:
            add("fold_u", layer, c)

    for b in range(NB):
        add("norm", "A", b)
    for b in range(NB):
        add("xt", "A", b)
    for w in "qkv":
        add("a_" + w, 0)
    for i in range(n + 8):
        if i < n:
            add("a_scores", i)
        if 1 <= i <= n:
            add("a_mix", i - 1)
        if 2 <= i <= n + 1:
            add("a_turn", i - 2)
        if i < n and i % H == H // 2 and i // H + 1 < NB:
            for w in "qkv":
                add("a_" + w, i // H + 1)
        if LAST_STAGE >= 2:
            if 2 <= i < 2 + NB:
                add("kv_turn", i - 2)
            if i < n and 9 <= i % H < 13:
                folds(0, i // H, i % H - 9)
        if i >= 6 and (i - 6) % 4 == 0 and (i - 6) // 4 < n // 4:
            g = (i - 6) // 4
            add("a_heads", g)
            if g % 4 == 3:
                add("a_out", g // 4)
                add("norm", "B", g // 4)

    def latent(L):
        nxt = "CF"[L]
        prepare = {1: ("w_start",), 22: ("w_count",), 24: ("w_dmax",), 25: ("w_dall",), 26: ("w_quant", 2)}
        for a in range(2):
            for k, e in enumerate((("w_quant", a), ("w_turn", a), ("w_gather", a, 0), ("w_gather", a, 1),
                                   ("w_row", a))):
                prepare[30 + 12 * a + 2 * k] = e

        def queries(b, part):
            if L == 0:
                if part % 8 == 4:
                    add("x_q", b, part // 8)
            elif part % 2 == 0:
                add("r_g", b, part // 2)
            else:
                add("r_q", b, part // 2)

        for b in range(NB):
            add("xt", "BE"[L], b)
        for part in range(H):
            queries(0, part)
        for i in range(n + 4):
            if i < n:
                add("x_scores", L, i)
            if 1 <= i <= n:
                add("x_norm", L, i - 1)
            if 2 <= i <= n + 1:
                add("x_turn", L, i - 2)
            if i < n and i // H + 1 < NB:
                queries(i // H + 1, i % H)
            if L == 1 and LAST_STAGE >= 6 and i in prepare:
                add(*prepare[i])
            if i >= 4 and i % 2 == 0 and (i - 4) // 2 < n // 2:
                g = (i - 4) // 2
                add("x_heads", L, g)
                if g % 8 == 7:
                    add("x_out", L, g // 8)
                    add("norm", nxt, g // 8)

    if LAST_STAGE >= 2:
        latent(0)

    if LAST_STAGE >= 3:
        for b in range(NB):
            add("xt", "C", b)
        for part in ("m_gate", "m_wdt", "m_flat", "m_wt"):
            for b in range(NB):
                add(part, b)
        for b in range(NB + 1):
            if b < NB:
                add("m_sg", b)
                add("m_su", b)
            if b >= 1:
                add("m_sy", b - 1)
        m = [(f, b) for f in range(NE) for b in range(NB)]
        for i in range(len(m) + 3):
            if i < len(m):
                add("m_xe", *m[i])
            if 1 <= i <= len(m):
                add("m_a", *m[i - 1])
                add("m_g", *m[i - 1])
            if 2 <= i <= len(m) + 1:
                add("m_a2", *m[i - 2])
            if i >= 3:
                f, b = m[i - 3]
                add("m_y", f, b)
                if f == NE - 1:
                    add("norm", "D", b)

    if LAST_STAGE >= 4:
        for b in range(NB):
            add("norm", "G", b)
        for t in range(NB + 3):
            if t < NB:
                add("xt", "G", t)
                add("d_x", t)
                add("d_z", t)
            if 1 <= t <= NB:
                add("d_out", t - 1)
                add("norm", "H", t - 1)
            if 2 <= t < NB + 2:
                add("xt", "H", t - 2)
                add("d_m1", t - 2, 0)
                add("d_m1", t - 2, 1)
                add("d_m2", t - 2)
                add("norm", "E", t - 2)
            if 3 <= t and LAST_STAGE >= 5:
                for part in range(4):
                    folds(1, t - 3, part)
    if LAST_STAGE >= 5:
        latent(1)

    if LAST_STAGE >= 6:
        def tokens(b):
            add("f_quant", b)
            add("f_xt", b)
            add("f_sel", b)

        tokens(0)
        for t in range(NT + 5):
            if t < NT:
                add("f_g", t)
                add("f_u", t)
                if t % TB == 0 and t // TB + 1 < NB:
                    tokens(t // TB + 1)
            if 1 <= t <= NT:
                add("f_scale", t - 1)
                add("f_exponent", t - 1)
            if 2 <= t <= NT + 1:
                add("f_round", t - 2)
            if t >= 4 and t - 4 < NT:
                add("f_y", t - 4)
            if 3 <= t <= NT + 2:
                add("f_t", t - 3)
    return ev


PE_STEPS = {"xt", "a_q", "a_k", "a_v", "a_scores", "a_turn", "a_heads", "a_out",
            "kv_turn", "fold_n", "fold_l", "fold_z", "fold_y", "fold_u",
            "m_gate", "m_wdt", "m_flat", "m_wt", "m_sg", "m_su", "m_sy", "m_xe", "m_a", "m_g", "m_a2", "m_y",
            "d_x", "d_z", "d_out", "d_m1", "d_m2",
            "w_count", "w_turn", "w_gather", "w_row", "f_xt", "f_sel", "f_g", "f_u", "f_t", "f_y",
            "x_q", "x_scores", "x_turn", "x_heads", "x_out", "r_g", "r_q"}


def decoder(nc, d, out):
    steps = schedule()
    slot_of, use_of = {}, {}
    count = 0
    for e in steps:
        if e[0] in PE_STEPS:
            slot_of[e], use_of[e] = count % SLOTS, count // SLOTS
            count += 1
    norm_no = {e[1:]: n for n, e in enumerate(e for e in steps if e[0] == "norm")}
    xt_no = {e[1:]: n for n, e in enumerate(e for e in steps if e[0] == "xt")}

    with ExitStack() as ctx:
        def sb(name, shape, dt=F32):
            return ctx.enter_context(nc.sbuf_tensor(name, shape, dt))

        def sem(name):
            return ctx.enter_context(nc.semaphore(name))

        X = sb("X", [P, NT, D])
        XN = sb("XN", [P, NT, D])
        XT = sb("XT", [P, KD, T])
        ident = sb("ident", [P, P])
        work = sb("work", [P, 22 * 1024])
        stats = sb("stats", [P, 2, TB, 6])
        mv = sb("mv", [P, 2, TB, 2])
        rstd = sb("rstd", [P, 2, 2, TB])
        neg_half = sb("neg_half", [P, TB])
        psum = [ctx.enter_context(nc.psum_tensor(f"slot{s}", [P, 1024], F32)) for s in range(SLOTS)]

        def view(e, *dims, rows=P, base=0):
            return carve(psum[slot_of[e]], 0, *dims, rows=rows, base=base)

        o = 0
        a_wq = carve(work, o, KD, 4, P); o += 1024
        a_wk = carve(work, o, KD, 4, P); o += 1024
        a_wv = carve(work, o, KD, D); o += 512
        a_wo = carve(work, o, 4, D); o += 1024
        a_Q = carve(work, o, 2, 4, S); o += 2048
        a_K = carve(work, o, 2 * 4, 2, S); o += 4096
        a_V = carve(work, o, 2, TB, H * 32); o += 2048
        a_P = carve(work, o, 3, 2 * TB, S); o += 3072
        a_A = carve(work, o, 3, TB, S); o += 1536
        a_AT = carve(work, o, 8, TB, S); o += 4096
        a_OT = carve(work, o, 4, S); o += 1024
        kvr = sb("kvr", [P, NB * LT, 2, DC])
        kvT = sb("kvT", [P, NB, LC])
        staged = sb("staged", [P, 2, CHUNK])
        fold = sb("fold", [P, 10 * 1024])
        Z = carve(fold, 0, KD, H * DC)
        Y = carve(fold, 0, KD, H, DCQ)
        N = carve(fold, KD * H * DCQ, H, 2, DC, rows=QH)
        U = carve(fold, KD * H * DCQ + H * 2 * DC, H // 2, D)
        x_Q = carve(work, 0, 2, H // 2, S)
        x_P = carve(work, 4096, 3, TB, LC)
        x_PT = carve(work, 7168, 4, LT, S)
        x_C = carve(work, 11264, H // 2, S)
        r_R = carve(work, 13312, 2 * 2, 2, S, rows=QH)
        r_M = carve(work, 15360, 2 * 2, 2, S, rows=QH)
        r_cos = carve(work, 21504, 2, S, rows=QH)
        r_sin = carve(work, 22016, 2, S, rows=QH)
        kv = carve(fold, 2048, NB * LT, DC)
        kv_m = carve(fold, 3072, NB * LT, DC)
        k_cos = carve(fold, 4096, LT, DC)
        k_sin = carve(fold, 4352, LT, DC)
        L = sb("L", [P, 4, DC])
        expert = staged[:, :, :].rearrange("p a b -> p (a b)")[:, 0:2 * EXPERT].rearrange("p (a b) -> p a b", a=2)
        m_mu = carve(work, 20480, NE, D, rows=NX)
        m_sgw = carve(fold, 2048, KD, 3 * P)
        m_suw = carve(fold, 2816, KD, 3 * P)
        m_sdw = carve(fold, 3584, 3, D)
        m_pick = carve(fold, 4352, NE, P, rows=NX)
        m_gw = carve(fold, 5376, KD, NX)
        m_sel = carve(fold, 5504, NX, rows=NX)
        m_inv = sb("m_inv", [NX, NX], I32)
        lane = sb("lane", [P, 1])
        w_W = carve(staged[:, :, :].rearrange("p a b -> p (a b)"), 0, 3, FC, D)
        flat_staged = staged[:, :, :].rearrange("p a b -> p (a b)")
        w_tmp = carve(flat_staged, 4608, FC, D)
        w_Q = carve_as(flat_staged, 6144, BF16, FC, D)
        w_QT = carve_as(flat_staged, 6912, BF16, KD, FI)
        w_sel = carve_as(flat_staged, 7616, BF16, KD, D)
        w_hit = carve_as(flat_staged, 7872, BF16, KD, D)
        w_urow = carve(flat_staged, 8128, D).bitcast(I32)
        w_iota = carve(flat_staged, 8384, D)
        w_in = [carve_as(work, 17408 + 704 * a, BF16, KD, FI) for a in range(2)]
        w_rows = [carve(work, 18816 + 704 * a, FI) for a in range(2)]
        w_drow = carve(work, 20224, D)
        w_down = carve_as(work, 20480, BF16, FC, D)
        w_mask = carve(work, 21248, D)
        w_didx = sb("w_didx", [P, FC], I32)
        w_ddidx = sb("w_ddidx", [P, FC], I32)
        w_uidx = sb("w_uidx", [P, KD], I32)
        w_uidxf = sb("w_uidxf", [P, KD])
        w_max = sb("w_max", [P, 3, FC])
        lanes = sb("lanes", [P, KD])
        ones16 = sb("ones16", [P, P], BF16)
        ident16 = sb("ident16", [P, P], BF16)
        o = 0
        f_X = carve(work, o, 2, TB, D); o += 1024
        f_Xt = carve(work, o, TB, D); o += 512
        f_XQ = carve_as(work, o, BF16, 2, TB, D); o += 512
        f_XT = carve_as(work, o, BF16, 2, KD, S); o += 512
        f_XS = carve_as(work, o, BF16, 2, KD, S); o += 512
        f_G = carve(work, o, 2, FI); o += 2 * FI
        f_SG = carve(work, o, 2, FI); o += 2 * FI
        f_T = carve(work, o, 4, FI); o += 4 * FI
        f_E = carve(work, o, 4, FI); o += 4 * FI
        f_TQ = carve_as(work, o, BF16, 2, FI); o += FI
        f_TT = carve_as(work, o, BF16, 2, FC, P); o += FC * P
        f_Y = carve(work, o, 2, D); o += 512
        f_s = sb("f_s", [P, 2, 3, NT])
        d_win = carve(work, 13312, KD, 2 * DI)
        d_wout = carve(work, 15360, DI // P, D)
        d_w1 = carve(work, 16384, KD, MLP)
        d_w2 = carve(work, 18432, MLP // P, D)
        d_conv = sb("d_conv", [P, DI // P, TAPS])
        d_bias = sb("d_bias", [P, DI // P])
        o = 0
        d_N = carve(work, o, 2 * TB, D); o += 1024
        d_J = carve(work, o, D); o += 256
        d_XP = carve(work, o, 2, DI // P, XPAD); o += 2 * DI // P * XPAD
        d_C = carve(work, o, 2, DI // P, S); o += 2048
        d_Z = carve(work, o, 2, DI // P, S); o += 2048
        d_M = carve(work, o, 2, MLP // P, S); o += 4096
        o = 0
        m_E = carve(work, o, NT, NX); o += 512
        m_sc = carve(work, o, NT, NX + 2); o += 528
        m_rep = carve(work, o, NT, NX + 2); o += 528
        m_wd = carve(work, o, NT, NX); o += 512
        m_wdT = carve(work, o, T, rows=NX); o += 1024
        m_flat = carve(work, o, NT, NX); o += 512
        m_val = carve(work, o, NT, NX); o += 512
        m_ex = carve(work, o, NT, NX); o += 512
        m_w = carve(work, o, NT, NX); o += 512
        m_WT = carve(work, o, T, rows=NX); o += 1024
        m_t8 = carve(work, o, NT, 8); o += 64
        m_scal = carve(work, o, NT, NE); o += 64
        m_mx = carve(work, o, NT, NE); o += 64
        m_sum = carve(work, o, NT, NE); o += 64
        m_rsum = carve(work, o, NT, NE); o += 64
        m_nm = carve(work, o, NT); o += 8
        m_rs = carve(work, o, NT); o += 8
        m_r = carve(work, o, NT); o += 8
        m_XE = carve(work, o, 2, KD, S); o += 1024
        m_WX = carve(work, o, 2, S); o += 512
        m_AW = carve(work, o, 2, S); o += 512
        m_SG = carve(work, o, 2, 2, S); o += 1024
        m_H = carve(work, o, 2, 2, S); o += 1024
        m_SS = carve(work, o, 2, 3, S); o += 1536
        m_HS = carve(work, o, 2, 3, S); o += 1536
        x_nm = sb("x_nm", [P, 4, TB])
        x_rs = sb("x_rs", [P, 4, TB])
        x_r = sb("x_r", [P, 4, TB])
        kmask = sb("kmask", [P, 2])
        neg_lambda = sb("neg_lambda", [P, H])
        a_nm = sb("a_nm", [P, 4, 2 * TB])
        a_rs = sb("a_rs", [P, 4, 2 * TB])
        a_r = sb("a_r", [P, 4, 2 * TB])
        a_c = sb("a_c", [P, 4, TB])

        slot_full = [sem(f"slot_full{s}") for s in range(SLOTS)]
        slot_free = [sem(f"slot_free{s}") for s in range(SLOTS)]
        dve_step = sem("dve_step")
        pool_step = sem("pool_step")
        x_loaded = sem("x_loaded")
        consts_loaded = sem("consts_loaded")
        a_weights = sem("a_weights")
        half_set = sem("half_set")
        norm_stats = sem("norm_stats")
        norm_rstd = sem("norm_rstd")
        normed = sem("normed")
        a_v_zeroed = sem("a_v_zeroed")
        a_max_ready = sem("a_max_ready")
        kv_loaded = sem("kv_loaded")
        kv_roped = sem("kv_roped")
        chunk_loaded = [[sem(f"chunk_loaded_{a}{c}") for c in range(4)] for a in range(2)]
        x_max_ready = sem("x_max_ready")
        d_loaded = sem("d_loaded")
        d_conv_ready = sem("d_conv_ready")
        d_silu_ready = sem("d_silu_ready")
        d_gated = sem("d_gated")
        d_added = sem("d_added")
        r_tables = sem("r_tables")
        w_indices = sem("w_indices")
        w_chained = sem("w_chained")
        w_fetched = [sem(f"w_fetched{a}") for a in range(3)]
        w_zeroed = sem("w_zeroed")
        w_tables = sem("w_tables")
        w_dmax_ready = sem("w_dmax_ready")
        w_dall_ready = sem("w_dall_ready")
        w_quantised = sem("w_quantised")
        f_xq_ready = sem("f_xq_ready")
        f_silu = sem("f_silu")
        f_product = sem("f_product")
        f_inverse = sem("f_inverse")
        f_scaled = sem("f_scaled")
        f_exponents = sem("f_exponents")
        f_summed = sem("f_summed")
        f_rounded = sem("f_rounded")
        x_done = sem("x_done")
        r_ready = sem("r_ready")
        m_loaded = sem("m_loaded")
        m_inv_loaded = sem("m_inv_loaded")
        expert_loaded = [sem(f"expert_loaded{f}") for f in range(NE)]
        expert_scaled = sem("expert_scaled")
        m_sel_ready = sem("m_sel_ready")
        m_max_ready = sem("m_max_ready")
        m_wd_ready = sem("m_wd_ready")
        m_val_ready = sem("m_val_ready")
        m_ex_ready = sem("m_ex_ready")
        m_w_ready = sem("m_w_ready")
        m_wx_ready = sem("m_wx_ready")
        m_silu_ready = sem("m_silu_ready")
        m_shared_silu = sem("m_shared_silu")
        m_pads = sem("m_pads")
        x_norm_ready = sem("x_norm_ready")
        a_mix_ready = sem("a_mix_ready")
        out_stored = sem("out_stored")
        x_final = sem("x_final")

        def full(eng, e):
            eng.wait_ge(slot_full[slot_of[e]], use_of[e] + 1)

        def free(ins, e):
            ins.then_inc(slot_free[slot_of[e]], 1)

        def taken(eng, e):
            eng.wait_ge(slot_free[slot_of[e]], use_of[e] + 1)

        block = ctx.enter_context(nc.Block())

        @block.sync
        def _(sp):
            sp.dma_start(X[:, :, :], d["x"].rearrange("b (t p) d -> p (b t) d", p=P)).then_inc(x_loaded, 16)
            sp.dma_start(ident[:, :], d["ident"]).then_inc(consts_loaded, 16)
            sp.dma_start(kmask[:, :], d["kmask"]).then_inc(consts_loaded, 16)
            sp.dma_start(neg_lambda[:, :], d["a_lambda"].partition_broadcast(P)).then_inc(consts_loaded, 16)
            sp.dma_start(a_wq, d["a_wq"]).then_inc(a_weights, 16)
            sp.dma_start(a_wk, d["a_wk"]).then_inc(a_weights, 16)
            sp.dma_start(a_wv, d["a_wv"]).then_inc(a_weights, 16)
            sp.dma_start(a_wo, d["a_wo"]).then_inc(a_weights, 16)
            if LAST_STAGE >= 2:
                sp.dma_start(kv, d["kv"].rearrange("b (t p) d -> p (b t) d", p=P)).then_inc(kv_loaded, 16)
                sp.dma_start(k_cos, d["k_cos"]).then_inc(kv_loaded, 16)
                sp.dma_start(k_sin, d["k_sin"]).then_inc(kv_loaded, 16)
                for c in range(4):
                    if c >= 2:
                        full(sp, ("fold_u", 0, c - 2))
                    sp.dma_start(staged[:, c % 2, :], d["chunks"][c]).then_inc(chunk_loaded[0][c], 16)
            if LAST_STAGE >= 3:
                sp.dma_start(m_inv[:, :], d["m_inv"].partition_broadcast(NX)).then_inc(m_inv_loaded, 16)
                sp.dma_start(lane[:, :], d["lane"]).then_inc(m_inv_loaded, 16)
                sp.wait_ge(kv_roped, NB)
                sp.dma_start(m_sgw, d["m_sgw"]).then_inc(m_loaded, 16)
                sp.dma_start(m_suw, d["m_suw"]).then_inc(m_loaded, 16)
                sp.dma_start(m_sdw, d["m_sdw"]).then_inc(m_loaded, 16)
                sp.dma_start(m_pick, d["m_pick"]).then_inc(m_loaded, 16)
                sp.dma_start(m_gw, d["m_gw"]).then_inc(m_loaded, 16)
                taken(sp, ("a_out", NB - 1))
                sp.dma_start(m_mu, d["m_mu"]).then_inc(m_loaded, 16)
                for f in range(NE):
                    if f < 2:
                        full(sp, ("fold_u", 0, 2 + f))
                    else:
                        full(sp, ("m_y", f - 2, NB - 1))
                        sp.wait_ge(expert_scaled, 2 * (f - 1))
                    if f == 0:
                        full(sp, ("fold_u", 0, 3))
                    sp.dma_start(expert[:, f % 2, :], d["m_experts"][f]).then_inc(expert_loaded[f], 16)
            if LAST_STAGE >= 4:
                sp.dma_start(d_win, d["d_win"]).then_inc(d_loaded, 16)
                sp.dma_start(d_wout, d["d_wout"]).then_inc(d_loaded, 16)
                sp.dma_start(d_w1, d["d_w1"]).then_inc(d_loaded, 16)
                sp.dma_start(d_w2, d["d_w2"]).then_inc(d_loaded, 16)
                sp.dma_start(d_conv[:, :, :], d["d_conv"]).then_inc(d_loaded, 16)
                sp.dma_start(d_bias[:, :], d["d_bias"]).then_inc(d_loaded, 16)
            if LAST_STAGE >= 5:
                full(sp, ("m_y", NE - 1, NB - 1))
                for c in range(4):
                    if c >= 2:
                        full(sp, ("fold_u", 1, c - 2))
                    sp.dma_start(staged[:, c % 2, :], d["chunks"][4 + c]).then_inc(chunk_loaded[1][c], 16)
                    if c == 1:
                        sp.dma_start(r_cos, d["r_cos"]).then_inc(r_tables, 16)
                        sp.dma_start(r_sin, d["r_sin"]).then_inc(r_tables, 16)
            if LAST_STAGE >= 6:
                sp.dma_start(lanes[:, :], d["lanes"]).then_inc(w_indices, 16)
                sp.dma_start(w_uidx[:, :], d["f_ucol"]).then_inc(w_indices, 16)
                sp.dma_start(w_didx[:, :], d["f_dcol"]).then_inc(w_indices, 16)
                full(sp, ("fold_u", 1, 3))
                sp.dma_start(w_urow, d["f_uidx"].partition_broadcast(P)).then_inc(w_indices, 16)
                sp.dma_start(w_iota, d["iota"]).then_inc(w_indices, 16)
                for b in range(NB):
                    sp.wait_ge(x_done, TB * (b + 1))
                    sp.dma_start(out[b].rearrange("(t p) d -> p t d", p=P), X[:, TB * b:TB * b + TB, :])\
                        .then_inc(out_stored, 16)
                sp.wait_ge(out_stored, 16 * NB)
            else:
                sp.wait_ge(x_final, 1)
                sp.dma_start(out.rearrange("b (t p) d -> p (b t) d", p=P), X[:, :, :]).then_inc(out_stored, 16)
                sp.wait_ge(out_stored, 16)

        @block.gpsimd
        def _(pool):
            pool.memset(neg_half[:, :], -0.5).then_inc(half_set, 1)
            pool.memset(a_V, 0.0).then_inc(a_v_zeroed, 1)
            pool.wait_ge(half_set, 1)
            steps_done = [0]

            def norm(e):
                _, kind, b = e
                n = norm_no[(kind, b)]
                pool.wait_ge(norm_stats, n + 1)
                if kind in "GH":
                    ins = pool.tensor_scalar(rstd[:, n % 2, 0, :], mv[:, n % 2, :, 1], 1e-24, 1.0 / D,
                                             ALU.max, ALU.mult)
                else:
                    ins = pool.tensor_scalar(rstd[:, n % 2, 0, :], mv[:, n % 2, :, 1], EPS, None, ALU.add)
                ins.then_inc(pool_step, 1)
                steps_done[0] += 1
                pool.wait_ge(pool_step, steps_done[0])
                pool.tensor_tensor(rstd[:, n % 2, 1, :], rstd[:, n % 2, 0, :], neg_half[:, :], ALU.pow)\
                    .then_inc(norm_rstd, 1)

            def rope_kv(b):
                t = slice(LT * b, LT * b + LT)
                h = DC // 2
                ro = kvr[:, t, 0, :]
                pool.tensor_tensor(ro, kv[:, t, :], k_cos, ALU.mult).then_inc(pool_step, 1)
                pool.tensor_tensor(kv_m[:, t, 0:h], kv[:, t, h:DC], k_sin[:, :, 0:h], ALU.mult).then_inc(pool_step, 1)
                pool.tensor_tensor(kv_m[:, t, h:DC], kv[:, t, 0:h], k_sin[:, :, h:DC], ALU.mult)\
                    .then_inc(pool_step, 1)
                steps_done[0] += 3
                pool.wait_ge(pool_step, steps_done[0])
                pool.tensor_tensor(ro, ro, kv_m[:, t, :], ALU.add).then_inc(pool_step, 1)
                steps_done[0] += 1
                pool.wait_ge(pool_step, steps_done[0])
                pool.tensor_copy(kvr[:, t, 1, :], ro).then_inc(kv_roped, 1)

            if LAST_STAGE >= 2:
                norm(steps[0])
                pool.wait_ge(kv_loaded, 48)
                for b in range(NB):
                    rope_kv(b)
            def scale_expert(f):
                w = expert[:, f % 2, :]
                pool.wait_ge(expert_loaded[f], 16)
                pool.tensor_tensor(w[:, EQB:EQB + 3 * P], w[:, EQB:EQB + 3 * P], w[:, EGS:EGS + 3 * P], ALU.mult)\
                    .then_inc(expert_scaled, 1)
                pool.tensor_tensor(w[:, EDW + D:EDW + 2 * D], w[:, EDW + D:EDW + 2 * D],
                                   w[:, EDS:EDS + D], ALU.mult).then_inc(expert_scaled, 1)

            def w_start(e):
                full(pool, ("fold_u", 1, 3))
                for a in range(3):
                    pool.memset(w_W[:, a, FC - 1, :], 0.0).then_inc(w_zeroed, 1)
                pool.wait_ge(w_indices, 80)
                sizes = [P] * (FC - 1) + [FI - (FC - 1) * P]
                for c, n in enumerate(sizes):
                    pool.indirect_dma_start(w_ddidx[0:n, c:c + 1], None, d["f_didx"],
                                            bass.IndirectOffsetOnAxis(ap=w_didx[0:n, c:c + 1], axis=0))\
                        .then_inc(w_chained, 16)
                pool.wait_ge(w_zeroed, 3)
                for c, n in enumerate(sizes):
                    pool.indirect_dma_start(w_W[0:n, 2, c, :], None, d["f_down"],
                                            bass.IndirectOffsetOnAxis(ap=w_didx[0:n, c:c + 1], axis=0))\
                        .then_inc(w_fetched[2], 16)
                pool.wait_ge(w_chained, 16 * FC)
                for a, name in enumerate(("f_gate", "f_up")):
                    for c, n in enumerate(sizes):
                        pool.indirect_dma_start(w_W[0:n, a, c, :], None, d[name],
                                                bass.IndirectOffsetOnAxis(ap=w_ddidx[0:n, c:c + 1], axis=0))\
                            .then_inc(w_fetched[a], 16)

            def w_dall(e):
                pool.wait_ge(w_dmax_ready, 1)
                pool.partition_all_reduce(w_drow, w_tmp[:, 0, :], P, RMAX).then_inc(w_dall_ready, 1)

            def f_u(e):
                n = e[1]
                taken(pool, e)
                pool.wait_ge(f_silu, n + 1)
                pool.tensor_tensor(f_T[:, n % 4, :], f_T[:, n % 4, :], f_SG[:, n % 2, :], ALU.mult)\
                    .then_inc(f_product, 1)

            def f_exponent(e):
                n = e[1]
                pool.wait_ge(f_exponents, n + 1)
                pool.tensor_scalar(f_E[:, n % 4, :], f_E[:, n % 4, :], FP8_NORMAL, FP8_ROUND, ALU.max, ALU.mult)\
                    .then_inc(pool_step, 1)
                steps_done[0] += 1
                pool.wait_ge(pool_step, steps_done[0])
                pool.tensor_tensor(f_T[:, n % 4, :], f_T[:, n % 4, :], f_E[:, n % 4, :], ALU.add)\
                    .then_inc(f_summed, 1)

            def f_y(e):
                n = e[1]
                taken(pool, e)
                pool.tensor_tensor(X[:, n, :], X[:, n, :], f_Y[:, n % 2, :], ALU.add).then_inc(x_done, 1)

            tail = {"w_start": w_start, "w_dall": w_dall, "f_u": f_u, "f_exponent": f_exponent, "f_y": f_y}
            for e in steps[1 if LAST_STAGE >= 2 else 0:]:
                if e[0] == "norm":
                    norm(e)
                if e[0] in tail:
                    tail[e[0]](e)
                if e[0] == "d_z":
                    b = e[1]
                    pool.wait_ge(d_silu_ready, b + 1)
                    pool.tensor_tensor(d_C[:, b % 2], d_C[:, b % 2], d_Z[:, b % 2], ALU.mult).then_inc(d_gated, 1)
                if e[0] == "r_g":
                    j = H // 2 * e[1] + e[2]
                    r = slice(2 * (j % 2), 2 * (j % 2) + 2)
                    taken(pool, e)
                    pool.tensor_tensor(r_R[:, r], r_R[:, r], r_M[:, r], ALU.add).then_inc(r_ready, 1)
                if e[0] == "m_gate" and e[1] == 0:
                    scale_expert(0)
                    scale_expert(1)
                if e[0] == "m_y" and e[2] == NB - 1 and e[1] + 2 < NE:
                    scale_expert(e[1] + 2)

        @block.scalar
        def _(act):
            def xt(e):
                b = e[2]
                full(act, e)
                free(act.activation(XT[:, :, b * S:(b + 1) * S], view(e, KD, S), ACT.Copy), e)

            def a_q(e):
                b = e[1]
                full(act, e)
                free(act.activation(a_Q[:, b % 2], view(e, 4, S), ACT.Copy), e)

            def a_v(e):
                b = e[1]
                full(act, e)
                act.wait_ge(a_v_zeroed, 1)
                for t in range(TB):
                    dst = a_V[:, b % 2, t, :].rearrange("p (h c) -> p h c", c=32)[:, :, 0:HD]
                    src = view(e, TB, H, HD)[:, t]
                    ins = act.activation(dst, src, ACT.Copy)
                free(ins, e)

            def a_scores(e):
                i = e[1]
                full(act, e)
                act.wait_ge(a_max_ready, i + 1)
                if i >= 3:
                    act.wait_ge(a_mix_ready, i - 2)
                s = view(e, 2 * TB, S)
                for j in range(2 * TB):
                    ins = act.activation(a_P[:, i % 3, j, :], s[:, j, :], ACT.Exp,
                                         bias=a_nm[:, i % 4, j:j + 1], accum_out=a_rs[:, i % 4, j:j + 1])
                free(ins, e)

            def a_turn(e):
                i = e[1]
                full(act, e)
                free(act.activation(a_AT[:, i % 8], view(e, TB, S), ACT.Copy), e)

            def a_heads(e):
                g = e[1]
                full(act, e)
                free(act.activation(a_OT[:, g % 4, :], view(e, S), ACT.Copy), e)

            def copy_to(dst, *dims, **kw):
                def f(e):
                    full(act, e)
                    free(act.activation(dst(e), view(e, *dims, **kw), ACT.Copy), e)
                return f

            def x_scores(e):
                _, lay, i = e
                n = lay * NB * H + i
                full(act, e)
                act.wait_ge(x_max_ready, n + 1)
                if i >= 3:
                    full(act, ("x_turn", lay, i - 3))
                s = view(e, TB, LC)
                for j in range(TB):
                    ins = act.activation(x_P[:, i % 3, j, :], s[:, j, :], ACT.Exp,
                                         bias=x_nm[:, i % 4, j:j + 1], accum_out=x_rs[:, i % 4, j:j + 1])
                free(ins, e)

            def m_gate(e):
                b = e[1]
                full(act, e)
                act.wait_ge(m_max_ready, b + 1)
                for t in range(TB):
                    n = TB * b + t
                    ins = act.activation(m_E[:, n, :], view(e, TB, NX)[:, t], ACT.Exp, bias=m_nm[:, n:n + 1],
                                         accum_out=m_rs[:, n:n + 1])
                free(ins, e)

            def m_flat(e):
                b = e[1]
                act.wait_ge(m_val_ready, b + 1)
                act.activation(m_ex[:, TB * b:TB * b + TB, :], m_val[:, TB * b:TB * b + TB, :], ACT.Exp)\
                    .then_inc(m_ex_ready, 1)

            def m_su(e):
                b = e[1]
                g = ("m_sg", b)
                full(act, g)
                if b >= 2:
                    taken(act, ("m_su", b - 2))
                free(act.activation(m_SS[:, b % 2], view(g, 3, S), ACT.Silu), g)

            def m_a(e):
                _, f, b = e
                i = NB * f + b
                full(act, e)
                if i >= 2:
                    taken(act, ("m_a2", *divmod(i - 2, NB)))
                act.activation(m_WX[:, i % 2, :], view(e, 2, S)[:, 1], ACT.Copy).then_inc(m_wx_ready, 1)

            def m_g(e):
                _, f, b = e
                i = NB * f + b
                full(act, e)
                if i >= 2:
                    taken(act, ("m_g", *divmod(i - 2, NB)))
                o = view(e, 3, S)
                act.activation(m_SG[:, i % 2, 0, :], o[:, 0], ACT.Silu)
                act.activation(m_SG[0:ML, i % 2, 1, :], o[0:ML, 2], ACT.Silu).then_inc(m_silu_ready, 1)

            def d_x(e):
                b = e[1]
                full(act, e)
                if b == 0:
                    act.wait_ge(m_pads, 1)
                    act.wait_ge(d_loaded, 96)
                if b >= 2:
                    act.wait_ge(d_conv_ready, b - 1)
                free(act.activation(d_XP[:, b % 2, :, TAPS - 1:XPAD], view(e, DI // P, S), ACT.Copy), e)

            def d_z(e):
                b = e[1]
                full(act, e)
                if b >= 2:
                    act.wait_ge(d_gated, b - 1)
                free(act.activation(d_Z[:, b % 2], view(e, DI // P, S), ACT.Silu), e)
                act.wait_ge(d_conv_ready, b + 1)
                for c in range(DI // P):
                    ins = act.activation(d_C[:, b % 2, c, :], d_C[:, b % 2, c, :], ACT.Silu, bias=d_bias[:, c:c + 1])
                ins.then_inc(d_silu_ready, 1)

            def d_m1(e):
                _, b, half = e
                full(act, e)
                free(act.activation(d_M[:, b % 2, 4 * half:4 * half + 4, :], view(e, 4, S), ACT.Relu), e)

            def fold_y(e):
                _, c, a = e
                full(act, e)
                for h in range(2):
                    n = 4 * c + 2 * a + h
                    src = view(e, 2, 512)[:, h, 0:KD * DCQ].rearrange("p (k q) -> p k q", k=KD)
                    ins = act.activation(Y[:, :, n, :], src, ACT.Copy)
                free(ins, e)

            def w_turn(e):
                full(act, e)
                src = carve_as(psum[slot_of[e]], 0, BF16, KD, FC * P)[:, :, 0:FI]
                free(act.activation(w_QT, src, ACT.Copy), e)

            def w_gather(e):
                _, a, k = e
                full(act, e)
                src = view(e, 2, 512)[:, :, 0:FH]
                free(act.activation(w_in[a][:, k, :].rearrange("p (a b) -> p a b", a=2), src, ACT.Copy), e)

            def f_xt(e):
                full(act, e)
                src = carve_as(psum[slot_of[e]], 0, BF16, KD, S)
                free(act.activation(f_XT[:, e[1] % 2], src, ACT.Copy), e)

            def f_g(e):
                n = e[1]
                taken(act, e)
                if n >= 2:
                    act.wait_ge(f_product, n - 1)
                act.activation(f_SG[:, n % 2, :], f_G[:, n % 2, :], ACT.Silu).then_inc(f_silu, 1)

            def f_scale(e):
                n = e[1]
                act.wait_ge(f_inverse, n + 1)
                act.activation(f_T[:, n % 4, :], f_T[:, n % 4, :], ACT.Copy, scale=f_s[:, 1, 2, n:n + 1])\
                    .then_inc(f_scaled, 1)

            def f_t(e):
                n = e[1]
                full(act, e)
                src = carve_as(psum[slot_of[e]], 0, BF16, FC, P)
                act.activation(f_TT[:, n % 2, 0:FC - 1, :], src[:, 0:FC - 1, :], ACT.Copy)
                free(act.activation(f_TT[0:FI - (FC - 1) * P, n % 2, FC - 1, :],
                                    src[0:FI - (FC - 1) * P, FC - 1, :], ACT.Copy), e)

            todo = {"xt": xt, "a_q": a_q, "a_v": a_v, "a_scores": a_scores, "a_turn": a_turn, "a_heads": a_heads,
                    "kv_turn": copy_to(lambda e: kvT[:, e[1], :], LC),
                    "fold_n": copy_to(lambda e: N[:, 4 * e[2]:4 * e[2] + 4], 4, 2, DC, rows=QH),
                    "fold_l": copy_to(lambda e: L[:, :, :], 4, DC),
                    "fold_z": copy_to(lambda e: Z[:, :, 4 * DC * e[1]:4 * DC * (e[1] + 1)], KD, 4 * DC),
                    "fold_u": copy_to(lambda e: U[:, 2 * e[2]:2 * e[2] + 2, :], 2, D),
                    "m_gate": m_gate, "m_flat": m_flat, "m_su": m_su, "m_a": m_a, "m_g": m_g,
                    "d_x": d_x, "d_z": d_z, "d_m1": d_m1, "fold_y": fold_y,
                    "w_turn": w_turn, "w_gather": w_gather,
                    "w_row": copy_to(lambda e: w_rows[e[1]], FI),
                    "f_xt": f_xt, "f_sel": copy_to(lambda e: f_XS[:, e[1] % 2], KD, S),
                    "f_g": f_g, "f_scale": f_scale, "f_t": f_t,
                    "r_q": copy_to(lambda e: x_Q[:, e[1] % 2, e[2], :], S),
                    "m_wdt": copy_to(lambda e: m_wdT[:, e[1] * S:(e[1] + 1) * S], S, rows=NX),
                    "m_wt": copy_to(lambda e: m_WT[:, e[1] * S:(e[1] + 1) * S], S, rows=NX),
                    "x_q": copy_to(lambda e: x_Q[:, e[1] % 2, 4 * e[2]:4 * e[2] + 4, :], 4, S),
                    "x_scores": x_scores,
                    "x_turn": copy_to(lambda e: x_PT[:, e[2] % 4], LT, S)}
            for e in steps:
                if e[0] in todo:
                    todo[e[0]](e)

        @block.vector
        def _(dve):
            chain = [0]

            def link(ins):
                chain[0] += 1
                ins.then_inc(dve_step, 1)
                dve.wait_ge(dve_step, chain[0])

            dve.wait_ge(consts_loaded, 48)
            link(dve.tensor_scalar(neg_lambda[:, :], neg_lambda[:, :], -1.0, None, ALU.mult))
            dve.wait_ge(x_loaded, 16)

            def norm(e):
                _, kind, b = e
                n = norm_no[(kind, b)]
                if kind in "GH":
                    for t in range(TB):
                        src = XN[:, TB * b + t, :]
                        ins = dve.scalar_tensor_tensor(out=d_J, in0=src, scalar=1.0, in1=src, op0=ALU.mult,
                                                       op1=ALU.mult, accum_out=mv[:, n % 2, t, 1:2])
                        if t == TB - 1:
                            ins.then_inc(norm_stats, 1)
                        else:
                            link(ins)
                    dve.wait_ge(norm_rstd, n + 1)
                    if b >= 2:
                        full(dve, ("xt", kind, b - 2))
                    elif kind == "H":
                        full(dve, ("xt", "G", b + 2))
                    for t in range(TB):
                        dve.tensor_scalar(d_N[:, TB * (b % 2) + t, :], XN[:, TB * b + t, :],
                                          rstd[:, n % 2, 1, t:t + 1], None, ALU.mult).then_inc(normed, 1)
                    return
                for t in range(TB):
                    link(dve.bn_stats(stats[:, n % 2, t, :], X[:, TB * b + t, :]))
                    dve.bn_aggr(mv[:, n % 2, t, :], stats[:, n % 2, t, :]).then_inc(norm_stats, 1) \
                        if t == TB - 1 else link(dve.bn_aggr(mv[:, n % 2, t, :], stats[:, n % 2, t, :]))
                dve.wait_ge(norm_rstd, n + 1)
                for t in range(TB):
                    dve.tensor_scalar(XN[:, TB * b + t, :], X[:, TB * b + t, :], mv[:, n % 2, t, 0:1],
                                      rstd[:, n % 2, 1, t:t + 1], ALU.subtract, ALU.mult)\
                        .then_inc(normed, 1)

            def a_k(e):
                b = e[1]
                full(dve, e)
                k = view(e, 4, S)
                for m in range(2):
                    ins = dve.tensor_scalar(a_K[:, 4 * (b % 2):4 * (b % 2) + 4, m, :], k, kmask[:, m:m + 1],
                                            None, ALU.mult)
                free(ins, e)

            def a_scores(e):
                i = e[1]
                full(dve, e)
                dve.tensor_reduce(a_nm[:, i % 4, :], view(e, 2 * TB, S), AX.X, ALU.max, negate=True)\
                    .then_inc(a_max_ready, 1)

            def a_mix(e):
                i = e[1]
                h = i % H
                taken(dve, ("a_scores", i))
                link(dve.reciprocal(a_r[:, i % 4, :], a_rs[:, i % 4, :]))
                link(dve.tensor_scalar(a_c[:, i % 4, :], a_r[:, i % 4, TB:2 * TB], neg_lambda[:, h:h + 1], None,
                                       ALU.mult))
                if i >= 3:
                    taken(dve, ("a_turn", i - 3))
                for t in range(TB):
                    link(dve.tensor_scalar(a_A[:, i % 3, t, :], a_P[:, i % 3, t, :], a_r[:, i % 4, t:t + 1],
                                           None, ALU.mult))
                for t in range(TB):
                    ins = dve.scalar_tensor_tensor(out=a_A[:, i % 3, t, :], in0=a_P[:, i % 3, TB + t, :],
                                                   scalar=a_c[:, i % 4, t:t + 1], in1=a_A[:, i % 3, t, :],
                                                   op0=ALU.mult, op1=ALU.add)
                ins.then_inc(a_mix_ready, 1)

            def residual(e):
                b = e[-1]
                full(dve, e)
                xb = X[:, TB * b:TB * b + TB, :]
                ins = dve.tensor_tensor(xb, view(e, TB, D), xb, ALU.add)
                free(ins, e)
                taken(dve, e)

            def x_scores(e):
                i = e[2]
                full(dve, e)
                dve.tensor_reduce(x_nm[:, i % 4, :], view(e, TB, LC), AX.X, ALU.max, negate=True)\
                    .then_inc(x_max_ready, 1)

            def x_norm(e):
                _, lay, i = e
                taken(dve, ("x_scores", lay, i))
                link(dve.reciprocal(x_r[:, i % 4, :], x_rs[:, i % 4, :]))
                for t in range(TB):
                    ins = dve.tensor_scalar(x_P[:, i % 3, t, :], x_P[:, i % 3, t, :], x_r[:, i % 4, t:t + 1],
                                            None, ALU.mult)
                ins.then_inc(x_norm_ready, 1)

            def x_heads(e):
                full(dve, e)
                free(dve.tensor_copy(x_C[:, e[2] % (H // 2), :], view(e, S)), e)

            def m_gate(e):
                b = e[1]
                ts = slice(TB * b, TB * b + TB)
                if b == 0:
                    dve.wait_ge(m_inv_loaded, 32)
                    dve.tensor_scalar(m_sel, m_inv[:, :], lane[0:NX, 0:1], None, ALU.is_equal)\
                        .then_inc(m_sel_ready, 1)
                full(dve, e)
                dve.tensor_reduce(m_nm[:, ts], view(e, TB, NX), AX.X, ALU.max, negate=True).then_inc(m_max_ready, 1)
                taken(dve, e)
                link(dve.reciprocal(m_r[:, ts], m_rs[:, ts]))
                link(dve.memset(m_sc[:, ts, NX:NX + 2], ABSENT))
                for n in range(TB * b, TB * b + TB):
                    link(dve.tensor_scalar(m_sc[:, n, 0:NX], m_E[:, n, :], m_r[:, n:n + 1], None, ALU.mult))
                    link(dve.max(m_t8[:, n, :], m_sc[:, n, 0:NX]))
                    link(dve.memset(m_t8[:, n, TOPK:8], ABSENT))
                    link(dve.match_replace(m_rep[:, n, :], m_t8[:, n, :], m_sc[:, n, :], 0.0))
                dve.tensor_tensor(m_wd[:, ts, :], m_sc[:, ts, 0:NX], m_rep[:, ts, 0:NX], ALU.subtract)\
                    .then_inc(m_wd_ready, 1)

            def grouped(ap, b):
                return ap[:, TB * b:TB * b + TB, :].rearrange("p t (f k) -> p (t f) k", k=MK)

            def per_group(ap, b):
                return ap[:, TB * b:TB * b + TB, :].rearrange("p t f -> p (t f)")

            def spread(ap, b):
                return per_group(ap, b).unsqueeze(2).to_broadcast([P, TB * NE, MK])

            def m_flat_(e):
                b = e[1]
                ts = slice(TB * b, TB * b + TB)
                full(dve, e)
                free(dve.tensor_copy(m_flat[:, ts, :], view(e, TB, NX)), e)
                taken(dve, e)
                link(dve.tensor_reduce(per_group(m_scal, b), grouped(m_flat, b), AX.X, ALU.add))
                link(dve.tensor_scalar(m_val[:, ts, :], m_flat[:, ts, :], 0.0, -1e9, ALU.is_equal, ALU.mult))
                link(dve.tensor_tensor(m_val[:, ts, :], m_val[:, ts, :], m_flat[:, ts, :], ALU.add))
                link(dve.tensor_reduce(per_group(m_mx, b), grouped(m_val, b), AX.X, ALU.max))
                dve.tensor_tensor(grouped(m_val, b), grouped(m_val, b), spread(m_mx, b), ALU.subtract)\
                    .then_inc(m_val_ready, 1)
                dve.wait_ge(m_ex_ready, b + 1)
                link(dve.tensor_reduce(per_group(m_sum, b), grouped(m_ex, b), AX.X, ALU.add))
                link(dve.reciprocal(per_group(m_rsum, b), per_group(m_sum, b)))
                dve.tensor_tensor(grouped(m_w, b), grouped(m_ex, b), spread(m_rsum, b), ALU.mult)\
                    .then_inc(m_w_ready, 1)

            def m_su(e):
                b = e[1]
                full(dve, e)
                taken(dve, ("m_sg", b))
                if b >= 2:
                    full(dve, ("m_sy", b - 2))
                free(dve.tensor_tensor(m_HS[:, b % 2], view(e, 3, S), m_SS[:, b % 2], ALU.mult), e)

            def m_xe(e):
                _, f, b = e
                i = NB * f + b
                full(dve, e)
                if i >= 2:
                    full(dve, ("m_g", *divmod(i - 2, NB)))
                free(dve.tensor_tensor(m_XE[:, i % 2], view(e, KD, S), XT[:, :, b * S:(b + 1) * S], ALU.add), e)

            def m_a(e):
                _, f, b = e
                i = NB * f + b
                full(dve, e)
                dve.wait_ge(m_wx_ready, i + 1)
                if i >= 2:
                    full(dve, ("m_g", *divmod(i - 2, NB)))
                free(dve.tensor_tensor(m_AW[:, i % 2, :], view(e, 2, S)[:, 0], m_WX[:, i % 2, :], ALU.mult), e)

            def m_g(e):
                _, f, b = e
                i = NB * f + b
                full(dve, e)
                if i == 0:
                    link(dve.memset(m_H[32:64, :, 1, :], 0.0))
                dve.wait_ge(m_silu_ready, i + 1)
                if i >= 2:
                    full(dve, ("m_y", *divmod(i - 2, NB)))
                o = view(e, 3, S)
                dve.tensor_tensor(m_H[:, i % 2, 0, :], o[:, 1], m_SG[:, i % 2, 0, :], ALU.mult)
                free(dve.tensor_tensor(m_H[0:ML, i % 2, 1, :], o[64:64 + ML, 2], m_SG[0:ML, i % 2, 1, :],
                                       ALU.mult), e)

            def m_a2(e):
                _, f, b = e
                i = NB * f + b
                full(dve, e)
                free(dve.tensor_tensor(m_H[64:P, i % 2, 1, :], view(e, S)[64:P], m_WX[64:P, i % 2, :], ALU.mult), e)

            def m_y(e):
                _, f, b = e
                full(dve, e)
                for t in range(TB):
                    n = TB * b + t
                    ins = dve.scalar_tensor_tensor(out=X[:, n, :], in0=view(e, TB, D)[:, t],
                                                   scalar=m_scal[:, n, f:f + 1], in1=X[:, n, :],
                                                   op0=ALU.mult, op1=ALU.add)
                free(ins, e)
                taken(dve, e)

            def d_x(e):
                b = e[1]
                if b == 0:
                    dve.memset(d_XP[:, :, :, 0:TAPS - 1].rearrange("p a b c -> p (a b) c"), 0.0).then_inc(m_pads, 1)
                taken(dve, e)
                if b >= 2:
                    full(dve, ("d_out", b - 2))
                for c in range(DI // P):
                    link(dve.tensor_scalar(d_C[:, b % 2, c, :], d_XP[:, b % 2, c, 0:S], d_conv[:, c, 0:1], None,
                                           ALU.mult))
                for j in range(1, TAPS):
                    for c in range(DI // P):
                        ins = dve.scalar_tensor_tensor(out=d_C[:, b % 2, c, :], in0=d_XP[:, b % 2, c, j:j + S],
                                                       scalar=d_conv[:, c, j:j + 1], in1=d_C[:, b % 2, c, :],
                                                       op0=ALU.mult, op1=ALU.add)
                        if j < TAPS - 1 or c < DI // P - 1:
                            link(ins)
                ins.then_inc(d_conv_ready, 1)

            def d_out(e):
                b = e[1]
                full(dve, e)
                n = XN[:, TB * b:TB * b + TB, :]
                free(dve.tensor_tensor(n, view(e, TB, D), n, ALU.add), e)
                taken(dve, e)

            def d_m2(e):
                b = e[1]
                xb = X[:, TB * b:TB * b + TB, :]
                link(dve.tensor_tensor(xb, xb, XN[:, TB * b:TB * b + TB, :], ALU.add))
                residual(e)

            def r_g(e):
                _, b, g = e
                j = H // 2 * b + g
                full(dve, e)
                if j == 0:
                    dve.wait_ge(r_tables, 32)
                if j >= 2:
                    full(dve, ("r_q", *divmod(j - 2, H // 2)))
                    dve.wait_ge(r_ready, j - 1)
                q = view(e, 2, 2, S, rows=QH)
                for a in range(2):
                    n = 2 * (j % 2) + a
                    dve.tensor_tensor(r_R[:, n], q[:, a], r_cos, ALU.mult)
                for a in range(2):
                    n = 2 * (j % 2) + a
                    for half in range(2):
                        ins = dve.tensor_tensor(r_M[:, n, half, :], q[:, a, 1 - half, :], r_sin[:, half, :], ALU.mult)
                        if a == 1 and half == 1:
                            free(ins, e)

            def over_range(s, b0, n, widest):
                link(dve.tensor_scalar(s[:, 1, b0:b0 + n], widest, 1.0 / FP8_MAX, TINY, ALU.mult, ALU.max))
                return dve.reciprocal(s[:, 2, b0:b0 + n], s[:, 1, b0:b0 + n])

            def to_fp8(v, e, q):
                link(dve.tensor_scalar(e.bitcast(I32), v.bitcast(I32), EXPONENT, None, ALU.bitwise_and))
                link(dve.tensor_scalar(e, e, FP8_NORMAL, FP8_ROUND, ALU.max, ALU.mult))
                link(dve.tensor_tensor(v, v, e, ALU.add))
                return dve.tensor_tensor(q, v, e, ALU.subtract)

            def w_count(e):
                dve.wait_ge(w_indices, 80)
                link(dve.memset(ones16[:, :], 1.0))
                link(dve.tensor_copy(ident16[:, :], ident[:, :]))
                link(dve.tensor_copy(w_uidxf[:, :], w_uidx[:, :]))
                for k in range(KD):
                    link(dve.tensor_scalar(w_sel[:, k, :], w_urow, lanes[:, k:k + 1], None, ALU.is_equal))
                    ins = dve.tensor_scalar(w_hit[:, k, :], w_iota, w_uidxf[:, k:k + 1], None, ALU.is_equal)
                    if k < KD - 1:
                        link(ins)
                ins.then_inc(w_tables, 1)
                full(dve, e)
                free(dve.tensor_scalar(w_mask, view(e, D), 0.0, None, ALU.is_gt), e)
                taken(dve, e)

            def w_dmax(e):
                dve.wait_ge(w_fetched[2], 16 * FC)
                dve.wait_ge(w_zeroed, 3)
                dve.tensor_reduce(w_tmp[:, 0, :], w_W[:, 2].rearrange("p c o -> p o c"), AX.X, ALU.max,
                                  apply_absolute_value=True).then_inc(w_dmax_ready, 1)

            def w_quant(e):
                a = e[1]
                if a == 2:
                    dve.wait_ge(w_dall_ready, 1)
                    link(dve.tensor_scalar(w_drow, w_drow, 1.0 / FP8_MAX, TINY, ALU.mult, ALU.max))
                    link(dve.reciprocal(w_tmp[:, 1, :], w_drow))
                    link(dve.tensor_tensor(w_W[:, 2], w_W[:, 2], w_tmp[:, 1:2, :].to_broadcast([P, FC, D]),
                                           ALU.mult))
                else:
                    dve.wait_ge(w_fetched[a], 16 * FC)
                    link(dve.tensor_tensor(w_W[:, a], w_W[:, a],
                                           w_mask.unsqueeze(1).to_broadcast([P, FC, D]), ALU.mult))
                    link(dve.tensor_reduce(w_max[:, 0, :], w_W[:, a], AX.X, ALU.max, apply_absolute_value=True))
                    if a == 1:
                        full(dve, ("w_row", 0))
                        full(dve, ("w_turn", 0))
                    link(over_range(w_max, 0, FC, w_max[:, 0, :]))
                    for c in range(FC):
                        link(dve.tensor_scalar(w_W[:, a, c, :], w_W[:, a, c, :], w_max[:, 2, c:c + 1], None,
                                               ALU.mult))
                to_fp8(w_W[:, a], w_tmp, w_down if a == 2 else w_Q).then_inc(w_quantised, 1)

            def f_quant(e):
                b = e[1]
                v = f_X[:, b % 2]
                link(dve.tensor_tensor(v, XN[:, TB * b:TB * b + TB, :],
                                       w_mask.unsqueeze(1).to_broadcast([P, TB, D]), ALU.mult))
                link(dve.tensor_reduce(f_s[:, 0, 0, TB * b:TB * b + TB], v, AX.X, ALU.max,
                                       apply_absolute_value=True))
                link(over_range(f_s[:, 0], TB * b, TB, f_s[:, 0, 0, TB * b:TB * b + TB]))
                for t in range(TB):
                    link(dve.tensor_scalar(v[:, t, :], v[:, t, :], f_s[:, 0, 2, TB * b + t:TB * b + t + 1], None,
                                           ALU.mult))
                if b >= 2:
                    full(dve, ("f_xt", b - 2))
                to_fp8(v, f_Xt, f_XQ[:, b % 2]).then_inc(f_xq_ready, 1)

            def halves(ap):
                return ap.rearrange("p (a b) -> p a b", a=2)

            def dequantise(e, a, n, dst):
                full(dve, e)
                free(dve.scalar_tensor_tensor(out=halves(dst), in0=view(e, 2, 512)[:, :, 0:FH],
                                              scalar=f_s[:, 0, 1, n:n + 1], in1=halves(w_rows[a]),
                                              op0=ALU.mult, op1=ALU.mult), e)

            def f_g(e):
                n = e[1]
                if n == 0:
                    for a in range(2):
                        taken(dve, ("w_row", a))
                if n >= 2:
                    dve.wait_ge(f_silu, n - 1)
                dequantise(e, 0, n, f_G[:, n % 2, :])

            def f_u(e):
                dequantise(e, 1, e[1], f_T[:, e[1] % 4, :])

            def f_scale(e):
                n = e[1]
                dve.wait_ge(f_product, n + 1)
                link(dve.tensor_reduce(f_s[:, 1, 0, n:n + 1], f_T[:, n % 4, :], AX.X, ALU.max,
                                       apply_absolute_value=True))
                over_range(f_s[:, 1], n, 1, f_s[:, 1, 0, n:n + 1]).then_inc(f_inverse, 1)

            def f_exponent(e):
                n = e[1]
                dve.wait_ge(f_scaled, n + 1)
                dve.tensor_scalar(f_E[:, n % 4, :].bitcast(I32), f_T[:, n % 4, :].bitcast(I32), EXPONENT, None,
                                  ALU.bitwise_and).then_inc(f_exponents, 1)

            def f_round(e):
                n = e[1]
                dve.wait_ge(f_summed, n + 1)
                if n >= 2:
                    full(dve, ("f_t", n - 2))
                dve.tensor_tensor(f_TQ[:, n % 2, :], f_T[:, n % 4, :], f_E[:, n % 4, :], ALU.subtract)\
                    .then_inc(f_rounded, 1)

            def f_y(e):
                n = e[1]
                full(dve, e)
                if n >= 2:
                    dve.wait_ge(x_done, n - 1)
                free(dve.scalar_tensor_tensor(out=f_Y[:, n % 2, :], in0=view(e, D), scalar=f_s[:, 1, 1, n:n + 1],
                                              in1=w_drow, op0=ALU.mult, op1=ALU.mult), e)

            todo = {"w_count": w_count, "w_dmax": w_dmax, "w_quant": w_quant, "f_quant": f_quant, "f_g": f_g,
                    "f_u": f_u, "f_scale": f_scale, "f_exponent": f_exponent, "f_round": f_round, "f_y": f_y,
                    "d_x": d_x, "d_out": d_out, "d_m2": d_m2, "r_g": r_g,
                    "m_gate": m_gate, "m_flat": m_flat_, "m_su": m_su, "m_xe": m_xe, "m_a": m_a, "m_g": m_g,
                    "m_a2": m_a2, "m_y": m_y, "m_sy": residual,
                    "norm": norm, "a_k": a_k, "a_scores": a_scores, "a_mix": a_mix, "a_out": residual,
                    "x_scores": x_scores, "x_norm": x_norm, "x_heads": x_heads, "x_out": residual}
            for e in steps:
                if e[0] in todo:
                    todo[e[0]](e)
            dve.memset(mv[:, 0, :, :], 0.0).then_inc(x_final, 1)

        @block.tensor
        def _(pe):
            def group(o, pairs):
                for n, (l, r) in enumerate(pairs):
                    ins = pe.matmul(o, l, r, start=(n == 0), stop=(n == len(pairs) - 1))
                return ins

            def xt(e):
                _, kind, b = e
                if xt_no[(kind, b)] == 0:
                    pe.wait_ge(consts_loaded, 48)
                pe.wait_ge(normed, TB * (norm_no[(kind, b)] + 1))
                o = view(e, KD, TB, P)
                for t in range(TB):
                    for k in range(KD):
                        if kind in "GH":
                            src = d_N[:, TB * (b % 2) + t, k * P:(k + 1) * P]
                        else:
                            src = XN[:, TB * b + t, k * P:(k + 1) * P]
                        ins = pe.transpose(o[:, k, t, :], src, ident[:, :])
                return ins

            def batch(b):
                return XT[:, :, b * S:(b + 1) * S]

            def a_q(e):
                b = e[1]
                if b == 0:
                    pe.wait_ge(a_weights, 64)
                taken(pe, ("xt", "A", b))
                for g in range(4):
                    ins = group(view(e, 4, S)[:, g], [(a_wq[:, k, g, :], batch(b)[:, k]) for k in range(KD)])
                return ins

            def a_k(e):
                b = e[1]
                for g in range(4):
                    ins = group(view(e, 4, S)[:, g], [(a_wk[:, k, g, :], batch(b)[:, k]) for k in range(KD)])
                return ins

            def a_v(e):
                b = e[1]
                for t in range(TB):
                    ins = group(view(e, TB, D)[:, t], [(batch(b)[:, k, t * P:(t + 1) * P], a_wv[:, k, :])
                                                       for k in range(KD)])
                return ins

            def a_scores(e):
                b, h = divmod(e[1], H)
                g, j = divmod(h, 4)
                if h == 0:
                    taken(pe, ("a_q", b))
                    taken(pe, ("a_k", b))
                rows = slice(32 * j, 32 * j + 32)
                o = view(e, 2, TB, S)
                for t in range(TB):
                    for m in range(2):
                        ins = pe.matmul(o[:, m, t, :], a_Q[rows, b % 2, g, t * P:(t + 1) * P],
                                        a_K[rows, 4 * (b % 2) + g, m, :], start=True, stop=True)
                return ins

            def a_turn(e):
                i = e[1]
                pe.wait_ge(a_mix_ready, i + 1)
                o = view(e, TB, S)
                for t in range(TB):
                    for k in range(TB):
                        ins = pe.transpose(o[:, k, t * P:(t + 1) * P], a_A[:, i % 3, t, k * P:(k + 1) * P],
                                           ident[:, :])
                return ins

            def a_heads(e):
                g = e[1]
                b = g // 4
                for j in range(4):
                    taken(pe, ("a_turn", 4 * g + j))
                taken(pe, ("a_v", b))
                for j in range(4):
                    i = 4 * g + j
                    h = i % H
                    ins = group(view(e, S, rows=32, base=32 * j),
                                [(a_V[:, b % 2, k, 32 * h:32 * h + 32], a_AT[:, i % 8, k, :])
                                 for k in range(TB)])
                return ins

            def a_out(e):
                b = e[1]
                for g in range(4):
                    taken(pe, ("a_heads", 4 * b + g))
                for t in range(TB):
                    ins = group(view(e, TB, D)[:, t],
                                [(a_OT[:, g, t * P:(t + 1) * P], a_wo[:, g, :]) for g in range(4)])
                return ins

            def kv_turn(e):
                b = e[1]
                pe.wait_ge(kv_roped, b + 1)
                for t in range(LT):
                    ins = pe.transpose(view(e, LT, P)[:, t], kvr[:, LT * b + t, :, :].rearrange("p a d -> p (a d)"),
                                       ident[:, :])
                return ins

            def fold_n(e):
                _, lay, c = e
                pe.wait_ge(chunk_loaded[lay][c], 16)
                qr = carve(staged[:, c % 2, :], CQR, 4, DCQ, rows=R)
                kr = carve(staged[:, c % 2, :], CKR, 4, DC, rows=R)
                o = view(e, 4, 2, DC, rows=QH)
                for h in range(4):
                    for a in range(2):
                        ins = pe.matmul(o[:, h, a, :], qr[:, h, a * QH:(a + 1) * QH], kr[:, h, :],
                                        start=True, stop=True)
                return ins

            def fold_l(e):
                c = e[1]
                taken(pe, ("fold_n", 0, c))
                kc = carve(staged[:, c % 2, :], CKC, 4, 2, KH, rows=QH)
                for h in range(4):
                    ins = group(view(e, 4, DC)[:, h], [(kc[:, h, a, :], N[:, 4 * c + h, a, :]) for a in range(2)])
                return ins

            def fold_z(e):
                c = e[1]
                taken(pe, ("fold_l", c))
                wq = carve(staged[:, c % 2, :], CWQ, 4, D)
                o = view(e, KD, 4, DC)
                for h in range(4):
                    for k in range(KD):
                        ins = pe.matmul(o[:, k, h, :], wq[:, h, k * P:(k + 1) * P], L[:, h, :],
                                        start=True, stop=True)
                return ins

            def fold_u(e):
                _, lay, c = e
                kvw = carve(staged[:, c % 2, :], CKV, 4, DC)
                wo = carve(staged[:, c % 2, :], CWO, 4, D)
                for h in range(4):
                    o = view(e, 2, D, rows=DC, base=DC * (h % 2))
                    ins = pe.matmul(o[:, h // 2, :], kvw[:, h, :], wo[:, h, :], start=True, stop=True)
                return ins

            def x_q(e):
                _, b, half = e
                if b == 0 and half == 0:
                    for c in range(4):
                        taken(pe, ("fold_z", c))
                taken(pe, ("xt", "B", b))
                for a in range(4):
                    g = 4 * half + a
                    ins = group(view(e, 4, S)[:, a], [(Z[:, k, g * P:(g + 1) * P], batch(b)[:, k])
                                                      for k in range(KD)])
                return ins

            def x_scores(e):
                _, lay, i = e
                b, h = divmod(i, H)
                if h == 0:
                    taken(pe, ("kv_turn", b))
                    for half in range(2 if lay == 0 else 0):
                        taken(pe, ("x_q", b, half))
                if lay == 1:
                    taken(pe, ("r_q", b, h // 2))
                rows = slice(DC * (h % 2), DC * (h % 2) + DC)
                for t in range(TB):
                    ins = pe.matmul(view(e, TB, LC)[:, t], x_Q[rows, b % 2, h // 2, t * P:(t + 1) * P],
                                    kvT[rows, b, :], start=True, stop=True)
                return ins

            def x_turn(e):
                _, lay, i = e
                pe.wait_ge(x_norm_ready, lay * NB * H + i + 1)
                o = view(e, LT, S)
                for t in range(TB):
                    for k in range(LT):
                        ins = pe.transpose(o[:, k, t * P:(t + 1) * P], x_P[:, i % 3, t, k * P:(k + 1) * P],
                                           ident[:, :])
                return ins

            def x_heads(e):
                _, lay, g = e
                b = g // (H // 2)
                for a in range(2):
                    i = 2 * g + a
                    taken(pe, ("x_turn", lay, i))
                    ins = group(view(e, S, rows=DC, base=DC * a),
                                [(kvr[:, LT * b + k, 0, :], x_PT[:, i % 4, k, :]) for k in range(LT)])
                return ins

            def x_out(e):
                _, lay, b = e
                if b == 0:
                    for c in range(4):
                        taken(pe, ("fold_u", lay, c))
                for g in range(H // 2):
                    taken(pe, ("x_heads", lay, H // 2 * b + g))
                for t in range(TB):
                    ins = group(view(e, TB, D)[:, t],
                                [(x_C[:, g, t * P:(t + 1) * P], U[:, g, :]) for g in range(H // 2)])
                return ins

            def m_gate(e):
                b = e[1]
                taken(pe, ("xt", "C", b))
                if b == 0:
                    pe.wait_ge(m_loaded, 96)
                for t in range(TB):
                    ins = group(view(e, TB, NX)[:, t], [(batch(b)[:, k, t * P:(t + 1) * P], m_gw[:, k, :])
                                                        for k in range(KD)])
                return ins

            def m_wdt(e):
                b = e[1]
                pe.wait_ge(m_wd_ready, b + 1)
                for t in range(TB):
                    ins = pe.transpose(view(e, TB, P, rows=NX)[:, t], m_wd[:, TB * b + t, :], ident[:, :])
                return ins

            def m_flat(e):
                b = e[1]
                taken(pe, ("m_wdt", b))
                pe.wait_ge(m_sel_ready, 1)
                for t in range(TB):
                    n = TB * b + t
                    ins = pe.matmul(view(e, TB, NX)[:, t], m_wdT[:, n * P:(n + 1) * P], m_sel, start=True, stop=True)
                return ins

            def m_wt(e):
                b = e[1]
                pe.wait_ge(m_w_ready, b + 1)
                for t in range(TB):
                    ins = pe.transpose(view(e, TB, P, rows=NX)[:, t], m_w[:, TB * b + t, :], ident[:, :])
                return ins

            def shared_in(w):
                def f(e):
                    b = e[1]
                    for c in range(3):
                        ins = group(view(e, 3, S)[:, c], [(w[:, k, c * P:(c + 1) * P], batch(b)[:, k])
                                                          for k in range(KD)])
                    return ins
                return f

            def m_sy(e):
                b = e[1]
                taken(pe, ("m_su", b))
                for t in range(TB):
                    ins = group(view(e, TB, D)[:, t], [(m_HS[:, b % 2, c, t * P:(t + 1) * P], m_sdw[:, c, :])
                                                       for c in range(3)])
                return ins

            def part(f, at, *dims, **kw):
                return carve(expert[:, f % 2, :], at, *dims, **kw)

            def m_xe(e):
                _, f, b = e
                if f == 0:
                    taken(pe, ("m_wt", b))
                for k in range(KD):
                    ins = pe.matmul(view(e, KD, S)[:, k], m_mu[:, f, k * P:(k + 1) * P], m_WT[:, b * S:(b + 1) * S],
                                    start=True, stop=True)
                return ins

            def m_a(e):
                _, f, b = e
                if b == 0:
                    pe.wait_ge(expert_loaded[f], 16)
                    pe.wait_ge(expert_scaled, 2 * (f + 1))
                i = NB * f + b
                o = view(e, 2, S)
                taken(pe, ("m_xe", f, b))
                pe.matmul(o[:, 1], m_pick[:, f, :], m_WT[:, b * S:(b + 1) * S], start=True, stop=True)
                return group(o[:, 0], [(part(f, EQA, KD, P)[:, k, :], m_XE[:, i % 2, k, :]) for k in range(KD)])

            def m_g(e):
                _, f, b = e
                i = NB * f + b
                for c in range(3):
                    pairs = [(part(f, EGU, KD, 3, P)[:, k, c, :], m_XE[:, i % 2, k, :]) for k in range(KD)]
                    if c == 0:
                        taken(pe, ("m_a", f, b))
                    pairs.append((part(f, EQB, 3, P)[:, c, :], m_AW[:, i % 2, :]))
                    ins = group(view(e, 3, S)[:, c], pairs)
                return ins

            def m_a2(e):
                _, f, b = e
                i = NB * f + b
                taken(pe, ("m_g", f, b))
                w = part(f, EDA, 2, 64)
                return group(view(e, S)[64:P], [(w[:, 0, :], m_H[:, i % 2, 0, :]),
                                                (w[0:ML, 1, :], m_H[0:ML, i % 2, 1, :])])

            def m_y(e):
                _, f, b = e
                i = NB * f + b
                taken(pe, ("m_a2", f, b))
                for t in range(TB):
                    ins = group(view(e, TB, D)[:, t],
                                [(m_H[:, i % 2, c, t * P:(t + 1) * P], part(f, EDW, 2, D)[:, c, :])
                                 for c in range(2)])
                return ins

            def wide_in(w, at):
                def f(e):
                    b = e[1]
                    c0 = at(e)
                    for c in range(4):
                        ins = group(view(e, 4, S)[:, c], [(w[:, k, (c0 + c) * P:(c0 + c + 1) * P], batch(b)[:, k])
                                                          for k in range(KD)])
                    return ins
                return f

            def d_x(e):
                taken(pe, ("xt", "G", e[1]))
                pe.wait_ge(d_loaded, 96)
                return wide_in(d_win, lambda e: 0)(e)

            def d_out(e):
                b = e[1]
                pe.wait_ge(d_gated, b + 1)
                for t in range(TB):
                    ins = group(view(e, TB, D)[:, t], [(d_C[:, b % 2, c, t * P:(t + 1) * P], d_wout[:, c, :])
                                                       for c in range(DI // P)])
                return ins

            def d_m1(e):
                taken(pe, ("xt", "H", e[1]))
                return wide_in(d_w1, lambda e: 4 * e[2])(e)

            def d_m2(e):
                b = e[1]
                taken(pe, ("d_m1", b, 1))
                for t in range(TB):
                    ins = group(view(e, TB, D)[:, t], [(d_M[:, b % 2, c, t * P:(t + 1) * P], d_w2[:, c, :])
                                                       for c in range(MLP // P)])
                return ins

            def fold_y(e):
                _, c, a = e
                wq = carve(staged[:, c % 2, :], CWQ, 4, D)
                kc = carve(staged[:, c % 2, :], CKC, 4, DCQ)
                for h in range(2):
                    o = view(e, 2, 512)[:, h, 0:KD * DCQ].rearrange("p (k q) -> p k q", k=KD)
                    for k in range(KD):
                        ins = pe.matmul(o[:, k, :], wq[:, 2 * a + h, k * P:(k + 1) * P], kc[:, 2 * a + h, :],
                                        start=True, stop=True)
                return ins

            def r_g(e):
                _, b, g = e
                if b == 0:
                    taken(pe, ("fold_y", g // 2, g % 2))
                taken(pe, ("xt", "E", b))
                o = view(e, 2, 2, S, rows=QH)
                for a in range(2):
                    for half in range(2):
                        ins = group(o[:, a, half, :], [(Y[:, k, 2 * g + a, half * QH:(half + 1) * QH],
                                                        batch(b)[:, k]) for k in range(KD)])
                return ins

            def r_q(e):
                _, b, g = e
                j = H // 2 * b + g
                pe.wait_ge(r_ready, j + 1)
                for a in range(2):
                    ins = group(view(e, S, rows=DC, base=DC * a),
                                [(N[:, 2 * g + a, half, :], r_R[:, 2 * (j % 2) + a, half, :]) for half in range(2)])
                return ins

            def w_count(e):
                pe.wait_ge(w_tables, 1)
                return group(view(e, D), [(ones16[:, :], w_hit[:, k, :]) for k in range(KD)])

            def w_turn(e):
                a = e[1]
                pe.wait_ge(w_quantised, a + 2)
                o = carve_as(psum[slot_of[e]], 0, BF16, KD, FC * P)
                for c in range(FC):
                    n = min(P, FI - c * P)
                    for k in range(KD):
                        ins = pe.transpose(o[:, k, c * P:c * P + n], w_Q[0:n, c, k * P:(k + 1) * P],
                                           ident16[0:n, 0:n])
                return ins

            def w_gather(e):
                _, a, k = e
                taken(pe, ("w_turn", a))
                for x in range(2):
                    ins = group(view(e, 2, 512)[:, x, 0:FH], [(w_sel[:, j, k * P:(k + 1) * P],
                                                               w_QT[:, j, x * FH:(x + 1) * FH]) for j in range(KD)])
                return ins

            def w_row(e):
                for c in range(FC):
                    n = min(P, FI - c * P)
                    ins = pe.matmul(view(e, FI)[:, c * P:c * P + n], w_max[0:n, 1, c:c + 1].to_broadcast([n, P]),
                                    ident[0:n, 0:n], start=True, stop=True)
                return ins

            def f_xt(e):
                b = e[1]
                pe.wait_ge(f_xq_ready, b + 1)
                o = carve_as(psum[slot_of[e]], 0, BF16, KD, S)
                for t in range(TB):
                    for k in range(KD):
                        ins = pe.transpose(o[:, k, t * P:(t + 1) * P], f_XQ[:, b % 2, t, k * P:(k + 1) * P],
                                           ident16[:, :])
                return ins

            def f_sel(e):
                b = e[1]
                taken(pe, ("f_xt", b))
                for k in range(KD):
                    ins = group(view(e, KD, S)[:, k], [(w_sel[:, j, k * P:(k + 1) * P], f_XT[:, b % 2, j, :])
                                                       for j in range(KD)])
                return ins

            def hidden(e):
                name, n = e
                a = 0 if name == "f_g" else 1
                b, t = divmod(n, TB)
                taken(pe, ("f_sel", b))
                taken(pe, ("w_gather", a, 1))
                for x in range(2):
                    ins = group(view(e, 2, 512)[:, x, 0:FH],
                                [(f_XS[:, b % 2, k, t * P:(t + 1) * P], w_in[a][:, k, x * FH:(x + 1) * FH])
                                 for k in range(KD)])
                return ins

            def f_t(e):
                n = e[1]
                pe.wait_ge(f_rounded, n + 1)
                o = carve_as(psum[slot_of[e]], 0, BF16, FC, P)
                for c in range(FC):
                    m = min(P, FI - c * P)
                    ins = pe.transpose(o[0:m, c, :], f_TQ[:, n % 2, c * P:c * P + m], ident16[:, :])
                return ins

            def f_y(e):
                n = e[1]
                taken(pe, ("f_t", n))
                pairs = []
                for c in range(FC):
                    m = min(P, FI - c * P)
                    pairs.append((f_TT[0:m, n % 2, c, :], w_down[0:m, c, :]))
                return group(view(e, D), pairs)

            todo = {"w_count": w_count, "w_turn": w_turn, "w_gather": w_gather, "w_row": w_row, "f_xt": f_xt,
                    "f_sel": f_sel, "f_g": hidden, "f_u": hidden, "f_t": f_t, "f_y": f_y,
                    "d_x": d_x, "d_z": wide_in(d_win, lambda e: 4), "d_out": d_out, "d_m1": d_m1, "d_m2": d_m2,
                    "fold_y": fold_y, "r_g": r_g, "r_q": r_q,
                    "m_gate": m_gate, "m_wdt": m_wdt, "m_flat": m_flat, "m_wt": m_wt, "m_sg": shared_in(m_sgw),
                    "m_su": shared_in(m_suw), "m_sy": m_sy, "m_xe": m_xe, "m_a": m_a, "m_g": m_g, "m_a2": m_a2,
                    "m_y": m_y,
                    "xt": xt, "a_q": a_q, "a_k": a_k, "a_v": a_v, "a_scores": a_scores, "a_turn": a_turn,
                    "a_heads": a_heads, "a_out": a_out, "kv_turn": kv_turn, "fold_n": fold_n, "fold_l": fold_l,
                    "fold_z": fold_z, "fold_u": fold_u, "x_q": x_q, "x_scores": x_scores, "x_turn": x_turn,
                    "x_heads": x_heads, "x_out": x_out}
            for e in steps:
                if e[0] in PE_STEPS:
                    s = slot_of[e]
                    if use_of[e] >= 1:
                        pe.wait_ge(slot_free[s], use_of[e])
                    todo[e[0]](e).then_inc(slot_full[s], 1)


def host_layout(i):
    import numpy as np
    f = lambda n: np.asarray(i[n], np.float32)
    a = {}
    a["x"] = f("x")
    a["ident"] = np.eye(P, dtype=np.float32)

    def rows(w, k):
        return w.reshape(k, P, -1).transpose(1, 0, 2)

    m = np.zeros((P, 2), np.float32)
    for r in range(P):
        m[r, (r // 16) % 2] = HD ** -0.5
    a["kmask"] = m
    for n, w1, w2 in (("a_wq", "L0_attn_q1_w", "L0_attn_q2_w"), ("a_wk", "L0_attn_k1_w", "L0_attn_k2_w")):
        w = np.stack([f(w1).T.reshape(D, H, HD), f(w2).T.reshape(D, H, HD)], axis=2)
        a[n] = rows(w.reshape(D, 2 * D), KD).reshape(P, KD, 4, P)
    a["a_wv"] = rows(f("L0_attn_v_w").T, KD)
    wo = np.zeros((4, 4, 32, D), np.float32)
    wo[:, :, :HD, :] = f("L0_attn_o_w").T.reshape(4, 4, HD, D)
    a["a_wo"] = wo.reshape(4, P, D).transpose(1, 0, 2)
    a["a_lambda"] = f("L0_attn_lambda_param")

    a["kv"] = f("ctx_512")

    def rope(length, dim):
        inv = (1.0 / 10000.0 ** (np.arange(0, dim, 2, dtype=np.float32) / np.float32(dim))).astype(np.float32)
        ang = np.arange(length, dtype=np.float32)[:, None] * inv[None, :]
        sin = np.repeat(np.sin(ang), 2, axis=-1).astype(np.float32)
        cos = np.repeat(np.cos(ang), 2, axis=-1).astype(np.float32)
        sin[:, :dim // 2] *= -1.0
        return cos, sin

    cos, sin = rope(LC, DC)
    a["k_cos"], a["k_sin"] = (w.reshape(LT, P, DC).transpose(1, 0, 2) for w in (cos, sin))
    cos, sin = rope(S, DCQ)
    a["r_cos"], a["r_sin"] = (w.T.reshape(2, QH, S).transpose(1, 0, 2) for w in (cos, sin))
    chunks = np.zeros((8, P, CHUNK), np.float32)
    for lay in range(2):
        w = {n: f(f"L{lay}_xattn_{n}") for n in ("Wq", "w_kc_q", "w_kc_kv", "W_qr", "W_kr", "Wo")}
        qr, kr = w["W_qr"].transpose(2, 0, 1), w["W_kr"].transpose(2, 0, 1)
        wq = w["Wq"].reshape(H, KH, D).transpose(1, 0, 2)
        kvw = w["w_kc_kv"].transpose(1, 0, 2)
        wo = w["Wo"].T.reshape(H, KH, D).transpose(1, 0, 2)
        if lay == 0:
            kc = w["w_kc_q"].transpose(2, 0, 1).reshape(2, QH, H, KH).transpose(1, 2, 0, 3)
        else:
            kc = w["w_kc_q"].transpose(1, 0, 2)
        for c in range(4):
            h = slice(4 * c, 4 * c + 4)
            for at, v in ((CQR, qr), (CKR, kr), (CKC, kc), (CWQ, wq), (CKV, kvw), (CWO, wo)):
                part = v[:, h].reshape(v.shape[0], -1)
                chunks[4 * lay + c, :part.shape[0], at:at + part.shape[1]] = part
    a["chunks"] = chunks

    a["d_win"] = rows(f("L1_attn_W_in").T, KD)
    a["d_wout"] = rows(f("L1_attn_W_out").T, DI // P)
    a["d_w1"] = rows(f("L1_attn_W_mlp1").T, KD)
    a["d_w2"] = rows(f("L1_attn_W_mlp2").T, MLP // P)
    a["d_conv"] = rows(f("L1_attn_conv_w").reshape(DI, TAPS), DI // P)
    a["d_bias"] = f("L1_attn_conv_b").reshape(DI // P, P).T

    a["lanes"] = np.arange(D, dtype=np.float32).reshape(KD, P).T
    a["iota"] = np.broadcast_to(np.arange(D, dtype=np.float32), (P, D))
    a["f_uidx"] = np.asarray(i["L1_ffn_up_reorder_index"], np.int32)
    a["f_ucol"] = a["f_uidx"].reshape(KD, P).T
    dcol = np.zeros(FC * P, np.int32)
    dcol[:FI] = np.asarray(i["L1_ffn_down_reorder_index"], np.int32)
    a["f_dcol"] = dcol.reshape(FC, P).T
    a["f_didx"] = np.asarray(i["L1_ffn_down_reorder_index"], np.int32).reshape(FI, 1)
    a["f_gate"], a["f_up"] = f("L1_ffn_w_gate"), f("L1_ffn_w_up")
    a["f_down"] = f("L1_ffn_w_down").T

    q = {n: f(f"L0_ffn_{n}") for n in ("gate_weight", "mask_up_W", "gate_W", "gate_qa", "gate_qb", "gate_scale",
                                       "up_W", "up_qa", "up_qb", "up_scale", "down_W", "down_qa", "down_qb",
                                       "down_scale", "sh_gate_W", "sh_up_W", "sh_down_W")}
    a["lane"] = np.arange(P, dtype=np.float32).reshape(P, 1)
    a["m_inv"] = np.asarray(i["L0_ffn_inv_mapping"], np.int32).reshape(NX)
    a["m_gw"] = rows(q["gate_weight"].T, KD)
    mu = np.zeros((NX, NE, D), np.float32)
    pick = np.zeros((NX, NE, P), np.float32)
    for e in range(NE):
        mu[MK * e:MK * (e + 1), e, :] = q["mask_up_W"][e].T
        for k in range(MK):
            for half in (0, 64):
                pick[MK * e + k, e, half + MR * k:half + MR * (k + 1)] = 1.0
    a["m_mu"], a["m_pick"] = mu, pick
    ex = np.zeros((NE, P, EXPERT), np.float32)
    for e in range(NE):
        gu = np.zeros((D, 3, P), np.float32)
        gu[:, 0, :] = q["gate_W"][e].T[:, :P]
        gu[:, 1, :] = q["up_W"][e].T[:, :P]
        gu[:, 2, :ML] = q["gate_W"][e].T[:, P:]
        gu[:, 2, 64:64 + ML] = q["up_W"][e].T[:, P:]
        ex[e, :, EGU:EQB] = rows(gu.reshape(D, 3 * P), KD).reshape(P, -1)
        gq = q["gate_qb"][e].transpose(0, 2, 1).reshape(MK * MR, MI)
        uq = q["up_qb"][e].transpose(0, 2, 1).reshape(MK * MR, MI)
        qb = np.zeros((P, 3, P), np.float32)
        qb[:64, 0, :], qb[64:, 1, :] = gq[:, :P], uq[:, :P]
        qb[:64, 2, :ML], qb[64:, 2, 64:64 + ML] = gq[:, P:], uq[:, P:]
        ex[e, :, EQB:EGS] = qb.reshape(P, -1)
        gs = np.zeros((3, P), np.float32)
        gs[0], gs[1] = q["gate_scale"][e][:P], q["up_scale"][e][:P]
        gs[2, :ML], gs[2, 64:64 + ML] = q["gate_scale"][e][P:], q["up_scale"][e][P:]
        ex[e, :, EGS:EQA] = gs.reshape(1, -1)
        qa = np.concatenate([q["gate_qa"][e].reshape(64, D).T, q["up_qa"][e].reshape(64, D).T], axis=1)
        ex[e, :, EQA:EDA] = rows(qa, KD).reshape(P, -1)
        da = q["down_qa"][e].reshape(64, MI).T
        ex[e, :, EDA:EDA + 64] = da[:P]
        ex[e, :ML, EDA + 64:EDW] = da[P:]
        dw = q["down_W"][e].T
        ex[e, :, EDW:EDW + D] = dw[:P]
        ex[e, :ML, EDW + D:EDS] = dw[P:]
        ex[e, 64:, EDW + D:EDS] = q["down_qb"][e].transpose(0, 2, 1).reshape(64, D)
        ex[e, :64, EDS:EXPERT] = 1.0
        ex[e, 64:, EDS:EXPERT] = q["down_scale"][e].reshape(1, D)
    a["m_experts"] = ex
    for n, w in (("m_sgw", "sh_gate_W"), ("m_suw", "sh_up_W")):
        wide = np.zeros((D, 3 * P), np.float32)
        wide[:, :MS] = q[w].T
        a[n] = rows(wide, KD)
    wide = np.zeros((3 * P, D), np.float32)
    wide[:MS] = q["sh_down_W"].T
    a["m_sdw"] = rows(wide, 3)
    return {k: np.ascontiguousarray(v) for k, v in a.items()}


def kernel(**inputs):
    import numpy as np
    import concourse.bacc as bacc
    from concourse.bass_utils import run_bass_kernel_spmd as run

    nc = bacc.Bacc("TRN2", target_bir_lowering=False, num_devices=1)
    arrays, aps = {}, {}
    for name, a in host_layout(inputs).items():
        arrays[f"in_{name}"] = a
        aps[name] = nc.dram_tensor(f"in_{name}", a.shape, mybir.dt.from_np(a.dtype), kind="ExternalInput").ap()
    out = nc.dram_tensor("out_x", (NB, S, D), F32, kind="ExternalOutput").ap()
    decoder(nc, aps, out)
    r = run(nc, [arrays], core_ids=[0])
    return r.results[0]["out_x"]
```

```python
from contextlib import ExitStack

import concourse.bass as bass
from concourse import mybir

P = 128
NB, S, D = 4, 256, 256
T = NB * S
TB = S // P
NT = T // P
KD = D // P
H = 16
HD = D // H
LC = 512
LT = LC // P
DC, DCQ, R, KH = 64, 192, 64, 128
QH = DCQ // 2
EPS = 1e-5
DI, TAPS, MLP = 512, 4, 1024
XPAD = S + TAPS - 1
FI = 704
FC = (FI + P - 1) // P
FH = FI // 2
FP8_MAX = 448.0
FP8_NORMAL = 2.0 ** -6
FP8_ROUND = 1.5 * 2.0 ** 20
EXPONENT = 0x7F800000
TINY = 1e-30
NX, NE, MK, MR, MI, TOPK = 64, 8, 8, 8, 176, 6
ML = MI - P
MS = 352
ABSENT = -7.0
EGU, EQB, EGS, EQA, EDA, EDW, EDS, EXPERT = 0, 768, 1152, 1536, 1792, 1920, 2432, 2688
CQR, CKR, CKC, CWQ, CKV, CWO, CHUNK = 0, 768, 1024, 2048, 3072, 3328, 4352
HEAD_PAIRS = H // 2 + 2
FOLDS_AT = (7, 9, 11, 15)
AHEAD, PAIRS = 2, 4

F32 = mybir.dt.float32
BF16 = mybir.dt.bfloat16
F32R = mybir.dt.float32r
I32 = mybir.dt.int32
ALU = mybir.AluOpType
ACT = mybir.ActivationFunctionType
AX = mybir.AxisListType
RMAX = bass.bass_isa.ReduceOp.max


def carve(region, start, *dims, rows=P, base=0):
    n = 1
    for d in dims:
        n *= d
    ap = region[base:base + rows, start:start + n]
    names = ["a", "b", "c", "d"][:len(dims)]
    if len(dims) > 1:
        ap = ap.rearrange(f"p ({' '.join(names)}) -> p {' '.join(names)}",
                          **dict(zip(names[1:], dims[1:])))
    return ap


def carve_as(region, start, dt, *dims, rows=P, base=0):
    n = 1
    for d in dims:
        n *= d
    ap = region[base:base + rows, start:start + n // 2].bitcast(dt)
    names = ["a", "b", "c", "d"][:len(dims)]
    if len(dims) > 1:
        ap = ap.rearrange(f"p ({' '.join(names)}) -> p {' '.join(names)}",
                          **dict(zip(names[1:], dims[1:])))
    return ap


def schedule():
    ev = []
    add = lambda *e: ev.append(e)
    n = NB * H

    def folds(layer, c, part):
        if part == 0:
            add("fold_n", layer, c)
        elif part == 1 and layer == 0:
            add("fold_l", c)
        elif part == 2 and layer == 0:
            add("fold_z", c)
        elif part in (1, 2):
            add("fold_y", c, part - 1)
        elif part == 3:
            add("fold_u", layer, c)

    for b in range(NB):
        add("norm", "A", b)
        add("xt", "A", b)
    add("a_q", 0)
    add("a_k", 0)
    add("a_low", 0, 0)
    add("a_low", 0, 1)
    add("a_mask", 0)
    add("a_v", 0)
    for i in range(n + 6):
        if i >= 6 and i % 2 == 0:
            add("a_heads", (i - 6) // 2)
        if 4 <= i < n + 4:
            add("a_turn", i - 4)
        if i < n:
            add("a_scores", i)
        if 2 <= i <= n + 1:
            add("a_mix", i - 2)
        if 1 <= i <= n:
            add("a_inverse", i - 1)
            add("a_scale", i - 1)
        if i % 2 == 1 and i // 4 + 1 < n // 4:
            add("a_low", i // 4 + 1, i % 4 // 2)
        if i >= 6 and (i - 6) % H == H - 2:
            add("a_out", (i - 6) // H)
            add("norm", "B", (i - 6) // H)
        if i % 2 == 0 and i // 4 + 1 < n // 4:
            add(("a_q", "a_k")[i % 4 // 2], i // 4 + 1)
        if i % 2 == 0 and i // 2 + 1 < n // 2:
            add("a_mask", i // 2 + 1)
        if i < n and i % H == 6 and i // H + 1 < NB:
            add("a_v", i // H + 1)
        if i < n and i % H in FOLDS_AT:
            folds(0, i // H, FOLDS_AT.index(i % H))

    def latent(L):
        nxt = "CF"[L]
        prepare = {1: ("w_start",), 22: ("w_count",), 24: ("w_dmax",), 25: ("w_dall",), 26: ("w_quant", 2)}
        for a in range(2):
            for k, e in enumerate((("w_quant", a), ("w_turn", a), ("w_gather", a, 0), ("w_gather", a, 1),
                                   ("w_row", a))):
                prepare[30 + 12 * a + 2 * k] = e

        def queries(i):
            b, g = divmod(i // 2, H // 2)
            if L == 1:
                if i % 2 == 0 and i >= 2:
                    rotated(i - 2)
                add("r_g", b, g, i % 2)
            elif i % 2 == 1:
                add("x_q", b, g)

        def rotated(i):
            b, g = divmod(i // 2, H // 2)
            add("r_q", b, g)
            add("x_low", 1, b, g)

        for b in range(NB):
            add("xt", "BE"[L], b)

        def low(i):
            if L == 0 and i % 2 == 1 and 2 * AHEAD < i < n:
                add("x_low", L, *divmod(i // 2, H // 2))

        add("kv_turn", L, 0)
        for i in range(2 * AHEAD):
            queries(i)
            if L == 0 and i % 2 == 1:
                add("x_low", L, *divmod(i // 2, H // 2))
        for i in range(n + 6):
            if 5 <= i < n + 5:
                add("x_heads", L, i - 5)
            if 3 <= i < n + 3:
                add("x_turn", L, i - 3, 0)
                add("x_turn", L, i - 3, 1)
            if i < n:
                add("x_scores", L, i)
            if 1 <= i <= n:
                add("x_norm", L, i - 1)
            low(i - 1 + 2 * AHEAD)
            if i >= 5 and (i - 5) % H == H - 1:
                add("x_out", L, (i - 5) // H, 0)
            if i >= 6 and (i - 6) % H == H - 1:
                add("x_out", L, (i - 6) // H, 1)
                add("norm", nxt, (i - 6) // H)
            if i + 2 * AHEAD < n:
                queries(i + 2 * AHEAD)
            elif i + 2 * AHEAD == n and L == 1:
                rotated(n - 2)
            if i < n and i % H == H // 2 and i // H + 1 < NB:
                add("kv_turn", L, i // H + 1)
            if L == 1 and i in prepare:
                add(*prepare[i])

    latent(0)

    for b in range(NB):
        add("xt", "C", b)
    for part in ("m_gate", "m_wdt", "m_flat", "m_wt"):
        for b in range(NB):
            add(part, b)
    for b in range(NB + 1):
        if b < NB:
            add("m_sg", b)
            add("m_su", b)
        if b >= 1:
            add("m_sy", b - 1)
    m = [(f, b) for f in range(NE) for b in range(NB)]
    for i in range(len(m) + 3):
        if i < len(m):
            add("m_xe", *m[i])
        if 1 <= i <= len(m):
            add("m_a", *m[i - 1])
            add("m_g", *m[i - 1])
        if 2 <= i <= len(m) + 1:
            add("m_a2", *m[i - 2])
        if i >= 3:
            f, b = m[i - 3]
            add("m_y", f, b)
            if f == NE - 1:
                add("norm", "D", b)

    for b in range(NB):
        add("norm", "G", b)
    for t in range(NB + 3):
        if t < NB:
            add("xt", "G", t)
            add("d_x", t)
            add("d_z", t)
        if 1 <= t < NB + 1:
            folds(1, t - 1, 0)
        if 1 <= t <= NB:
            add("d_out", t - 1)
            add("norm", "H", t - 1)
        if 1 <= t < NB + 1:
            folds(1, t - 1, 1)
        if 1 <= t < NB + 1:
            folds(1, t - 1, 2)
        if 2 <= t < NB + 2:
            add("xt", "H", t - 2)
            add("d_m1", t - 2, 0)
            add("d_m1", t - 2, 1)
            add("d_m2", t - 2)
            add("norm", "E", t - 2)
        if 1 <= t < NB + 1:
            folds(1, t - 1, 3)
    latent(1)

    def tokens(b):
        add("f_quant", b)
        add("f_xt", b)
        add("f_sel", b)

    tokens(0)
    tokens(1)
    for t in range(NT + 5):
        if t < NT:
            add("f_g", t)
            add("f_u", t)
            if t % TB == 1 and t // TB + 2 < NB:
                tokens(t // TB + 2)
        if 1 <= t <= NT:
            add("f_scale", t - 1)
            add("f_exponent", t - 1)
        if 2 <= t <= NT + 1:
            add("f_round", t - 2)
        if t >= 4 and t - 4 < NT:
            add("f_y", t - 4)
        if 3 <= t <= NT + 2:
            add("f_t", t - 3)
    return ev


PE_STEPS = {"xt", "a_q", "a_k", "a_v", "a_scores", "a_turn", "a_heads", "a_out",
            "kv_turn", "fold_n", "fold_l", "fold_z", "fold_y", "fold_u",
            "m_gate", "m_wdt", "m_flat", "m_wt", "m_sg", "m_su", "m_sy", "m_xe", "m_a", "m_g", "m_a2", "m_y",
            "d_x", "d_z", "d_out", "d_m1", "d_m2",
            "w_count", "w_turn", "w_gather", "w_row", "f_xt", "f_sel", "f_g", "f_u", "f_t", "f_y",
            "x_q", "x_scores", "x_turn", "x_heads", "x_out", "r_g", "r_q"}


WIDE, TURN, HEADS, QUERIES, ANY = (0, 2), (2, 2), (4, 1), (5, 1), (6, 4)
RINGS = {n: ring for ring, names in (
    (WIDE, ("a_scores", "x_scores", "fold_y", "w_turn", "w_gather", "w_row")),
    (HEADS, ("a_heads", "x_heads")),
    (QUERIES, ("a_q", "a_k", "x_q", "r_g"))) for n in names}
SLOTS = 10


def area(s):
    if s < 2:
        return s, 0
    if s < 6:
        return s // 2 + 1, 512 * (s % 2)
    return s - 6, 0


def decoder(nc, d, out):
    steps = schedule()
    slot_of, use_of = {}, {}
    used = {ring: 0 for ring in (WIDE, TURN, HEADS, QUERIES, ANY)}
    switch = {}
    last, attention = [{}, {}], True
    for e in steps:
        if e[0] in PE_STEPS:
            if e[:2] in (("xt", "C"), ("xt", "E")) and e[2] == 0:
                attention = e[1] == "E"
                switch[e] = list(last[attention].values())
            if e[0] == "f_xt" and e[1] == 0:
                attention = False
                switch[e] = list(last[attention].values())
            ring = RINGS.get(e[0], TURN) if attention else ANY
            first, size = ring
            slot_of[e], use_of[e] = first + used[ring] % size, used[ring] // size
            used[ring] += 1
            last[not attention][slot_of[e]] = e
    norm_no = {e[1:]: n for n, e in enumerate(e for e in steps if e[0] == "norm")}
    xt_no = {e[1:]: n for n, e in enumerate(e for e in steps if e[0] == "xt")}

    with ExitStack() as ctx:
        def sb(name, shape, dt=F32):
            return ctx.enter_context(nc.sbuf_tensor(name, shape, dt))

        def sem(name):
            return ctx.enter_context(nc.semaphore(name))

        X = sb("X", [P, NT, D])
        XN = sb("XN", [P, NT, D])
        XT = sb("XT", [P, KD, T])
        ident = sb("ident", [P, P])
        work = sb("work", [P, 20 * 1024])
        stats = sb("stats", [P, 2, TB, 6])
        mv = sb("mv", [P, 2, TB, 2])
        rstd = sb("rstd", [P, 2, 2, TB])
        neg_half = sb("neg_half", [P, TB])
        psum = [ctx.enter_context(nc.psum_tensor(f"banks{2 * s}_{2 * s + 1}", [P, 1024], F32)) for s in range(4)]

        def view(e, *dims, rows=P, base=0):
            tensor, start = area(slot_of[e])
            return carve(psum[tensor], start, *dims, rows=rows, base=base)

        def halfwords(e, *dims):
            tensor, start = area(slot_of[e])
            return carve_as(psum[tensor], start, BF16, *dims)

        o = 0
        a_wq = carve(work, o, KD, 4, P); o += 1024
        a_wk = carve(work, o, KD, 4, P); o += 1024
        a_wv = carve(work, o, KD, D); o += 512
        a_wo = carve(work, o, 4, D); o += 1024
        a_V = carve(work, o, 2, TB, H * 32); o += 2048
        a_P = carve(work, o, 3, 2 * TB, S); o += 3072
        a_A = carve(work, o, 4, TB, S); o += 2048
        a_AT = carve(work, o, 8, TB, S); o += 4096
        a_OT = carve(work, o, 4, S); o += 1024
        kvr = sb("kvr", [P, NB * LT, DC])
        split = sb("split", [P, 5 * 1024], F32R)
        kv_split = carve(split, 0, 2, 2, LC)
        q_split = carve(split, 2048, PAIRS, 2, S)
        a_KS = carve(split, 0, 2, 2, 2, S)
        a_QM = carve(split, 2048, 2, 4, S)
        a_QS = carve(split, 4096, 2, 2, S)
        staged = sb("staged", [P, 2, CHUNK])
        fold = sb("fold", [P, 10 * 1024])
        Z = carve(fold, 0, KD, H * DC)
        Y = carve(fold, 0, KD, H, DCQ)
        N = carve(fold, KD * H * DCQ, H, 2, DC, rows=QH)
        U = carve(fold, KD * H * DCQ + H * 2 * DC, H // 2, D)
        x_P = carve(work, 0, 3, TB, LC)
        x_PT = carve(work, 3072, 4, LT, S)
        x_C = carve(work, 7168, HEAD_PAIRS, S)
        r_R = carve(work, 9728, 2 * 2, 2, S, rows=QH)
        r_cos = carve(work, 11776, 2, S, rows=QH)
        r_sin = carve(work, 12288, 2, S, rows=QH)
        r_M = carve(work, 12800, 2 * 2, 2, S, rows=QH)
        kv = carve(fold, 2048, NB * LT, DC)
        kv_m = carve(fold, 3072, NB * LT, DC)
        k_cos = carve(fold, 4096, LT, DC)
        k_sin = carve(fold, 4352, LT, DC)
        L = carve(fold, 5632, 4, DC)
        expert = staged[:, :, :].rearrange("p a b -> p (a b)")[:, 0:2 * EXPERT].rearrange("p (a b) -> p a b", a=2)
        m_mu = carve(fold, KD * H * DCQ, NE, D, rows=NX)
        m_sgw = carve(fold, 2048, KD, 3 * P)
        m_suw = carve(fold, 2816, KD, 3 * P)
        m_sdw = carve(fold, 3584, 3, D)
        m_pick = carve(fold, 4352, NE, P, rows=NX)
        m_gw = carve(fold, 5376, KD, NX)
        m_sel = carve(fold, 5504, NX, rows=NX)
        m_inv = sb("m_inv", [NX, NX], I32)
        lane = sb("lane", [P, 1])
        w_W = carve(staged[:, :, :].rearrange("p a b -> p (a b)"), 0, 3, FC, D)
        flat_staged = staged[:, :, :].rearrange("p a b -> p (a b)")
        w_tmp = carve(flat_staged, 4608, FC, D)
        w_Q = carve_as(flat_staged, 6144, BF16, FC, D)
        w_QT = carve_as(flat_staged, 6912, BF16, KD, FI)
        w_sel = carve_as(flat_staged, 7616, BF16, KD, D)
        w_hit = carve_as(flat_staged, 7872, BF16, KD, D)
        w_urow = carve(flat_staged, 8128, D).bitcast(I32)
        w_iota = carve(flat_staged, 8384, D)
        w_in = [carve_as(work, 17408 + 704 * a, BF16, KD, FI) for a in range(2)]
        w_rows = [carve(work, 18816 + 704 * a, FI) for a in range(2)]
        w_drow = carve(work, 20224, D)
        w_down = carve_as(work, 14848, BF16, FC, D)
        w_mask = carve(work, 15616, D)
        w_didx = sb("w_didx", [P, FC], I32)
        w_ddidx = sb("w_ddidx", [P, FC], I32)
        w_uidx = sb("w_uidx", [P, KD], I32)
        w_uidxf = sb("w_uidxf", [P, KD])
        w_max = sb("w_max", [P, 3, FC])
        lanes = sb("lanes", [P, KD])
        ones16 = sb("ones16", [P, P], BF16)
        ident16 = sb("ident16", [P, P], BF16)
        o = 0
        f_X = carve(work, o, 2, TB, D); o += 1024
        f_Xt = carve(work, o, TB, D); o += 512
        f_XQ = carve_as(work, o, BF16, 2, TB, D); o += 512
        f_XT = carve_as(work, o, BF16, 2, KD, S); o += 512
        f_XS = carve_as(work, o, BF16, 2, KD, S); o += 512
        f_G = carve(work, o, 2, FI); o += 2 * FI
        f_SG = carve(work, o, 2, FI); o += 2 * FI
        f_T = carve(work, o, 4, FI); o += 4 * FI
        f_E = carve(work, o, 4, FI); o += 4 * FI
        f_TQ = carve_as(work, o, BF16, 2, FI); o += FI
        f_TT = carve_as(work, o, BF16, 2, FC, P); o += FC * P
        f_Y = carve(work, o, 2, D); o += 512
        f_s = sb("f_s", [P, 2, 3, NT])
        d_win = carve(work, 13312, KD, 2 * DI)
        d_wout = carve(work, 15360, DI // P, D)
        d_w1 = carve(work, 16384, KD, MLP)
        d_w2 = carve(work, 18432, MLP // P, D)
        d_conv = sb("d_conv", [P, DI // P, TAPS])
        d_bias = sb("d_bias", [P, DI // P])
        o = 0
        d_N = carve(work, o, 2 * TB, D); o += 1024
        d_J = carve(work, o, D); o += 256
        d_XP = carve(work, o, 2, DI // P, XPAD); o += 2 * DI // P * XPAD
        d_C = carve(work, o, 2, DI // P, S); o += 2048
        d_Z = carve(work, o, 2, DI // P, S); o += 2048
        d_M = carve(work, o, 2, MLP // P, S); o += 4096
        o = 0
        m_E = carve(work, o, NT, NX); o += 512
        m_sc = carve(work, o, NT, NX + 2); o += 528
        m_rep = carve(work, o, NT, NX + 2); o += 528
        m_wd = carve(work, o, NT, NX); o += 512
        m_wdT = carve(work, o, T, rows=NX); o += 1024
        m_flat = carve(work, o, NT, NX); o += 512
        m_val = carve(work, o, NT, NX); o += 512
        m_ex = carve(work, o, NT, NX); o += 512
        m_w = carve(work, o, NT, NX); o += 512
        m_WT = carve(work, o, T, rows=NX); o += 1024
        m_t8 = carve(work, o, NT, 8); o += 64
        m_scal = carve(work, o, NT, NE); o += 64
        m_mx = carve(work, o, NT, NE); o += 64
        m_sum = carve(work, o, NT, NE); o += 64
        m_rsum = carve(work, o, NT, NE); o += 64
        m_nm = carve(work, o, NT); o += 8
        m_rs = carve(work, o, NT); o += 8
        m_r = carve(work, o, NT); o += 8
        m_XE = carve(work, o, 2, KD, S); o += 1024
        m_WX = carve(work, o, 2, S); o += 512
        m_AW = carve(work, o, 2, S); o += 512
        m_SG = carve(work, o, 2, 2, S); o += 1024
        m_H = carve(work, o, 2, 2, S); o += 1024
        m_SS = carve(work, o, 2, 3, S); o += 1536
        m_HS = carve(work, o, 2, 3, S); o += 1536
        x_nm = sb("x_nm", [P, 4, TB])
        x_rs = sb("x_rs", [P, 4, TB])
        x_r = sb("x_r", [P, 4, TB])
        qmask = sb("qmask", [P, 4])
        neg_lambda = sb("neg_lambda", [P, H])
        a_nm = sb("a_nm", [P, 4, 2 * TB])
        a_rs = sb("a_rs", [P, 4, 2 * TB])
        a_r = sb("a_r", [P, 4, 2 * TB])
        a_c = sb("a_c", [P, 4, TB])

        slot_full = [sem(f"slot_full{s}") for s in range(SLOTS)]
        slot_free = [sem(f"slot_free{s}") for s in range(SLOTS)]
        dve_step = sem("dve_step")
        pool_step = sem("pool_step")
        x_loaded = [sem(f"x_loaded{b}") for b in range(NB)]
        aq_weights = sem("aq_weights")
        consts_loaded = sem("consts_loaded")
        a_weights = sem("a_weights")
        half_set = sem("half_set")
        norm_stats = sem("norm_stats")
        norm_rstd = sem("norm_rstd")
        normed = sem("normed")
        a_v_zeroed = sem("a_v_zeroed")
        a_max_ready = sem("a_max_ready")
        a_q_high_ready = sem("a_q_high_ready")
        a_k_high_ready = sem("a_k_high_ready")
        a_masked = sem("a_masked")
        a_scaled = sem("a_scaled")
        a_inverted = sem("a_inverted")
        kv_loaded = sem("kv_loaded")
        kv_roped = sem("kv_roped")
        chunk_loaded = [[sem(f"chunk_loaded_{a}{c}") for c in range(4)] for a in range(2)]
        x_max_ready = sem("x_max_ready")
        kv_high_ready = sem("kv_high_ready")
        q_high_ready = sem("q_high_ready")
        d_loaded = sem("d_loaded")
        d_conv_ready = sem("d_conv_ready")
        d_silu_ready = sem("d_silu_ready")
        d_gated = sem("d_gated")
        d_added = sem("d_added")
        r_tables = sem("r_tables")
        w_indices = sem("w_indices")
        w_chained = sem("w_chained")
        w_fetched = [sem(f"w_fetched{a}") for a in range(3)]
        w_zeroed = sem("w_zeroed")
        w_tables = sem("w_tables")
        w_dmax_ready = sem("w_dmax_ready")
        w_dall_ready = sem("w_dall_ready")
        w_quantised = sem("w_quantised")
        f_xq_ready = sem("f_xq_ready")
        f_silu = sem("f_silu")
        f_product = sem("f_product")
        f_inverse = sem("f_inverse")
        f_scaled = sem("f_scaled")
        f_exponents = sem("f_exponents")
        f_summed = sem("f_summed")
        f_rounded = sem("f_rounded")
        x_done = sem("x_done")
        r_ready = sem("r_ready")
        m_loaded = sem("m_loaded")
        m_inv_loaded = sem("m_inv_loaded")
        expert_loaded = [sem(f"expert_loaded{f}") for f in range(NE)]
        expert_scaled = sem("expert_scaled")
        m_sel_ready = sem("m_sel_ready")
        m_max_ready = sem("m_max_ready")
        m_wd_ready = sem("m_wd_ready")
        m_val_ready = sem("m_val_ready")
        m_ex_ready = sem("m_ex_ready")
        m_w_ready = sem("m_w_ready")
        m_wx_ready = sem("m_wx_ready")
        m_silu_ready = sem("m_silu_ready")
        m_shared_silu = sem("m_shared_silu")
        m_pads = sem("m_pads")
        x_norm_ready = sem("x_norm_ready")
        a_mix_ready = sem("a_mix_ready")
        out_stored = sem("out_stored")

        def full(eng, e):
            eng.wait_ge(slot_full[slot_of[e]], use_of[e] + 1)

        def free(ins, e):
            ins.then_inc(slot_free[slot_of[e]], 1)

        def taken(eng, e):
            eng.wait_ge(slot_free[slot_of[e]], use_of[e] + 1)

        def pair_rows(p):
            return (slice(64 * c, 64 * c + 64) for c in (p, 1 - p))

        def kv_halves(b, part, half):
            return kv_split[DC * half:DC * half + DC, b % 2, part, :].rearrange("p (c t k) -> p c t k", t=2, k=P)

        def kv_slot(e, half):
            return view(e, LT // 2, P)[DC * half:DC * half + DC]

        block = ctx.enter_context(nc.Block())

        @block.sync
        def _(sp):
            sp.dma_start(X[:, 0:TB, :], d["x"][0].rearrange("(t p) d -> p t d", p=P)).then_inc(x_loaded[0], 16)
            sp.dma_start(ident[:, :], d["ident"]).then_inc(consts_loaded, 16)
            sp.dma_start(a_wq, d["a_wq"]).then_inc(aq_weights, 16)
            sp.dma_start(qmask[:, :], d["qmask"]).then_inc(consts_loaded, 16)
            sp.dma_start(neg_lambda[:, :], d["a_lambda"].partition_broadcast(P)).then_inc(consts_loaded, 16)
            sp.dma_start(a_wk, d["a_wk"]).then_inc(a_weights, 16)
            sp.dma_start(a_wv, d["a_wv"]).then_inc(a_weights, 16)
            sp.dma_start(a_wo, d["a_wo"]).then_inc(a_weights, 16)
            sp.dma_start(kv, d["kv"].rearrange("b (t p) d -> p (b t) d", p=P)).then_inc(kv_loaded, 16)
            sp.dma_start(k_cos, d["k_cos"]).then_inc(kv_loaded, 16)
            sp.dma_start(k_sin, d["k_sin"]).then_inc(kv_loaded, 16)
            for c in range(4):
                if c >= 2:
                    full(sp, ("fold_u", 0, c - 2))
                sp.dma_start(staged[:, c % 2, :], d["chunks"][c]).then_inc(chunk_loaded[0][c], 16)
            sp.dma_start(m_inv[:, :], d["m_inv"].partition_broadcast(NX)).then_inc(m_inv_loaded, 16)
            sp.dma_start(lane[:, :], d["lane"]).then_inc(m_inv_loaded, 16)
            sp.wait_ge(kv_roped, NB)
            sp.dma_start(m_sgw, d["m_sgw"]).then_inc(m_loaded, 16)
            sp.dma_start(m_suw, d["m_suw"]).then_inc(m_loaded, 16)
            sp.dma_start(m_sdw, d["m_sdw"]).then_inc(m_loaded, 16)
            sp.dma_start(m_pick, d["m_pick"]).then_inc(m_loaded, 16)
            sp.dma_start(m_gw, d["m_gw"]).then_inc(m_loaded, 16)
            full(sp, ("fold_l", 3))
            sp.dma_start(m_mu, d["m_mu"]).then_inc(m_loaded, 16)
            for f in range(NE):
                if f < 2:
                    full(sp, ("fold_u", 0, 2 + f))
                else:
                    full(sp, ("m_y", f - 2, NB - 1))
                    sp.wait_ge(expert_scaled, 2 * (f - 1))
                if f == 0:
                    full(sp, ("fold_u", 0, 3))
                sp.dma_start(expert[:, f % 2, :], d["m_experts"][f]).then_inc(expert_loaded[f], 16)
            sp.dma_start(d_win, d["d_win"]).then_inc(d_loaded, 16)
            sp.dma_start(d_wout, d["d_wout"]).then_inc(d_loaded, 16)
            sp.dma_start(d_w1, d["d_w1"]).then_inc(d_loaded, 16)
            sp.dma_start(d_w2, d["d_w2"]).then_inc(d_loaded, 16)
            sp.dma_start(d_conv[:, :, :], d["d_conv"]).then_inc(d_loaded, 16)
            sp.dma_start(d_bias[:, :], d["d_bias"]).then_inc(d_loaded, 16)
            full(sp, ("m_y", NE - 1, NB - 1))
            for c in range(4):
                if c >= 2:
                    full(sp, ("fold_u", 1, c - 2))
                sp.dma_start(staged[:, c % 2, :], d["chunks"][4 + c]).then_inc(chunk_loaded[1][c], 16)
                if c == 1:
                    sp.dma_start(r_cos, d["r_cos"]).then_inc(r_tables, 16)
                    sp.dma_start(r_sin, d["r_sin"]).then_inc(r_tables, 16)
            sp.dma_start(lanes[:, :], d["lanes"]).then_inc(w_indices, 16)
            sp.dma_start(w_uidx[:, :], d["f_ucol"]).then_inc(w_indices, 16)
            sp.dma_start(w_didx[:, :], d["f_dcol"]).then_inc(w_indices, 16)
            full(sp, ("fold_u", 1, 3))
            sp.dma_start(w_urow, d["f_uidx"].partition_broadcast(P)).then_inc(w_indices, 16)
            sp.dma_start(w_iota, d["iota"]).then_inc(w_indices, 16)
            for b in range(NB):
                sp.wait_ge(x_done, TB * (b + 1))
                sp.dma_start(out[b].rearrange("(t p) d -> p t d", p=P), X[:, TB * b:TB * b + TB, :])\
                    .then_inc(out_stored, 16)
            sp.wait_ge(out_stored, 16 * NB)

        @block.gpsimd
        def _(pool):
            pool.memset(neg_half[:, :], -0.5).then_inc(half_set, 1)
            pool.memset(a_V, 0.0).then_inc(a_v_zeroed, 1)
            pool.wait_ge(half_set, 1)
            steps_done = [0]

            def norm(e):
                _, kind, b = e
                n = norm_no[(kind, b)]
                pool.wait_ge(norm_stats, n + 1)
                if kind in "GH":
                    ins = pool.tensor_scalar(rstd[:, n % 2, 0, :], mv[:, n % 2, :, 1], 1e-24, 1.0 / D,
                                             ALU.max, ALU.mult)
                else:
                    ins = pool.tensor_scalar(rstd[:, n % 2, 0, :], mv[:, n % 2, :, 1], EPS, None, ALU.add)
                ins.then_inc(pool_step, 1)
                steps_done[0] += 1
                pool.wait_ge(pool_step, steps_done[0])
                pool.tensor_tensor(rstd[:, n % 2, 1, :], rstd[:, n % 2, 0, :], neg_half[:, :], ALU.pow)\
                    .then_inc(norm_rstd, 1)

            def rope_kv(b):
                t = slice(LT * b, LT * b + LT)
                h = DC // 2
                ro = kvr[:, t, :]
                pool.tensor_tensor(ro, kv[:, t, :], k_cos, ALU.mult).then_inc(pool_step, 1)
                pool.tensor_tensor(kv_m[:, t, 0:h], kv[:, t, h:DC], k_sin[:, :, 0:h], ALU.mult).then_inc(pool_step, 1)
                pool.tensor_tensor(kv_m[:, t, h:DC], kv[:, t, 0:h], k_sin[:, :, h:DC], ALU.mult)\
                    .then_inc(pool_step, 1)
                steps_done[0] += 3
                pool.wait_ge(pool_step, steps_done[0])
                pool.tensor_tensor(ro, ro, kv_m[:, t, :], ALU.add).then_inc(kv_roped, 1)

            norm(steps[0])
            pool.wait_ge(kv_loaded, 48)
            for b in range(NB):
                rope_kv(b)
            def scale_expert(f):
                w = expert[:, f % 2, :]
                pool.wait_ge(expert_loaded[f], 16)
                pool.tensor_tensor(w[:, EQB:EQB + 3 * P], w[:, EQB:EQB + 3 * P], w[:, EGS:EGS + 3 * P], ALU.mult)\
                    .then_inc(expert_scaled, 1)
                pool.tensor_tensor(w[:, EDW + D:EDW + 2 * D], w[:, EDW + D:EDW + 2 * D],
                                   w[:, EDS:EDS + D], ALU.mult).then_inc(expert_scaled, 1)

            def w_start(e):
                full(pool, ("fold_u", 1, 3))
                for a in range(3):
                    pool.memset(w_W[:, a, FC - 1, :], 0.0).then_inc(w_zeroed, 1)
                pool.wait_ge(w_indices, 80)
                sizes = [P] * (FC - 1) + [FI - (FC - 1) * P]
                for c, n in enumerate(sizes):
                    pool.indirect_dma_start(w_ddidx[0:n, c:c + 1], None, d["f_didx"],
                                            bass.IndirectOffsetOnAxis(ap=w_didx[0:n, c:c + 1], axis=0))\
                        .then_inc(w_chained, 16)
                pool.wait_ge(w_zeroed, 3)
                for c, n in enumerate(sizes):
                    pool.indirect_dma_start(w_W[0:n, 2, c, :], None, d["f_down"],
                                            bass.IndirectOffsetOnAxis(ap=w_didx[0:n, c:c + 1], axis=0))\
                        .then_inc(w_fetched[2], 16)
                pool.wait_ge(w_chained, 16 * FC)
                for a, name in enumerate(("f_gate", "f_up")):
                    for c, n in enumerate(sizes):
                        pool.indirect_dma_start(w_W[0:n, a, c, :], None, d[name],
                                                bass.IndirectOffsetOnAxis(ap=w_ddidx[0:n, c:c + 1], axis=0))\
                            .then_inc(w_fetched[a], 16)

            def w_dall(e):
                pool.wait_ge(w_dmax_ready, 1)
                pool.partition_all_reduce(w_drow, w_tmp[:, 0, :], P, RMAX).then_inc(w_dall_ready, 1)

            def f_u(e):
                n = e[1]
                taken(pool, e)
                pool.wait_ge(f_silu, n + 1)
                pool.tensor_tensor(f_T[:, n % 4, :], f_T[:, n % 4, :], f_SG[:, n % 2, :], ALU.mult)\
                    .then_inc(f_product, 1)

            def f_exponent(e):
                n = e[1]
                pool.wait_ge(f_exponents, n + 1)
                pool.tensor_scalar(f_E[:, n % 4, :], f_E[:, n % 4, :], FP8_NORMAL, FP8_ROUND, ALU.max, ALU.mult)\
                    .then_inc(pool_step, 1)
                steps_done[0] += 1
                pool.wait_ge(pool_step, steps_done[0])
                pool.tensor_tensor(f_T[:, n % 4, :], f_T[:, n % 4, :], f_E[:, n % 4, :], ALU.add)\
                    .then_inc(f_summed, 1)

            def f_y(e):
                n = e[1]
                taken(pool, e)
                pool.tensor_tensor(X[:, n, :], X[:, n, :], f_Y[:, n % 2, :], ALU.add).then_inc(x_done, 1)

            def a_mask(e):
                j = e[1]
                taken(pool, ("a_q", j // 2))
                if j == 0:
                    pool.wait_ge(consts_loaded, 48)
                if j >= 2:
                    full(pool, ("a_scores", 2 * (j - 2) + 1))
                q = a_QS[:, j // 2 % 2, j % 2, :].bitcast(F32)
                pool.tensor_tensor(a_QM[:, j % 2], q.unsqueeze(1).to_broadcast([P, 4, S]),
                                   qmask[:, :].unsqueeze(2).to_broadcast([P, 4, S]), ALU.mult).then_inc(a_masked, 1)

            def a_scale(e):
                i = e[1]
                pool.wait_ge(a_inverted, i + 1)
                if i >= 4:
                    full(pool, ("a_turn", i - 4))
                pool.tensor_tensor(a_A[:, i % 4], a_P[:, i % 3, 0:TB],
                                   a_r[:, i % 4, 0:TB].unsqueeze(2).to_broadcast([P, TB, S]), ALU.mult)\
                    .then_inc(a_scaled, 1)

            tail = {"a_mask": a_mask, "a_scale": a_scale, "w_start": w_start, "w_dall": w_dall, "f_u": f_u, "f_exponent": f_exponent, "f_y": f_y}
            for e in steps[1:]:
                if e[0] == "norm":
                    norm(e)
                if e[0] in tail:
                    tail[e[0]](e)
                if e[0] == "d_z":
                    b = e[1]
                    pool.wait_ge(d_silu_ready, b + 1)
                    pool.tensor_tensor(d_C[:, b % 2], d_C[:, b % 2], d_Z[:, b % 2], ALU.mult).then_inc(d_gated, 1)
                if e[0] == "r_g":
                    r = 2 * (e[2] % 2) + e[3]
                    taken(pool, e)
                    pool.tensor_tensor(r_R[:, r], r_R[:, r], r_M[:, r], ALU.add).then_inc(r_ready, 1)
                if e[0] == "m_gate" and e[1] == 0:
                    scale_expert(0)
                    scale_expert(1)
                if e[0] == "m_y" and e[2] == NB - 1 and e[1] + 2 < NE:
                    scale_expert(e[1] + 2)

        @block.scalar
        def _(act):
            for b in range(1, NB):
                act.dma_start(X[:, TB * b:TB * b + TB, :], d["x"][b].rearrange("(t p) d -> p t d", p=P))\
                    .then_inc(x_loaded[b], 16)

            def xt(e):
                b = e[2]
                full(act, e)
                free(act.activation(XT[:, :, b * S:(b + 1) * S], view(e, KD, S), ACT.Copy), e)

            def a_q(e):
                full(act, e)
                for p in range(2):
                    rows, _ = pair_rows(p)
                    ins = act.activation(a_QS[rows, e[1] % 2, p, :], view(e, S)[rows], ACT.Copy)
                ins.then_inc(a_q_high_ready, 1)

            def a_k(e):
                full(act, e)
                for p in range(2):
                    rows, other = pair_rows(p)
                    for dst in (rows, other):
                        ins = act.activation(a_KS[dst, e[1] % 2, p, 0, :], view(e, S)[rows], ACT.Copy)
                ins.then_inc(a_k_high_ready, 1)

            def a_v(e):
                b = e[1]
                full(act, e)
                act.wait_ge(a_v_zeroed, 1)
                for t in range(TB):
                    dst = a_V[:, b % 2, t, :].rearrange("p (h c) -> p h c", c=32)[:, :, 0:HD]
                    src = view(e, TB, H, HD)[:, t]
                    ins = act.activation(dst, src, ACT.Copy)
                free(ins, e)

            def a_scores(e):
                i = e[1]
                full(act, e)
                act.wait_ge(a_max_ready, i + 1)
                if i >= 3:
                    act.wait_ge(a_mix_ready, i - 2)
                s = view(e, 2 * TB, S)
                for j in range(2 * TB):
                    ins = act.activation(a_P[:, i % 3, j, :], s[:, j, :], ACT.Exp,
                                         bias=a_nm[:, i % 4, j:j + 1], accum_out=a_rs[:, i % 4, j:j + 1])
                free(ins, e)

            def a_turn(e):
                i = e[1]
                full(act, e)
                free(act.activation(a_AT[:, i % 8], view(e, TB, S), ACT.Copy), e)

            def a_heads(e):
                g = e[1]
                full(act, e)
                rows = slice(64 * (g % 2), 64 * (g % 2) + 64)
                free(act.activation(a_OT[rows, g // 2 % 4, :], view(e, S)[rows], ACT.Copy), e)

            def copy_to(dst, *dims, **kw):
                def f(e):
                    full(act, e)
                    free(act.activation(dst(e), view(e, *dims, **kw), ACT.Copy), e)
                return f

            def kv_turn(e):
                _, lay, b = e
                full(act, e)
                for a in range(2):
                    for c in range(2):
                        ins = act.activation(kv_halves(b, 0, c)[:, :, a, :], kv_slot(e, a), ACT.Copy)
                ins.then_inc(kv_high_ready, 1)

            def x_q(e):
                _, b, g = e
                j = (H // 2 * b + g) % PAIRS
                full(act, e)
                for a in range(2):
                    rows = slice(DC * a, DC * a + DC)
                    ins = act.activation(q_split[rows, j, a, :], view(e, S)[rows], ACT.Copy)
                ins.then_inc(q_high_ready, 1)

            def x_scores(e):
                _, lay, i = e
                n = lay * NB * H + i
                full(act, e)
                act.wait_ge(x_max_ready, n + 1)
                if i >= 3:
                    full(act, ("x_turn", lay, i - 3, 1))
                s = view(e, TB, LC)
                for j in range(TB):
                    ins = act.activation(x_P[:, i % 3, j, :], s[:, j, :], ACT.Exp,
                                         bias=x_nm[:, i % 4, j:j + 1], accum_out=x_rs[:, i % 4, j:j + 1])
                free(ins, e)

            def m_gate(e):
                b = e[1]
                full(act, e)
                act.wait_ge(m_max_ready, b + 1)
                for t in range(TB):
                    n = TB * b + t
                    ins = act.activation(m_E[:, n, :], view(e, TB, NX)[:, t], ACT.Exp, bias=m_nm[:, n:n + 1],
                                         accum_out=m_rs[:, n:n + 1])
                free(ins, e)

            def m_flat(e):
                b = e[1]
                act.wait_ge(m_val_ready, b + 1)
                act.activation(m_ex[:, TB * b:TB * b + TB, :], m_val[:, TB * b:TB * b + TB, :], ACT.Exp)\
                    .then_inc(m_ex_ready, 1)

            def m_su(e):
                b = e[1]
                g = ("m_sg", b)
                full(act, g)
                if b >= 2:
                    taken(act, ("m_su", b - 2))
                free(act.activation(m_SS[:, b % 2], view(g, 3, S), ACT.Silu), g)

            def m_a(e):
                _, f, b = e
                i = NB * f + b
                full(act, e)
                if i >= 2:
                    taken(act, ("m_a2", *divmod(i - 2, NB)))
                act.activation(m_WX[:, i % 2, :], view(e, 2, S)[:, 1], ACT.Copy).then_inc(m_wx_ready, 1)

            def m_g(e):
                _, f, b = e
                i = NB * f + b
                full(act, e)
                if i >= 2:
                    taken(act, ("m_g", *divmod(i - 2, NB)))
                o = view(e, 3, S)
                act.activation(m_SG[:, i % 2, 0, :], o[:, 0], ACT.Silu)
                act.activation(m_SG[0:ML, i % 2, 1, :], o[0:ML, 2], ACT.Silu).then_inc(m_silu_ready, 1)

            def d_x(e):
                b = e[1]
                full(act, e)
                if b == 0:
                    act.wait_ge(m_pads, 1)
                    act.wait_ge(d_loaded, 96)
                if b >= 2:
                    act.wait_ge(d_conv_ready, b - 1)
                free(act.activation(d_XP[:, b % 2, :, TAPS - 1:XPAD], view(e, DI // P, S), ACT.Copy), e)

            def d_z(e):
                b = e[1]
                full(act, e)
                if b >= 2:
                    act.wait_ge(d_gated, b - 1)
                free(act.activation(d_Z[:, b % 2], view(e, DI // P, S), ACT.Silu), e)
                act.wait_ge(d_conv_ready, b + 1)
                for c in range(DI // P):
                    ins = act.activation(d_C[:, b % 2, c, :], d_C[:, b % 2, c, :], ACT.Silu, bias=d_bias[:, c:c + 1])
                ins.then_inc(d_silu_ready, 1)

            def d_m1(e):
                _, b, half = e
                full(act, e)
                free(act.activation(d_M[:, b % 2, 4 * half:4 * half + 4, :], view(e, 4, S), ACT.Relu), e)

            def fold_y(e):
                _, c, a = e
                full(act, e)
                for h in range(2):
                    n = 4 * c + 2 * a + h
                    src = view(e, 2, 512)[:, h, 0:KD * DCQ].rearrange("p (k q) -> p k q", k=KD)
                    ins = act.activation(Y[:, :, n, :], src, ACT.Copy)
                free(ins, e)

            def w_turn(e):
                full(act, e)
                src = halfwords(e, KD, FC * P)[:, :, 0:FI]
                free(act.activation(w_QT, src, ACT.Copy), e)

            def w_gather(e):
                _, a, k = e
                full(act, e)
                src = view(e, 2, 512)[:, :, 0:FH]
                free(act.activation(w_in[a][:, k, :].rearrange("p (a b) -> p a b", a=2), src, ACT.Copy), e)

            def f_xt(e):
                full(act, e)
                src = halfwords(e, KD, S)
                free(act.activation(f_XT[:, e[1] % 2], src, ACT.Copy), e)

            def f_g(e):
                n = e[1]
                taken(act, e)
                if n >= 2:
                    act.wait_ge(f_product, n - 1)
                act.activation(f_SG[:, n % 2, :], f_G[:, n % 2, :], ACT.Silu).then_inc(f_silu, 1)

            def f_scale(e):
                n = e[1]
                act.wait_ge(f_inverse, n + 1)
                act.activation(f_T[:, n % 4, :], f_T[:, n % 4, :], ACT.Copy, scale=f_s[:, 1, 2, n:n + 1])\
                    .then_inc(f_scaled, 1)

            def f_t(e):
                n = e[1]
                full(act, e)
                src = halfwords(e, FC, P)
                act.activation(f_TT[:, n % 2, 0:FC - 1, :], src[:, 0:FC - 1, :], ACT.Copy)
                free(act.activation(f_TT[0:FI - (FC - 1) * P, n % 2, FC - 1, :],
                                    src[0:FI - (FC - 1) * P, FC - 1, :], ACT.Copy), e)

            todo = {"xt": xt, "a_q": a_q, "a_k": a_k, "a_v": a_v, "a_scores": a_scores, "a_turn": a_turn, "a_heads": a_heads,
                    "kv_turn": kv_turn, "x_q": x_q, "r_q": x_q,
                    "fold_n": copy_to(lambda e: N[:, 4 * e[2]:4 * e[2] + 4], 4, 2, DC, rows=QH),
                    "fold_l": copy_to(lambda e: L, 4, DC),
                    "fold_z": copy_to(lambda e: Z[:, :, 4 * DC * e[1]:4 * DC * (e[1] + 1)], KD, 4 * DC),
                    "fold_u": copy_to(lambda e: U[:, 2 * e[2]:2 * e[2] + 2, :], 2, D),
                    "m_gate": m_gate, "m_flat": m_flat, "m_su": m_su, "m_a": m_a, "m_g": m_g,
                    "d_x": d_x, "d_z": d_z, "d_m1": d_m1, "fold_y": fold_y,
                    "w_turn": w_turn, "w_gather": w_gather,
                    "w_row": copy_to(lambda e: w_rows[e[1]], FI),
                    "f_xt": f_xt, "f_sel": copy_to(lambda e: f_XS[:, e[1] % 2], KD, S),
                    "f_g": f_g, "f_scale": f_scale, "f_t": f_t,
                    "m_wdt": copy_to(lambda e: m_wdT[:, e[1] * S:(e[1] + 1) * S], S, rows=NX),
                    "m_wt": copy_to(lambda e: m_WT[:, e[1] * S:(e[1] + 1) * S], S, rows=NX),
                    "x_scores": x_scores,
                    "x_turn": copy_to(lambda e: x_PT[:, e[2] % 4, 2 * e[3]:2 * e[3] + 2], 2, S)}
            for e in steps:
                if e[0] in todo:
                    todo[e[0]](e)

        @block.vector
        def _(dve):
            chain = [0]

            def link(ins):
                chain[0] += 1
                ins.then_inc(dve_step, 1)
                dve.wait_ge(dve_step, chain[0])

            dve.wait_ge(consts_loaded, 48)
            link(dve.tensor_scalar(neg_lambda[:, :], neg_lambda[:, :], -1.0, None, ALU.mult))

            def norm(e):
                _, kind, b = e
                n = norm_no[(kind, b)]
                if kind in "GH":
                    for t in range(TB):
                        src = XN[:, TB * b + t, :]
                        ins = dve.scalar_tensor_tensor(out=d_J, in0=src, scalar=1.0, in1=src, op0=ALU.mult,
                                                       op1=ALU.mult, accum_out=mv[:, n % 2, t, 1:2])
                        if t == TB - 1:
                            ins.then_inc(norm_stats, 1)
                        else:
                            link(ins)
                    dve.wait_ge(norm_rstd, n + 1)
                    if b >= 2:
                        full(dve, ("xt", kind, b - 2))
                    elif kind == "H":
                        full(dve, ("xt", "G", b + 2))
                    for t in range(TB):
                        dve.tensor_scalar(d_N[:, TB * (b % 2) + t, :], XN[:, TB * b + t, :],
                                          rstd[:, n % 2, 1, t:t + 1], None, ALU.mult).then_inc(normed, 1)
                    return
                if kind == "A":
                    dve.wait_ge(x_loaded[b], 16)
                for t in range(TB):
                    link(dve.bn_stats(stats[:, n % 2, t, :], X[:, TB * b + t, :]))
                    dve.bn_aggr(mv[:, n % 2, t, :], stats[:, n % 2, t, :]).then_inc(norm_stats, 1) \
                        if t == TB - 1 else link(dve.bn_aggr(mv[:, n % 2, t, :], stats[:, n % 2, t, :]))
                dve.wait_ge(norm_rstd, n + 1)
                for t in range(TB):
                    dve.tensor_scalar(XN[:, TB * b + t, :], X[:, TB * b + t, :], mv[:, n % 2, t, 0:1],
                                      rstd[:, n % 2, 1, t:t + 1], ALU.subtract, ALU.mult)\
                        .then_inc(normed, 1)

            def a_q(e):
                n = e[1] % 2
                dve.wait_ge(a_q_high_ready, e[1] + 1)
                for p in range(2):
                    rows, other = pair_rows(p)
                    ins = dve.tensor_tensor(a_QS[other, n, p, :], view(e, S)[rows],
                                            a_QS[rows, n, p, :].bitcast(F32), ALU.subtract)
                free(ins, e)

            def a_k(e):
                n = e[1] % 2
                dve.wait_ge(a_k_high_ready, e[1] + 1)
                for p in range(2):
                    rows, other = pair_rows(p)
                    for dst in (rows, other):
                        ins = dve.tensor_tensor(a_KS[dst, n, p, 1, :], view(e, S)[rows],
                                                a_KS[rows, n, p, 0, :].bitcast(F32), ALU.subtract)
                free(ins, e)

            def x_out(e):
                _, lay, b, t = e
                full(dve, e)
                x = X[:, TB * b + t, :]
                free(dve.tensor_tensor(x, view(e, D), x, ALU.add), e)
                taken(dve, e)

            def a_low(e):
                _, n, keys = e
                (a_k if keys else a_q)(("a_k" if keys else "a_q", n))

            def a_scores(e):
                i = e[1]
                full(dve, e)
                dve.tensor_reduce(a_nm[:, i % 4, :], view(e, 2 * TB, S), AX.X, ALU.max, negate=True)\
                    .then_inc(a_max_ready, 1)

            def a_inverse(e):
                i = e[1]
                taken(dve, ("a_scores", i))
                link(dve.reciprocal(a_r[:, i % 4, :], a_rs[:, i % 4, :]))
                dve.tensor_scalar(a_c[:, i % 4, :], a_r[:, i % 4, TB:2 * TB], neg_lambda[:, i % H:i % H + 1], None,
                                  ALU.mult).then_inc(a_inverted, 1)

            def a_mix(e):
                i = e[1]
                dve.wait_ge(a_inverted, i + 1)
                dve.wait_ge(a_scaled, i + 1)
                for t in range(TB):
                    ins = dve.scalar_tensor_tensor(out=a_A[:, i % 4, t, :], in0=a_P[:, i % 3, TB + t, :],
                                                   scalar=a_c[:, i % 4, t:t + 1], in1=a_A[:, i % 4, t, :],
                                                   op0=ALU.mult, op1=ALU.add)
                ins.then_inc(a_mix_ready, 1)

            def residual(e):
                b = e[-1]
                full(dve, e)
                xb = X[:, TB * b:TB * b + TB, :]
                ins = dve.tensor_tensor(xb, view(e, TB, D), xb, ALU.add)
                free(ins, e)
                taken(dve, e)

            def kv_turn(e):
                _, lay, b = e
                dve.wait_ge(kv_high_ready, NB * lay + b + 1)
                for a in range(2):
                    for c in range(2):
                        ins = dve.tensor_tensor(kv_halves(b, 1, c)[:, :, a, :], kv_slot(e, a),
                                                kv_halves(b, 0, a)[:, :, a, :].bitcast(F32), ALU.subtract)
                free(ins, e)

            def x_low(e):
                _, lay, b, g = e
                e = ("r_q" if lay else "x_q", b, g)
                n = NB * H // 2 * lay + H // 2 * b + g
                dve.wait_ge(q_high_ready, n + 1)
                for a in range(2):
                    rows, other = (slice(DC * c, DC * c + DC) for c in (a, 1 - a))
                    ins = dve.tensor_tensor(q_split[other, n % PAIRS, a, :], view(e, S)[rows],
                                            q_split[rows, n % PAIRS, a, :].bitcast(F32), ALU.subtract)
                free(ins, e)

            def x_scores(e):
                i = e[2]
                full(dve, e)
                dve.tensor_reduce(x_nm[:, i % 4, :], view(e, TB, LC), AX.X, ALU.max, negate=True)\
                    .then_inc(x_max_ready, 1)

            def x_norm(e):
                _, lay, i = e
                taken(dve, ("x_scores", lay, i))
                link(dve.reciprocal(x_r[:, i % 4, :], x_rs[:, i % 4, :]))
                for t in range(TB):
                    ins = dve.tensor_scalar(x_P[:, i % 3, t, :], x_P[:, i % 3, t, :], x_r[:, i % 4, t:t + 1],
                                            None, ALU.mult)
                ins.then_inc(x_norm_ready, 1)

            def x_heads(e):
                full(dve, e)
                rows = slice(DC * (e[2] % 2), DC * (e[2] % 2) + DC)
                free(dve.tensor_copy(x_C[rows, e[2] // 2 % HEAD_PAIRS, :], view(e, S)[rows]), e)

            def m_gate(e):
                b = e[1]
                ts = slice(TB * b, TB * b + TB)
                if b == 0:
                    dve.wait_ge(m_inv_loaded, 32)
                    dve.tensor_scalar(m_sel, m_inv[:, :], lane[0:NX, 0:1], None, ALU.is_equal)\
                        .then_inc(m_sel_ready, 1)
                full(dve, e)
                dve.tensor_reduce(m_nm[:, ts], view(e, TB, NX), AX.X, ALU.max, negate=True).then_inc(m_max_ready, 1)
                taken(dve, e)
                link(dve.reciprocal(m_r[:, ts], m_rs[:, ts]))
                link(dve.memset(m_sc[:, ts, NX:NX + 2], ABSENT))
                for n in range(TB * b, TB * b + TB):
                    link(dve.tensor_scalar(m_sc[:, n, 0:NX], m_E[:, n, :], m_r[:, n:n + 1], None, ALU.mult))
                    link(dve.max(m_t8[:, n, :], m_sc[:, n, 0:NX]))
                    link(dve.memset(m_t8[:, n, TOPK:8], ABSENT))
                    link(dve.match_replace(m_rep[:, n, :], m_t8[:, n, :], m_sc[:, n, :], 0.0))
                dve.tensor_tensor(m_wd[:, ts, :], m_sc[:, ts, 0:NX], m_rep[:, ts, 0:NX], ALU.subtract)\
                    .then_inc(m_wd_ready, 1)

            def grouped(ap, b):
                return ap[:, TB * b:TB * b + TB, :].rearrange("p t (f k) -> p (t f) k", k=MK)

            def per_group(ap, b):
                return ap[:, TB * b:TB * b + TB, :].rearrange("p t f -> p (t f)")

            def spread(ap, b):
                return per_group(ap, b).unsqueeze(2).to_broadcast([P, TB * NE, MK])

            def m_flat_(e):
                b = e[1]
                ts = slice(TB * b, TB * b + TB)
                full(dve, e)
                free(dve.tensor_copy(m_flat[:, ts, :], view(e, TB, NX)), e)
                taken(dve, e)
                link(dve.tensor_reduce(per_group(m_scal, b), grouped(m_flat, b), AX.X, ALU.add))
                link(dve.tensor_scalar(m_val[:, ts, :], m_flat[:, ts, :], 0.0, -1e9, ALU.is_equal, ALU.mult))
                link(dve.tensor_tensor(m_val[:, ts, :], m_val[:, ts, :], m_flat[:, ts, :], ALU.add))
                link(dve.tensor_reduce(per_group(m_mx, b), grouped(m_val, b), AX.X, ALU.max))
                dve.tensor_tensor(grouped(m_val, b), grouped(m_val, b), spread(m_mx, b), ALU.subtract)\
                    .then_inc(m_val_ready, 1)
                dve.wait_ge(m_ex_ready, b + 1)
                link(dve.tensor_reduce(per_group(m_sum, b), grouped(m_ex, b), AX.X, ALU.add))
                link(dve.reciprocal(per_group(m_rsum, b), per_group(m_sum, b)))
                dve.tensor_tensor(grouped(m_w, b), grouped(m_ex, b), spread(m_rsum, b), ALU.mult)\
                    .then_inc(m_w_ready, 1)

            def m_su(e):
                b = e[1]
                full(dve, e)
                taken(dve, ("m_sg", b))
                if b >= 2:
                    full(dve, ("m_sy", b - 2))
                free(dve.tensor_tensor(m_HS[:, b % 2], view(e, 3, S), m_SS[:, b % 2], ALU.mult), e)

            def m_xe(e):
                _, f, b = e
                i = NB * f + b
                full(dve, e)
                if i >= 2:
                    full(dve, ("m_g", *divmod(i - 2, NB)))
                free(dve.tensor_tensor(m_XE[:, i % 2], view(e, KD, S), XT[:, :, b * S:(b + 1) * S], ALU.add), e)

            def m_a(e):
                _, f, b = e
                i = NB * f + b
                full(dve, e)
                dve.wait_ge(m_wx_ready, i + 1)
                if i >= 2:
                    full(dve, ("m_g", *divmod(i - 2, NB)))
                free(dve.tensor_tensor(m_AW[:, i % 2, :], view(e, 2, S)[:, 0], m_WX[:, i % 2, :], ALU.mult), e)

            def m_g(e):
                _, f, b = e
                i = NB * f + b
                full(dve, e)
                if i == 0:
                    link(dve.memset(m_H[32:64, :, 1, :], 0.0))
                dve.wait_ge(m_silu_ready, i + 1)
                if i >= 2:
                    full(dve, ("m_y", *divmod(i - 2, NB)))
                o = view(e, 3, S)
                dve.tensor_tensor(m_H[:, i % 2, 0, :], o[:, 1], m_SG[:, i % 2, 0, :], ALU.mult)
                free(dve.tensor_tensor(m_H[0:ML, i % 2, 1, :], o[64:64 + ML, 2], m_SG[0:ML, i % 2, 1, :],
                                       ALU.mult), e)

            def m_a2(e):
                _, f, b = e
                i = NB * f + b
                full(dve, e)
                free(dve.tensor_tensor(m_H[64:P, i % 2, 1, :], view(e, S)[64:P], m_WX[64:P, i % 2, :], ALU.mult), e)

            def m_y(e):
                _, f, b = e
                full(dve, e)
                for t in range(TB):
                    n = TB * b + t
                    ins = dve.scalar_tensor_tensor(out=X[:, n, :], in0=view(e, TB, D)[:, t],
                                                   scalar=m_scal[:, n, f:f + 1], in1=X[:, n, :],
                                                   op0=ALU.mult, op1=ALU.add)
                free(ins, e)
                taken(dve, e)

            def d_x(e):
                b = e[1]
                if b == 0:
                    dve.memset(d_XP[:, :, :, 0:TAPS - 1].rearrange("p a b c -> p (a b) c"), 0.0).then_inc(m_pads, 1)
                taken(dve, e)
                if b >= 2:
                    full(dve, ("d_out", b - 2))
                for c in range(DI // P):
                    link(dve.tensor_scalar(d_C[:, b % 2, c, :], d_XP[:, b % 2, c, 0:S], d_conv[:, c, 0:1], None,
                                           ALU.mult))
                for j in range(1, TAPS):
                    for c in range(DI // P):
                        ins = dve.scalar_tensor_tensor(out=d_C[:, b % 2, c, :], in0=d_XP[:, b % 2, c, j:j + S],
                                                       scalar=d_conv[:, c, j:j + 1], in1=d_C[:, b % 2, c, :],
                                                       op0=ALU.mult, op1=ALU.add)
                        if j < TAPS - 1 or c < DI // P - 1:
                            link(ins)
                ins.then_inc(d_conv_ready, 1)

            def d_out(e):
                b = e[1]
                full(dve, e)
                n = XN[:, TB * b:TB * b + TB, :]
                free(dve.tensor_tensor(n, view(e, TB, D), n, ALU.add), e)
                taken(dve, e)

            def d_m2(e):
                b = e[1]
                xb = X[:, TB * b:TB * b + TB, :]
                link(dve.tensor_tensor(xb, xb, XN[:, TB * b:TB * b + TB, :], ALU.add))
                residual(e)

            def r_g(e):
                _, b, g, a = e
                j = H // 2 * b + g
                full(dve, e)
                if j == 0 and a == 0:
                    dve.wait_ge(r_tables, 32)
                if j >= 2 and a == 0:
                    full(dve, ("r_q", *divmod(j - 2, H // 2)))
                    dve.wait_ge(r_ready, 2 * (j - 1))
                q = view(e, 2, S, rows=QH)
                n = 2 * (j % 2) + a
                dve.tensor_tensor(r_R[:, n], q, r_cos, ALU.mult)
                for half in range(2):
                    ins = dve.tensor_tensor(r_M[:, n, half, :], q[:, 1 - half, :], r_sin[:, half, :], ALU.mult)
                free(ins, e)

            def over_range(s, b0, n, widest):
                link(dve.tensor_scalar(s[:, 1, b0:b0 + n], widest, 1.0 / FP8_MAX, TINY, ALU.mult, ALU.max))
                return dve.reciprocal(s[:, 2, b0:b0 + n], s[:, 1, b0:b0 + n])

            def to_fp8(v, e, q):
                link(dve.tensor_scalar(e.bitcast(I32), v.bitcast(I32), EXPONENT, None, ALU.bitwise_and))
                link(dve.tensor_scalar(e, e, FP8_NORMAL, FP8_ROUND, ALU.max, ALU.mult))
                link(dve.tensor_tensor(v, v, e, ALU.add))
                return dve.tensor_tensor(q, v, e, ALU.subtract)

            def w_count(e):
                dve.wait_ge(w_indices, 80)
                link(dve.memset(ones16[:, :], 1.0))
                link(dve.tensor_copy(ident16[:, :], ident[:, :]))
                link(dve.tensor_copy(w_uidxf[:, :], w_uidx[:, :]))
                for k in range(KD):
                    link(dve.tensor_scalar(w_sel[:, k, :], w_urow, lanes[:, k:k + 1], None, ALU.is_equal))
                    ins = dve.tensor_scalar(w_hit[:, k, :], w_iota, w_uidxf[:, k:k + 1], None, ALU.is_equal)
                    if k < KD - 1:
                        link(ins)
                ins.then_inc(w_tables, 1)
                full(dve, e)
                free(dve.tensor_scalar(w_mask, view(e, D), 0.0, None, ALU.is_gt), e)
                taken(dve, e)

            def w_dmax(e):
                dve.wait_ge(w_fetched[2], 16 * FC)
                dve.wait_ge(w_zeroed, 3)
                dve.tensor_reduce(w_tmp[:, 0, :], w_W[:, 2].rearrange("p c o -> p o c"), AX.X, ALU.max,
                                  apply_absolute_value=True).then_inc(w_dmax_ready, 1)

            def w_quant(e):
                a = e[1]
                if a == 2:
                    dve.wait_ge(w_dall_ready, 1)
                    link(dve.tensor_scalar(w_drow, w_drow, 1.0 / FP8_MAX, TINY, ALU.mult, ALU.max))
                    link(dve.reciprocal(w_tmp[:, 1, :], w_drow))
                    link(dve.tensor_tensor(w_W[:, 2], w_W[:, 2], w_tmp[:, 1:2, :].to_broadcast([P, FC, D]),
                                           ALU.mult))
                else:
                    dve.wait_ge(w_fetched[a], 16 * FC)
                    link(dve.tensor_tensor(w_W[:, a], w_W[:, a],
                                           w_mask.unsqueeze(1).to_broadcast([P, FC, D]), ALU.mult))
                    link(dve.tensor_reduce(w_max[:, 0, :], w_W[:, a], AX.X, ALU.max, apply_absolute_value=True))
                    if a == 1:
                        full(dve, ("w_row", 0))
                        full(dve, ("w_turn", 0))
                    link(over_range(w_max, 0, FC, w_max[:, 0, :]))
                    for c in range(FC):
                        link(dve.tensor_scalar(w_W[:, a, c, :], w_W[:, a, c, :], w_max[:, 2, c:c + 1], None,
                                               ALU.mult))
                to_fp8(w_W[:, a], w_tmp, w_down if a == 2 else w_Q).then_inc(w_quantised, 1)

            def f_quant(e):
                b = e[1]
                v = f_X[:, b % 2]
                link(dve.tensor_tensor(v, XN[:, TB * b:TB * b + TB, :],
                                       w_mask.unsqueeze(1).to_broadcast([P, TB, D]), ALU.mult))
                link(dve.tensor_reduce(f_s[:, 0, 0, TB * b:TB * b + TB], v, AX.X, ALU.max,
                                       apply_absolute_value=True))
                link(over_range(f_s[:, 0], TB * b, TB, f_s[:, 0, 0, TB * b:TB * b + TB]))
                for t in range(TB):
                    link(dve.tensor_scalar(v[:, t, :], v[:, t, :], f_s[:, 0, 2, TB * b + t:TB * b + t + 1], None,
                                           ALU.mult))
                if b >= 2:
                    full(dve, ("f_xt", b - 2))
                to_fp8(v, f_Xt, f_XQ[:, b % 2]).then_inc(f_xq_ready, 1)

            def halves(ap):
                return ap.rearrange("p (a b) -> p a b", a=2)

            def dequantise(e, a, n, dst):
                full(dve, e)
                free(dve.scalar_tensor_tensor(out=halves(dst), in0=view(e, 2, 512)[:, :, 0:FH],
                                              scalar=f_s[:, 0, 1, n:n + 1], in1=halves(w_rows[a]),
                                              op0=ALU.mult, op1=ALU.mult), e)

            def f_g(e):
                n = e[1]
                if n == 0:
                    for a in range(2):
                        taken(dve, ("w_row", a))
                if n >= 2:
                    dve.wait_ge(f_silu, n - 1)
                dequantise(e, 0, n, f_G[:, n % 2, :])

            def f_u(e):
                dequantise(e, 1, e[1], f_T[:, e[1] % 4, :])

            def f_scale(e):
                n = e[1]
                dve.wait_ge(f_product, n + 1)
                link(dve.tensor_reduce(f_s[:, 1, 0, n:n + 1], f_T[:, n % 4, :], AX.X, ALU.max,
                                       apply_absolute_value=True))
                over_range(f_s[:, 1], n, 1, f_s[:, 1, 0, n:n + 1]).then_inc(f_inverse, 1)

            def f_exponent(e):
                n = e[1]
                dve.wait_ge(f_scaled, n + 1)
                dve.tensor_scalar(f_E[:, n % 4, :].bitcast(I32), f_T[:, n % 4, :].bitcast(I32), EXPONENT, None,
                                  ALU.bitwise_and).then_inc(f_exponents, 1)

            def f_round(e):
                n = e[1]
                dve.wait_ge(f_summed, n + 1)
                if n >= 2:
                    full(dve, ("f_t", n - 2))
                dve.tensor_tensor(f_TQ[:, n % 2, :], f_T[:, n % 4, :], f_E[:, n % 4, :], ALU.subtract)\
                    .then_inc(f_rounded, 1)

            def f_y(e):
                n = e[1]
                full(dve, e)
                if n >= 2:
                    dve.wait_ge(x_done, n - 1)
                free(dve.scalar_tensor_tensor(out=f_Y[:, n % 2, :], in0=view(e, D), scalar=f_s[:, 1, 1, n:n + 1],
                                              in1=w_drow, op0=ALU.mult, op1=ALU.mult), e)

            todo = {"w_count": w_count, "w_dmax": w_dmax, "w_quant": w_quant, "f_quant": f_quant, "f_g": f_g,
                    "f_u": f_u, "f_scale": f_scale, "f_exponent": f_exponent, "f_round": f_round, "f_y": f_y,
                    "d_x": d_x, "d_out": d_out, "d_m2": d_m2, "r_g": r_g,
                    "m_gate": m_gate, "m_flat": m_flat_, "m_su": m_su, "m_xe": m_xe, "m_a": m_a, "m_g": m_g,
                    "m_a2": m_a2, "m_y": m_y, "m_sy": residual,
                    "norm": norm, "a_low": a_low, "a_scores": a_scores, "a_inverse": a_inverse, "a_mix": a_mix, "a_out": residual,
                    "x_scores": x_scores, "x_norm": x_norm, "x_heads": x_heads, "x_out": x_out,
                    "kv_turn": kv_turn, "x_low": x_low}
            for e in steps:
                if e[0] in todo:
                    todo[e[0]](e)

        @block.tensor
        def _(pe):
            def group(o, pairs):
                for n, (l, r) in enumerate(pairs):
                    ins = pe.matmul(o, l, r, start=(n == 0), stop=(n == len(pairs) - 1))
                return ins

            def xt(e):
                _, kind, b = e
                if xt_no[(kind, b)] == 0:
                    pe.wait_ge(consts_loaded, 48)
                pe.wait_ge(normed, TB * (norm_no[(kind, b)] + 1))
                o = view(e, KD, TB, P)
                for t in range(TB):
                    for k in range(KD):
                        if kind in "GH":
                            src = d_N[:, TB * (b % 2) + t, k * P:(k + 1) * P]
                        else:
                            src = XN[:, TB * b + t, k * P:(k + 1) * P]
                        ins = pe.transpose(o[:, k, t, :], src, ident[:, :])
                return ins

            def batch(b):
                return XT[:, :, b * S:(b + 1) * S]

            def a_in(w):
                def f(e):
                    b, g = divmod(e[1], 4)
                    if e[1] == 0:
                        pe.wait_ge(*((aq_weights, 16) if e[0] == "a_q" else (a_weights, 48)))
                        taken(pe, ("xt", "A", 0))
                    elif g == 0:
                        taken(pe, ("xt", "A", b))
                    return group(view(e, S), [(w[:, k, g, :], batch(b)[:, k]) for k in range(KD)])
                return f

            def a_v(e):
                b = e[1]
                for t in range(TB):
                    ins = group(view(e, TB, D)[:, t], [(batch(b)[:, k, t * P:(t + 1) * P], a_wv[:, k, :])
                                                       for k in range(KD)])
                return ins

            def a_scores(e):
                b, h = divmod(e[1], H)
                g, j = divmod(e[1], 4)
                pe.wait_ge(a_masked, e[1] // 2 + 1)
                if j == 0:
                    taken(pe, ("a_k", e[1] // 4))
                o = view(e, 2, TB, S)
                for t in range(TB):
                    for m in range(2):
                        q = a_QM[:, e[1] // 2 % 2, 2 * (j % 2) + m, t * P:(t + 1) * P]
                        ins = group(o[:, m, t, :], [(q, a_KS[:, g % 2, j // 2, part, :]) for part in range(2)])
                return ins

            def a_turn(e):
                i = e[1]
                pe.wait_ge(a_mix_ready, i + 1)
                o = view(e, TB, S)
                for t in range(TB):
                    for k in range(TB):
                        ins = pe.transpose(o[:, k, t * P:(t + 1) * P], a_A[:, i % 4, t, k * P:(k + 1) * P],
                                           ident[:, :])
                return ins

            def a_heads(e):
                g = e[1]
                b = g // 8
                taken(pe, ("a_v", b))
                for j in range(2):
                    i = 2 * g + j
                    taken(pe, ("a_turn", i))
                    h = i % H
                    ins = group(view(e, S, rows=32, base=32 * (i % 4)),
                                [(a_V[:, b % 2, k, 32 * h:32 * h + 32], a_AT[:, i % 8, k, :])
                                 for k in range(TB)])
                return ins

            def a_out(e):
                b = e[1]
                for g in range(8):
                    taken(pe, ("a_heads", 8 * b + g))
                for t in range(TB):
                    ins = group(view(e, TB, D)[:, t],
                                [(a_OT[:, g, t * P:(t + 1) * P], a_wo[:, g, :]) for g in range(4)])
                return ins

            def kv_turn(e):
                b = e[2]
                pe.wait_ge(kv_roped, b + 1)
                for c in range(LT // 2):
                    pair = kvr[:, LT * b + 2 * c:LT * b + 2 * c + 2, :].rearrange("p t d -> p (t d)")
                    ins = pe.transpose(view(e, LT // 2, P)[:, c], pair, ident[:, :])
                return ins

            def fold_n(e):
                _, lay, c = e
                pe.wait_ge(chunk_loaded[lay][c], 16)
                qr = carve(staged[:, c % 2, :], CQR, 4, DCQ, rows=R)
                kr = carve(staged[:, c % 2, :], CKR, 4, DC, rows=R)
                o = view(e, 4, 2, DC, rows=QH)
                for h in range(4):
                    for a in range(2):
                        ins = pe.matmul(o[:, h, a, :], qr[:, h, a * QH:(a + 1) * QH], kr[:, h, :],
                                        start=True, stop=True)
                return ins

            def fold_l(e):
                c = e[1]
                taken(pe, ("fold_n", 0, c))
                kc = carve(staged[:, c % 2, :], CKC, 4, 2, KH, rows=QH)
                for h in range(4):
                    ins = group(view(e, 4, DC)[:, h], [(kc[:, h, a, :], N[:, 4 * c + h, a, :]) for a in range(2)])
                return ins

            def fold_z(e):
                c = e[1]
                taken(pe, ("fold_l", c))
                wq = carve(staged[:, c % 2, :], CWQ, 4, D)
                o = view(e, KD, 4, DC)
                for h in range(4):
                    for k in range(KD):
                        ins = pe.matmul(o[:, k, h, :], wq[:, h, k * P:(k + 1) * P], L[:, h, :],
                                        start=True, stop=True)
                return ins

            def fold_u(e):
                _, lay, c = e
                kvw = carve(staged[:, c % 2, :], CKV, 4, DC)
                wo = carve(staged[:, c % 2, :], CWO, 4, D)
                for h in range(4):
                    o = view(e, 2, D, rows=DC, base=DC * (h % 2))
                    ins = pe.matmul(o[:, h // 2, :], kvw[:, h, :], wo[:, h, :], start=True, stop=True)
                return ins

            def x_q(e):
                _, b, g = e
                if b == 0:
                    taken(pe, ("fold_z", g // 2))
                taken(pe, ("xt", "B", b))
                return group(view(e, S), [(Z[:, k, g * P:(g + 1) * P], batch(b)[:, k]) for k in range(KD)])

            def x_scores(e):
                _, lay, i = e
                b, h = divmod(i, H)
                if h == 0:
                    taken(pe, ("kv_turn", lay, b))
                taken(pe, ("r_q" if lay else "x_q", b, h // 2))
                for t in range(TB):
                    q = q_split[:, i // 2 % PAIRS, h % 2, t * P:(t + 1) * P]
                    ins = group(view(e, TB, LC)[:, t], [(q, kv_split[:, b % 2, part, :]) for part in range(2)])
                return ins

            def x_turn(e):
                _, lay, i, half = e
                pe.wait_ge(x_norm_ready, lay * NB * H + i + 1)
                o = view(e, 2, S)
                for t in range(TB):
                    for k in range(2):
                        keys = slice((2 * half + k) * P, (2 * half + k + 1) * P)
                        ins = pe.transpose(o[:, k, t * P:(t + 1) * P], x_P[:, i % 3, t, keys], ident[:, :])
                return ins

            def x_heads(e):
                _, lay, i = e
                b = i // H
                for half in range(2):
                    taken(pe, ("x_turn", lay, i, half))
                return group(view(e, S, rows=DC, base=DC * (i % 2)),
                             [(kvr[:, LT * b + k, :], x_PT[:, i % 4, k, :]) for k in range(LT)])

            def x_out(e):
                _, lay, b, t = e
                if b == 0 and t == 0:
                    for c in range(4):
                        taken(pe, ("fold_u", lay, c))
                if t == 0:
                    for h in range(H):
                        taken(pe, ("x_heads", lay, H * b + h))
                return group(view(e, D), [(x_C[:, (H // 2 * b + g) % HEAD_PAIRS, t * P:(t + 1) * P], U[:, g, :])
                                          for g in range(H // 2)])

            def m_gate(e):
                b = e[1]
                taken(pe, ("xt", "C", b))
                if b == 0:
                    pe.wait_ge(m_loaded, 96)
                for t in range(TB):
                    ins = group(view(e, TB, NX)[:, t], [(batch(b)[:, k, t * P:(t + 1) * P], m_gw[:, k, :])
                                                        for k in range(KD)])
                return ins

            def m_wdt(e):
                b = e[1]
                pe.wait_ge(m_wd_ready, b + 1)
                for t in range(TB):
                    ins = pe.transpose(view(e, TB, P, rows=NX)[:, t], m_wd[:, TB * b + t, :], ident[:, :])
                return ins

            def m_flat(e):
                b = e[1]
                taken(pe, ("m_wdt", b))
                pe.wait_ge(m_sel_ready, 1)
                for t in range(TB):
                    n = TB * b + t
                    ins = pe.matmul(view(e, TB, NX)[:, t], m_wdT[:, n * P:(n + 1) * P], m_sel, start=True, stop=True)
                return ins

            def m_wt(e):
                b = e[1]
                pe.wait_ge(m_w_ready, b + 1)
                for t in range(TB):
                    ins = pe.transpose(view(e, TB, P, rows=NX)[:, t], m_w[:, TB * b + t, :], ident[:, :])
                return ins

            def shared_in(w):
                def f(e):
                    b = e[1]
                    for c in range(3):
                        ins = group(view(e, 3, S)[:, c], [(w[:, k, c * P:(c + 1) * P], batch(b)[:, k])
                                                          for k in range(KD)])
                    return ins
                return f

            def m_sy(e):
                b = e[1]
                taken(pe, ("m_su", b))
                for t in range(TB):
                    ins = group(view(e, TB, D)[:, t], [(m_HS[:, b % 2, c, t * P:(t + 1) * P], m_sdw[:, c, :])
                                                       for c in range(3)])
                return ins

            def part(f, at, *dims, **kw):
                return carve(expert[:, f % 2, :], at, *dims, **kw)

            def m_xe(e):
                _, f, b = e
                if f == 0:
                    taken(pe, ("m_wt", b))
                for k in range(KD):
                    ins = pe.matmul(view(e, KD, S)[:, k], m_mu[:, f, k * P:(k + 1) * P], m_WT[:, b * S:(b + 1) * S],
                                    start=True, stop=True)
                return ins

            def m_a(e):
                _, f, b = e
                if b == 0:
                    pe.wait_ge(expert_loaded[f], 16)
                    pe.wait_ge(expert_scaled, 2 * (f + 1))
                i = NB * f + b
                o = view(e, 2, S)
                taken(pe, ("m_xe", f, b))
                pe.matmul(o[:, 1], m_pick[:, f, :], m_WT[:, b * S:(b + 1) * S], start=True, stop=True)
                return group(o[:, 0], [(part(f, EQA, KD, P)[:, k, :], m_XE[:, i % 2, k, :]) for k in range(KD)])

            def m_g(e):
                _, f, b = e
                i = NB * f + b
                for c in range(3):
                    pairs = [(part(f, EGU, KD, 3, P)[:, k, c, :], m_XE[:, i % 2, k, :]) for k in range(KD)]
                    if c == 0:
                        taken(pe, ("m_a", f, b))
                    pairs.append((part(f, EQB, 3, P)[:, c, :], m_AW[:, i % 2, :]))
                    ins = group(view(e, 3, S)[:, c], pairs)
                return ins

            def m_a2(e):
                _, f, b = e
                i = NB * f + b
                taken(pe, ("m_g", f, b))
                w = part(f, EDA, 2, 64)
                return group(view(e, S)[64:P], [(w[:, 0, :], m_H[:, i % 2, 0, :]),
                                                (w[0:ML, 1, :], m_H[0:ML, i % 2, 1, :])])

            def m_y(e):
                _, f, b = e
                i = NB * f + b
                taken(pe, ("m_a2", f, b))
                for t in range(TB):
                    ins = group(view(e, TB, D)[:, t],
                                [(m_H[:, i % 2, c, t * P:(t + 1) * P], part(f, EDW, 2, D)[:, c, :])
                                 for c in range(2)])
                return ins

            def wide_in(w, at):
                def f(e):
                    b = e[1]
                    c0 = at(e)
                    for c in range(4):
                        ins = group(view(e, 4, S)[:, c], [(w[:, k, (c0 + c) * P:(c0 + c + 1) * P], batch(b)[:, k])
                                                          for k in range(KD)])
                    return ins
                return f

            def d_x(e):
                taken(pe, ("xt", "G", e[1]))
                pe.wait_ge(d_loaded, 96)
                return wide_in(d_win, lambda e: 0)(e)

            def d_out(e):
                b = e[1]
                pe.wait_ge(d_gated, b + 1)
                for t in range(TB):
                    ins = group(view(e, TB, D)[:, t], [(d_C[:, b % 2, c, t * P:(t + 1) * P], d_wout[:, c, :])
                                                       for c in range(DI // P)])
                return ins

            def d_m1(e):
                taken(pe, ("xt", "H", e[1]))
                return wide_in(d_w1, lambda e: 4 * e[2])(e)

            def d_m2(e):
                b = e[1]
                taken(pe, ("d_m1", b, 1))
                for t in range(TB):
                    ins = group(view(e, TB, D)[:, t], [(d_M[:, b % 2, c, t * P:(t + 1) * P], d_w2[:, c, :])
                                                       for c in range(MLP // P)])
                return ins

            def fold_y(e):
                _, c, a = e
                wq = carve(staged[:, c % 2, :], CWQ, 4, D)
                kc = carve(staged[:, c % 2, :], CKC, 4, DCQ)
                for h in range(2):
                    o = view(e, 2, 512)[:, h, 0:KD * DCQ].rearrange("p (k q) -> p k q", k=KD)
                    for k in range(KD):
                        ins = pe.matmul(o[:, k, :], wq[:, 2 * a + h, k * P:(k + 1) * P], kc[:, 2 * a + h, :],
                                        start=True, stop=True)
                return ins

            def r_g(e):
                _, b, g, a = e
                if b == 0:
                    taken(pe, ("fold_y", g // 2, g % 2))
                taken(pe, ("xt", "E", b))
                o = view(e, 2, S, rows=QH)
                for half in range(2):
                    ins = group(o[:, half, :], [(Y[:, k, 2 * g + a, half * QH:(half + 1) * QH], batch(b)[:, k])
                                                for k in range(KD)])
                return ins

            def r_q(e):
                _, b, g = e
                j = H // 2 * b + g
                pe.wait_ge(r_ready, 2 * (j + 1))
                for a in range(2):
                    ins = group(view(e, S, rows=DC, base=DC * a),
                                [(N[:, 2 * g + a, half, :], r_R[:, 2 * (j % 2) + a, half, :]) for half in range(2)])
                return ins

            def w_count(e):
                pe.wait_ge(w_tables, 1)
                return group(view(e, D), [(ones16[:, :], w_hit[:, k, :]) for k in range(KD)])

            def w_turn(e):
                a = e[1]
                pe.wait_ge(w_quantised, a + 2)
                o = halfwords(e, KD, FC * P)
                for c in range(FC):
                    n = min(P, FI - c * P)
                    for k in range(KD):
                        ins = pe.transpose(o[:, k, c * P:c * P + n], w_Q[0:n, c, k * P:(k + 1) * P],
                                           ident16[0:n, 0:n])
                return ins

            def w_gather(e):
                _, a, k = e
                taken(pe, ("w_turn", a))
                for x in range(2):
                    ins = group(view(e, 2, 512)[:, x, 0:FH], [(w_sel[:, j, k * P:(k + 1) * P],
                                                               w_QT[:, j, x * FH:(x + 1) * FH]) for j in range(KD)])
                return ins

            def w_row(e):
                for c in range(FC):
                    n = min(P, FI - c * P)
                    ins = pe.matmul(view(e, FI)[:, c * P:c * P + n], w_max[0:n, 1, c:c + 1].to_broadcast([n, P]),
                                    ident[0:n, 0:n], start=True, stop=True)
                return ins

            def f_xt(e):
                b = e[1]
                pe.wait_ge(f_xq_ready, b + 1)
                o = halfwords(e, KD, S)
                for t in range(TB):
                    for k in range(KD):
                        ins = pe.transpose(o[:, k, t * P:(t + 1) * P], f_XQ[:, b % 2, t, k * P:(k + 1) * P],
                                           ident16[:, :])
                return ins

            def f_sel(e):
                b = e[1]
                taken(pe, ("f_xt", b))
                for k in range(KD):
                    ins = group(view(e, KD, S)[:, k], [(w_sel[:, j, k * P:(k + 1) * P], f_XT[:, b % 2, j, :])
                                                       for j in range(KD)])
                return ins

            def hidden(e):
                name, n = e
                a = 0 if name == "f_g" else 1
                b, t = divmod(n, TB)
                taken(pe, ("f_sel", b))
                taken(pe, ("w_gather", a, 1))
                for x in range(2):
                    ins = group(view(e, 2, 512)[:, x, 0:FH],
                                [(f_XS[:, b % 2, k, t * P:(t + 1) * P], w_in[a][:, k, x * FH:(x + 1) * FH])
                                 for k in range(KD)])
                return ins

            def f_t(e):
                n = e[1]
                pe.wait_ge(f_rounded, n + 1)
                o = halfwords(e, FC, P)
                for c in range(FC):
                    m = min(P, FI - c * P)
                    ins = pe.transpose(o[0:m, c, :], f_TQ[:, n % 2, c * P:c * P + m], ident16[:, :])
                return ins

            def f_y(e):
                n = e[1]
                taken(pe, ("f_t", n))
                pairs = []
                for c in range(FC):
                    m = min(P, FI - c * P)
                    pairs.append((f_TT[0:m, n % 2, c, :], w_down[0:m, c, :]))
                return group(view(e, D), pairs)

            todo = {"w_count": w_count, "w_turn": w_turn, "w_gather": w_gather, "w_row": w_row, "f_xt": f_xt,
                    "f_sel": f_sel, "f_g": hidden, "f_u": hidden, "f_t": f_t, "f_y": f_y,
                    "d_x": d_x, "d_z": wide_in(d_win, lambda e: 4), "d_out": d_out, "d_m1": d_m1, "d_m2": d_m2,
                    "fold_y": fold_y, "r_g": r_g, "r_q": r_q,
                    "m_gate": m_gate, "m_wdt": m_wdt, "m_flat": m_flat, "m_wt": m_wt, "m_sg": shared_in(m_sgw),
                    "m_su": shared_in(m_suw), "m_sy": m_sy, "m_xe": m_xe, "m_a": m_a, "m_g": m_g, "m_a2": m_a2,
                    "m_y": m_y,
                    "xt": xt, "a_q": a_in(a_wq), "a_k": a_in(a_wk), "a_v": a_v, "a_scores": a_scores, "a_turn": a_turn,
                    "a_heads": a_heads, "a_out": a_out, "kv_turn": kv_turn, "fold_n": fold_n, "fold_l": fold_l,
                    "fold_z": fold_z, "fold_u": fold_u, "x_q": x_q, "x_scores": x_scores, "x_turn": x_turn,
                    "x_heads": x_heads, "x_out": x_out}
            for e in steps:
                if e[0] in PE_STEPS:
                    s = slot_of[e]
                    for before in switch.get(e, ()):
                        taken(pe, before)
                    if use_of[e] >= 1:
                        pe.wait_ge(slot_free[s], use_of[e])
                    todo[e[0]](e).then_inc(slot_full[s], 1)


def host_layout(i):
    import numpy as np
    f = lambda n: np.asarray(i[n], np.float32)
    a = {}
    a["x"] = f("x")
    a["ident"] = np.eye(P, dtype=np.float32)

    def rows(w, k):
        return w.reshape(k, P, -1).transpose(1, 0, 2)

    m = np.zeros((P, 4), np.float32)
    for r in range(P):
        m[r, (r // 16) % 4] = HD ** -0.5
    a["qmask"] = m
    for n, w1, w2 in (("a_wq", "L0_attn_q1_w", "L0_attn_q2_w"), ("a_wk", "L0_attn_k1_w", "L0_attn_k2_w")):
        w = np.stack([f(w1).T.reshape(D, H, HD), f(w2).T.reshape(D, H, HD)], axis=2)
        a[n] = rows(w.reshape(D, 2 * D), KD).reshape(P, KD, 4, P)
    a["a_wv"] = rows(f("L0_attn_v_w").T, KD)
    wo = np.zeros((4, 4, 32, D), np.float32)
    wo[:, :, :HD, :] = f("L0_attn_o_w").T.reshape(4, 4, HD, D)
    a["a_wo"] = wo.reshape(4, P, D).transpose(1, 0, 2)
    a["a_lambda"] = f("L0_attn_lambda_param")

    a["kv"] = f("ctx_512")

    def rope(length, dim):
        inv = (1.0 / 10000.0 ** (np.arange(0, dim, 2, dtype=np.float32) / np.float32(dim))).astype(np.float32)
        ang = np.arange(length, dtype=np.float32)[:, None] * inv[None, :]
        sin = np.repeat(np.sin(ang), 2, axis=-1).astype(np.float32)
        cos = np.repeat(np.cos(ang), 2, axis=-1).astype(np.float32)
        sin[:, :dim // 2] *= -1.0
        return cos, sin

    cos, sin = rope(LC, DC)
    a["k_cos"], a["k_sin"] = (w.reshape(LT, P, DC).transpose(1, 0, 2) for w in (cos, sin))
    cos, sin = rope(S, DCQ)
    a["r_cos"], a["r_sin"] = (w.T.reshape(2, QH, S).transpose(1, 0, 2) for w in (cos, sin))
    chunks = np.zeros((8, P, CHUNK), np.float32)
    for lay in range(2):
        w = {n: f(f"L{lay}_xattn_{n}") for n in ("Wq", "w_kc_q", "w_kc_kv", "W_qr", "W_kr", "Wo")}
        qr, kr = w["W_qr"].transpose(2, 0, 1), w["W_kr"].transpose(2, 0, 1)
        wq = w["Wq"].reshape(H, KH, D).transpose(1, 0, 2)
        kvw = w["w_kc_kv"].transpose(1, 0, 2)
        wo = w["Wo"].T.reshape(H, KH, D).transpose(1, 0, 2)
        if lay == 0:
            kc = w["w_kc_q"].transpose(2, 0, 1).reshape(2, QH, H, KH).transpose(1, 2, 0, 3)
        else:
            kc = w["w_kc_q"].transpose(1, 0, 2)
        for c in range(4):
            h = slice(4 * c, 4 * c + 4)
            for at, v in ((CQR, qr), (CKR, kr), (CKC, kc), (CWQ, wq), (CKV, kvw), (CWO, wo)):
                part = v[:, h].reshape(v.shape[0], -1)
                chunks[4 * lay + c, :part.shape[0], at:at + part.shape[1]] = part
    a["chunks"] = chunks

    a["d_win"] = rows(f("L1_attn_W_in").T, KD)
    a["d_wout"] = rows(f("L1_attn_W_out").T, DI // P)
    a["d_w1"] = rows(f("L1_attn_W_mlp1").T, KD)
    a["d_w2"] = rows(f("L1_attn_W_mlp2").T, MLP // P)
    a["d_conv"] = rows(f("L1_attn_conv_w").reshape(DI, TAPS), DI // P)
    a["d_bias"] = f("L1_attn_conv_b").reshape(DI // P, P).T

    a["lanes"] = np.arange(D, dtype=np.float32).reshape(KD, P).T
    a["iota"] = np.broadcast_to(np.arange(D, dtype=np.float32), (P, D))
    a["f_uidx"] = np.asarray(i["L1_ffn_up_reorder_index"], np.int32)
    a["f_ucol"] = a["f_uidx"].reshape(KD, P).T
    dcol = np.zeros(FC * P, np.int32)
    dcol[:FI] = np.asarray(i["L1_ffn_down_reorder_index"], np.int32)
    a["f_dcol"] = dcol.reshape(FC, P).T
    a["f_didx"] = np.asarray(i["L1_ffn_down_reorder_index"], np.int32).reshape(FI, 1)
    a["f_gate"], a["f_up"] = f("L1_ffn_w_gate"), f("L1_ffn_w_up")
    a["f_down"] = f("L1_ffn_w_down").T

    q = {n: f(f"L0_ffn_{n}") for n in ("gate_weight", "mask_up_W", "gate_W", "gate_qa", "gate_qb", "gate_scale",
                                       "up_W", "up_qa", "up_qb", "up_scale", "down_W", "down_qa", "down_qb",
                                       "down_scale", "sh_gate_W", "sh_up_W", "sh_down_W")}
    a["lane"] = np.arange(P, dtype=np.float32).reshape(P, 1)
    a["m_inv"] = np.asarray(i["L0_ffn_inv_mapping"], np.int32).reshape(NX)
    a["m_gw"] = rows(q["gate_weight"].T, KD)
    mu = np.zeros((NX, NE, D), np.float32)
    pick = np.zeros((NX, NE, P), np.float32)
    for e in range(NE):
        mu[MK * e:MK * (e + 1), e, :] = q["mask_up_W"][e].T
        for k in range(MK):
            for half in (0, 64):
                pick[MK * e + k, e, half + MR * k:half + MR * (k + 1)] = 1.0
    a["m_mu"], a["m_pick"] = mu, pick
    ex = np.zeros((NE, P, EXPERT), np.float32)
    for e in range(NE):
        gu = np.zeros((D, 3, P), np.float32)
        gu[:, 0, :] = q["gate_W"][e].T[:, :P]
        gu[:, 1, :] = q["up_W"][e].T[:, :P]
        gu[:, 2, :ML] = q["gate_W"][e].T[:, P:]
        gu[:, 2, 64:64 + ML] = q["up_W"][e].T[:, P:]
        ex[e, :, EGU:EQB] = rows(gu.reshape(D, 3 * P), KD).reshape(P, -1)
        gq = q["gate_qb"][e].transpose(0, 2, 1).reshape(MK * MR, MI)
        uq = q["up_qb"][e].transpose(0, 2, 1).reshape(MK * MR, MI)
        qb = np.zeros((P, 3, P), np.float32)
        qb[:64, 0, :], qb[64:, 1, :] = gq[:, :P], uq[:, :P]
        qb[:64, 2, :ML], qb[64:, 2, 64:64 + ML] = gq[:, P:], uq[:, P:]
        ex[e, :, EQB:EGS] = qb.reshape(P, -1)
        gs = np.zeros((3, P), np.float32)
        gs[0], gs[1] = q["gate_scale"][e][:P], q["up_scale"][e][:P]
        gs[2, :ML], gs[2, 64:64 + ML] = q["gate_scale"][e][P:], q["up_scale"][e][P:]
        ex[e, :, EGS:EQA] = gs.reshape(1, -1)
        qa = np.concatenate([q["gate_qa"][e].reshape(64, D).T, q["up_qa"][e].reshape(64, D).T], axis=1)
        ex[e, :, EQA:EDA] = rows(qa, KD).reshape(P, -1)
        da = q["down_qa"][e].reshape(64, MI).T
        ex[e, :, EDA:EDA + 64] = da[:P]
        ex[e, :ML, EDA + 64:EDW] = da[P:]
        dw = q["down_W"][e].T
        ex[e, :, EDW:EDW + D] = dw[:P]
        ex[e, :ML, EDW + D:EDS] = dw[P:]
        ex[e, 64:, EDW + D:EDS] = q["down_qb"][e].transpose(0, 2, 1).reshape(64, D)
        ex[e, :64, EDS:EXPERT] = 1.0
        ex[e, 64:, EDS:EXPERT] = q["down_scale"][e].reshape(1, D)
    a["m_experts"] = ex
    for n, w in (("m_sgw", "sh_gate_W"), ("m_suw", "sh_up_W")):
        wide = np.zeros((D, 3 * P), np.float32)
        wide[:, :MS] = q[w].T
        a[n] = rows(wide, KD)
    wide = np.zeros((3 * P, D), np.float32)
    wide[:MS] = q["sh_down_W"].T
    a["m_sdw"] = rows(wide, 3)
    return {k: np.ascontiguousarray(v) for k, v in a.items()}


def kernel(**inputs):
    import numpy as np
    import concourse.bacc as bacc
    from concourse.bass_utils import run_bass_kernel_spmd as run

    nc = bacc.Bacc("TRN2", target_bir_lowering=False, num_devices=1)
    arrays, aps = {}, {}
    for name, a in host_layout(inputs).items():
        arrays[f"in_{name}"] = a
        aps[name] = nc.dram_tensor(f"in_{name}", a.shape, mybir.dt.from_np(a.dtype), kind="ExternalInput").ap()
    out = nc.dram_tensor("out_x", (NB, S, D), F32, kind="ExternalOutput").ap()
    decoder(nc, aps, out)
    r = run(nc, [arrays], core_ids=[0])
    return r.results[0]["out_x"]
```
